# Optimizing a Trainium2 kernel written in Bass

```python
import numpy as np
import jax
import jax.numpy as jnp

def _softmax(x, axis=-1):
    return jax.nn.softmax(x, axis=axis)

def _gelu(x):
    return jax.nn.gelu(x, approximate=True)

def _silu(x):
    return jax.nn.silu(x)

def _sigmoid(x):
    return jax.nn.sigmoid(x)

def _layernorm(x, axis=-1, eps=1e-05):
    m = jnp.mean(x, axis=axis, keepdims=True)
    v = jnp.var(x, axis=axis, keepdims=True)
    return (x - m) / jnp.sqrt(v + eps)

def _scatter_add(tgt, idx, src, axis=0):
    return tgt.at[idx].add(src)

def _segment_sum(src, seg, n):
    return jax.ops.segment_sum(src, seg, n)
kernel_name = 'mk_decoder_postln_d1_seqx_r8_5794b4'

def setup_inputs(seed: int=0):
    np.random.seed(seed)
    _w = jnp.asarray

    def _rec_inputs():
        import jax
        import jax.numpy as jnp
        _rk = jax.random.key(seed)
        x = 0.0001212 + 1 * jax.random.normal(jax.random.fold_in(_rk, 1), (16, 128, 256), jnp.float32)
        _lenS = 128 - jax.random.randint(jax.random.fold_in(_rk, 7), (16,), 0, max(1, 128 // 4) + 1, jnp.int32)
        _lenS2 = 128 - jax.random.randint(jax.random.fold_in(_rk, 8), (16,), 0, max(1, 128 // 4) + 1, jnp.int32)
        _ctx_2048P = jax.random.normal(jax.random.fold_in(_rk, 11), (16, 16, 256), jnp.float32)
        _ctx_2048c = jax.random.dirichlet(jax.random.fold_in(_rk, 511), 0.3 * jnp.ones((16,), jnp.float32), (16, 128))
        _ctx_2048t = jnp.einsum('bsk,bkd->bsd', _ctx_2048c, _ctx_2048P)
        _ctx_2048t = _ctx_2048t * jax.lax.rsqrt(jnp.mean(jnp.square(_ctx_2048t)) + 1e-12) * 0.953939
        ctx_2048 = 0.000173663 + 1.0001 * (_ctx_2048t + 0.3 * jax.random.normal(jax.random.fold_in(_rk, 611), (16, 128, 256), jnp.float32))
        return (x, ctx_2048)
    x, ctx_2048 = _rec_inputs()

    def _L0_attn_setup():
        import jax, jax.numpy as jnp
        import numpy as np
        B, N, H = (2, 512, 256)
        NH, HD = (16, 128)
        BLK = 32
        EPS = 1e-06

        def _lightning_attn(x, slope_rate, w_qkv, w_gate, w_out, norm_w):
            b, n, _ = x.shape
            h, d = (NH, HD)
            nb = n // BLK
            qkv = jax.nn.silu(jnp.einsum('bnf,of->bno', x, w_qkv))
            qkv = qkv.reshape(b, n, h, 3 * d)
            q, k, v = jnp.split(qkv, 3, axis=-1)
            q = q.transpose(0, 2, 1, 3)
            k = k.transpose(0, 2, 1, 3)
            v = v.transpose(0, 2, 1, 3)
            s = slope_rate.astype(jnp.float32)
            arr = jnp.arange(1, BLK + 1, dtype=jnp.float32)
            q_decay = jnp.exp(-s * arr[:, None])
            k_decay = jnp.exp(-s * (BLK - arr)[:, None])
            idx = arr[:, None] - arr[None, :]
            diag_decay = jnp.where(idx >= 0, jnp.exp(-s * idx), 0.0)
            block_decay = jnp.exp(-s * BLK)
            qb = q.reshape(b, h, nb, BLK, d).transpose(2, 0, 1, 3, 4)
            kb = k.reshape(b, h, nb, BLK, d).transpose(2, 0, 1, 3, 4)
            vb = v.reshape(b, h, nb, BLK, d).transpose(2, 0, 1, 3, 4)

            def step(kv, blk):
                qi, ki, vi = blk
                o_inter = jnp.einsum('bhmd,bhde->bhme', qi * q_decay, kv)
                qk = jnp.einsum('bhmd,bhnd->bhmn', qi, ki) * diag_decay
                o_intra = jnp.einsum('bhmn,bhne->bhme', qk, vi)
                kv_new = block_decay * kv + jnp.einsum('bhmd,bhme->bhde', ki * k_decay, vi)
                return (kv_new, o_inter + o_intra)
            kv0 = jnp.zeros((b, h, d, d), dtype=jnp.float32)
            _, out = jax.lax.scan(step, kv0, (qb, kb, vb))
            out = out.transpose(1, 2, 0, 3, 4).reshape(b, h, n, d)
            out = out.transpose(0, 2, 1, 3).reshape(b, n, h * d)
            var = jnp.mean(out * out, axis=-1, keepdims=True)
            out = norm_w * (out * jax.lax.rsqrt(var + EPS))
            gate = jax.nn.sigmoid(jnp.einsum('bnf,of->bno', x, w_gate))
            return jnp.einsum('bno,fo->bnf', gate * out, w_out)
        key = jax.random.key(seed)
        ks = jax.random.split(key, 5)
        scale = 0.02
        x = jax.random.normal(ks[0], (B, N, H), dtype=jnp.float32)
        slopes = (1.0 / 2.0 ** (8.0 * np.arange(1, NH + 1) / NH)).astype(np.float32)
        slope_rate = jnp.asarray(slopes).reshape(NH, 1, 1)
        w_qkv = jax.random.normal(ks[1], (3 * NH * HD, H), dtype=jnp.float32) * scale
        w_gate = jax.random.normal(ks[2], (NH * HD, H), dtype=jnp.float32) * scale
        w_out = jax.random.normal(ks[3], (H, NH * HD), dtype=jnp.float32) * scale
        norm_w = jnp.ones((NH * HD,), dtype=jnp.float32)
        return {'hidden_states': x, 'slope_rate': slope_rate, 'w_qkv': w_qkv, 'w_gate': w_gate, 'w_out': w_out, 'norm_w': norm_w}
    _L0_attn_all = _L0_attn_setup()
    _L0_attn_in = {k: v for k, v in _L0_attn_all.items() if k in ('slope_rate', 'w_qkv', 'w_gate', 'w_out', 'norm_w')}
    del _L0_attn_all

    def _L0_xattn_setup():
        import jax, jax.numpy as jnp
        import numpy as np
        B_DIM, T_DIM, C_DIM = (16, 128, 256)

        def _wkv(w, u, k, v):
            Bn, Tn, Cn = k.shape
            NEG_INF = jnp.float32(-1e+38)

            def step(carry, kv_t):
                p, q, o = carry
                kt, vt = kv_t
                no = jnp.maximum(o, u + kt)
                A = jnp.exp(o - no)
                E = jnp.exp(u + kt - no)
                y = (A * p + E * vt) / (A * q + E)
                no2 = jnp.maximum(w + o, kt)
                A2 = jnp.exp(w + o - no2)
                E2 = jnp.exp(kt - no2)
                return ((A2 * p + E2 * vt, A2 * q + E2, no2), y)
            init = (jnp.zeros((Bn, Cn), k.dtype), jnp.zeros((Bn, Cn), k.dtype), jnp.full((Bn, Cn), NEG_INF, k.dtype))
            kT = jnp.moveaxis(k, 1, 0)
            vT = jnp.moveaxis(v, 1, 0)
            _, yT = jax.lax.scan(step, init, (kT, vT))
            return jnp.moveaxis(yT, 0, 1)
        key = jax.random.key(seed)
        k1, k2, k3, k4 = jax.random.split(key, 4)
        w = -jnp.exp(jax.random.normal(k1, (C_DIM,), jnp.float32))
        u = jax.random.normal(k2, (C_DIM,), jnp.float32)
        k = jax.random.normal(k3, (B_DIM, T_DIM, C_DIM), jnp.float32)
        v = jax.random.normal(k4, (B_DIM, T_DIM, C_DIM), jnp.float32)
        return {'B': B_DIM, 'T': T_DIM, 'C': C_DIM, 'w': w, 'u': u, 'k': k, 'v': v}
    _L0_xattn_all = _L0_xattn_setup()
    _L0_xattn_in = {k: v for k, v in _L0_xattn_all.items() if k in ('w', 'u')}
    del _L0_xattn_all

    def _L0_ffn_setup():
        import jax, jax.numpy as jnp
        import numpy as np
        from jax import lax
        DIM = 256
        E = 8
        K = 2
        RANK = 32
        CAP_FACTOR = 1.25

        def gelu(x):
            return jax.nn.gelu(x, approximate=False)

        def _moe_forward(x, gate_w, w1, b1, w2, b2, wd, wu, sw1, sb1, sw2, sb2, swd, swu):
            B, S, D = x.shape
            T = B * S
            cap = max(1, int(T * CAP_FACTOR / E))
            xt = x.reshape(T, D)
            logits = xt @ gate_w
            probs_full = jax.nn.softmax(logits, axis=-1)
            top_p, top_i = lax.top_k(probs_full, K)
            out = jnp.zeros_like(xt)
            for k in range(K):
                e = top_i[:, k]
                w = top_p[:, k]
                onehot = jax.nn.one_hot(e, E, dtype=jnp.int32)
                pos_all = jnp.cumsum(onehot, axis=0) - 1
                pos = jnp.take_along_axis(pos_all, e[:, None], axis=1)[:, 0]
                keep = pos < cap
                pos_c = jnp.where(keep, pos, cap)
                buf = jnp.zeros((E, cap, D), x.dtype).at[e, pos_c].set(xt * keep[:, None].astype(x.dtype), mode='drop')
                h = gelu(jnp.einsum('ecd,edf->ecf', buf, w1) + b1[:, None, :])
                y = jnp.einsum('ecf,efd->ecd', h, w2) + b2[:, None, :]
                a = jnp.einsum('ecr,erd->ecd', gelu(jnp.einsum('ecd,edr->ecr', buf, wd)), wu)
                y = y + a
                tok = y[e, jnp.minimum(pos_c, cap - 1)]
                out = out + tok * keep[:, None].astype(x.dtype) * w[:, None]
            sh = gelu(xt @ sw1 + sb1) @ sw2 + sb2
            sh = sh + gelu(xt @ swd) @ swu
            out = out + 0.2 * sh
            return out.reshape(B, S, D)
        key = jax.random.key(seed)
        ks = jax.random.split(key, 16)
        s = 0.02
        d, h = (DIM, 4 * DIM)
        inp = {'x': jax.random.normal(ks[0], (4, 256, d), dtype=jnp.float32), 'gate_w': jax.random.normal(ks[1], (d, E), dtype=jnp.float32) * s, 'w1': jax.random.normal(ks[2], (E, d, h), dtype=jnp.float32) * s, 'b1': jnp.zeros((E, h), dtype=jnp.float32), 'w2': jax.random.normal(ks[3], (E, h, d), dtype=jnp.float32) * s, 'b2': jnp.zeros((E, d), dtype=jnp.float32), 'wd': jax.random.normal(ks[4], (E, d, RANK), dtype=jnp.float32) * s, 'wu': jax.random.normal(ks[5], (E, RANK, d), dtype=jnp.float32) * s, 'sw1': jax.random.normal(ks[6], (d, h), dtype=jnp.float32) * s, 'sb1': jnp.zeros((h,), dtype=jnp.float32), 'sw2': jax.random.normal(ks[7], (h, d), dtype=jnp.float32) * s, 'sb2': jnp.zeros((d,), dtype=jnp.float32), 'swd': jax.random.normal(ks[8], (d, RANK), dtype=jnp.float32) * s, 'swu': jax.random.normal(ks[9], (RANK, d), dtype=jnp.float32) * s}
        return inp
    _L0_ffn_all = _L0_ffn_setup()
    _L0_ffn_in = {k: v for k, v in _L0_ffn_all.items() if k in ('gate_w', 'w1', 'b1', 'w2', 'b2', 'wd', 'wu', 'sw1', 'sb1', 'sw2', 'sb2', 'swd', 'swu')}
    del _L0_ffn_all
    return {'x': x, 'ctx_2048': ctx_2048, 'L0_attn_slope_rate': _L0_attn_in['slope_rate'], 'L0_attn_w_qkv': _L0_attn_in['w_qkv'], 'L0_attn_w_gate': _L0_attn_in['w_gate'], 'L0_attn_w_out': _L0_attn_in['w_out'], 'L0_attn_norm_w': _L0_attn_in['norm_w'], 'L0_xattn_w': _L0_xattn_in['w'], 'L0_xattn_u': _L0_xattn_in['u'], 'L0_ffn_gate_w': _L0_ffn_in['gate_w'], 'L0_ffn_w1': _L0_ffn_in['w1'], 'L0_ffn_b1': _L0_ffn_in['b1'], 'L0_ffn_w2': _L0_ffn_in['w2'], 'L0_ffn_b2': _L0_ffn_in['b2'], 'L0_ffn_wd': _L0_ffn_in['wd'], 'L0_ffn_wu': _L0_ffn_in['wu'], 'L0_ffn_sw1': _L0_ffn_in['sw1'], 'L0_ffn_sb1': _L0_ffn_in['sb1'], 'L0_ffn_sw2': _L0_ffn_in['sw2'], 'L0_ffn_sb2': _L0_ffn_in['sb2'], 'L0_ffn_swd': _L0_ffn_in['swd'], 'L0_ffn_swu': _L0_ffn_in['swu']}

def reference(x, ctx_2048, L0_attn_slope_rate, L0_attn_w_qkv, L0_attn_w_gate, L0_attn_w_out, L0_attn_norm_w, L0_xattn_w, L0_xattn_u, L0_ffn_gate_w, L0_ffn_w1, L0_ffn_b1, L0_ffn_w2, L0_ffn_b2, L0_ffn_wd, L0_ffn_wu, L0_ffn_sw1, L0_ffn_sb1, L0_ffn_sw2, L0_ffn_sb2, L0_ffn_swd, L0_ffn_swu):
    import jax
    import jax.numpy as jnp

    def _L0_attn_ref(hidden_states, slope_rate, w_qkv, w_gate, w_out, norm_w):
        import jax, jax.numpy as jnp
        import numpy as np
        B, N, H = (2, 512, 256)
        NH, HD = (16, 128)
        BLK = 32
        EPS = 1e-06

        def _lightning_attn(x, slope_rate, w_qkv, w_gate, w_out, norm_w):
            b, n, _ = x.shape
            h, d = (NH, HD)
            nb = n // BLK
            qkv = jax.nn.silu(jnp.einsum('bnf,of->bno', x, w_qkv))
            qkv = qkv.reshape(b, n, h, 3 * d)
            q, k, v = jnp.split(qkv, 3, axis=-1)
            q = q.transpose(0, 2, 1, 3)
            k = k.transpose(0, 2, 1, 3)
            v = v.transpose(0, 2, 1, 3)
            s = slope_rate.astype(jnp.float32)
            arr = jnp.arange(1, BLK + 1, dtype=jnp.float32)
            q_decay = jnp.exp(-s * arr[:, None])
            k_decay = jnp.exp(-s * (BLK - arr)[:, None])
            idx = arr[:, None] - arr[None, :]
            diag_decay = jnp.where(idx >= 0, jnp.exp(-s * idx), 0.0)
            block_decay = jnp.exp(-s * BLK)
            qb = q.reshape(b, h, nb, BLK, d).transpose(2, 0, 1, 3, 4)
            kb = k.reshape(b, h, nb, BLK, d).transpose(2, 0, 1, 3, 4)
            vb = v.reshape(b, h, nb, BLK, d).transpose(2, 0, 1, 3, 4)

            def step(kv, blk):
                qi, ki, vi = blk
                o_inter = jnp.einsum('bhmd,bhde->bhme', qi * q_decay, kv)
                qk = jnp.einsum('bhmd,bhnd->bhmn', qi, ki) * diag_decay
                o_intra = jnp.einsum('bhmn,bhne->bhme', qk, vi)
                kv_new = block_decay * kv + jnp.einsum('bhmd,bhme->bhde', ki * k_decay, vi)
                return (kv_new, o_inter + o_intra)
            kv0 = jnp.zeros((b, h, d, d), dtype=jnp.float32)
            _, out = jax.lax.scan(step, kv0, (qb, kb, vb))
            out = out.transpose(1, 2, 0, 3, 4).reshape(b, h, n, d)
            out = out.transpose(0, 2, 1, 3).reshape(b, n, h * d)
            var = jnp.mean(out * out, axis=-1, keepdims=True)
            out = norm_w * (out * jax.lax.rsqrt(var + EPS))
            gate = jax.nn.sigmoid(jnp.einsum('bnf,of->bno', x, w_gate))
            return jnp.einsum('bno,fo->bnf', gate * out, w_out)
        return _lightning_attn(hidden_states, slope_rate, w_qkv, w_gate, w_out, norm_w)

    def _L0_xattn_ref(B, T, C, w, u, k, v):
        import jax, jax.numpy as jnp
        import numpy as np
        B_DIM, T_DIM, C_DIM = (16, 128, 256)

        def _wkv(w, u, k, v):
            Bn, Tn, Cn = k.shape
            NEG_INF = jnp.float32(-1e+38)

            def step(carry, kv_t):
                p, q, o = carry
                kt, vt = kv_t
                no = jnp.maximum(o, u + kt)
                A = jnp.exp(o - no)
                E = jnp.exp(u + kt - no)
                y = (A * p + E * vt) / (A * q + E)
                no2 = jnp.maximum(w + o, kt)
                A2 = jnp.exp(w + o - no2)
                E2 = jnp.exp(kt - no2)
                return ((A2 * p + E2 * vt, A2 * q + E2, no2), y)
            init = (jnp.zeros((Bn, Cn), k.dtype), jnp.zeros((Bn, Cn), k.dtype), jnp.full((Bn, Cn), NEG_INF, k.dtype))
            kT = jnp.moveaxis(k, 1, 0)
            vT = jnp.moveaxis(v, 1, 0)
            _, yT = jax.lax.scan(step, init, (kT, vT))
            return jnp.moveaxis(yT, 0, 1)
        return _wkv(w, u, k, v)

    def _L0_ffn_ref(x, gate_w, w1, b1, w2, b2, wd, wu, sw1, sb1, sw2, sb2, swd, swu):
        import jax, jax.numpy as jnp
        import numpy as np
        from jax import lax
        DIM = 256
        E = 8
        K = 2
        RANK = 32
        CAP_FACTOR = 1.25

        def gelu(x):
            return jax.nn.gelu(x, approximate=False)

        def _moe_forward(x, gate_w, w1, b1, w2, b2, wd, wu, sw1, sb1, sw2, sb2, swd, swu):
            B, S, D = x.shape
            T = B * S
            cap = max(1, int(T * CAP_FACTOR / E))
            xt = x.reshape(T, D)
            logits = xt @ gate_w
            probs_full = jax.nn.softmax(logits, axis=-1)
            top_p, top_i = lax.top_k(probs_full, K)
            out = jnp.zeros_like(xt)
            for k in range(K):
                e = top_i[:, k]
                w = top_p[:, k]
                onehot = jax.nn.one_hot(e, E, dtype=jnp.int32)
                pos_all = jnp.cumsum(onehot, axis=0) - 1
                pos = jnp.take_along_axis(pos_all, e[:, None], axis=1)[:, 0]
                keep = pos < cap
                pos_c = jnp.where(keep, pos, cap)
                buf = jnp.zeros((E, cap, D), x.dtype).at[e, pos_c].set(xt * keep[:, None].astype(x.dtype), mode='drop')
                h = gelu(jnp.einsum('ecd,edf->ecf', buf, w1) + b1[:, None, :])
                y = jnp.einsum('ecf,efd->ecd', h, w2) + b2[:, None, :]
                a = jnp.einsum('ecr,erd->ecd', gelu(jnp.einsum('ecd,edr->ecr', buf, wd)), wu)
                y = y + a
                tok = y[e, jnp.minimum(pos_c, cap - 1)]
                out = out + tok * keep[:, None].astype(x.dtype) * w[:, None]
            sh = gelu(xt @ sw1 + sb1) @ sw2 + sb2
            sh = sh + gelu(xt @ swd) @ swu
            out = out + 0.2 * sh
            return out.reshape(B, S, D)
        return _moe_forward(x, gate_w, w1, b1, w2, b2, wd, wu, sw1, sb1, sw2, sb2, swd, swu)
    x = _layernorm(x + _L0_attn_ref(x, L0_attn_slope_rate, L0_attn_w_qkv, L0_attn_w_gate, L0_attn_w_out, L0_attn_norm_w), axis=-1)
    x = _layernorm(x + _L0_xattn_ref(16, 128, 256, L0_xattn_w, L0_xattn_u, x, ctx_2048), axis=-1)
    x = _layernorm(x + _L0_ffn_ref(x, L0_ffn_gate_w, L0_ffn_w1, L0_ffn_b1, L0_ffn_w2, L0_ffn_b2, L0_ffn_wd, L0_ffn_wu, L0_ffn_sw1, L0_ffn_sb1, L0_ffn_sw2, L0_ffn_sb2, L0_ffn_swd, L0_ffn_swu), axis=-1)
    return x

_drawn_inputs = setup_inputs


def setup_inputs(seed=0):
    import zlib

    import numpy as np

    out = dict(_drawn_inputs(seed))
    spreads = {'L0_attn_norm_w': (1.0, 0.2),
     'L0_ffn_b1': (0.0, 0.8),
     'L0_ffn_b2': (0.0, 0.322),
     'L0_ffn_sb1': (0.0, 0.8),
     'L0_ffn_sb2': (0.0, 0.375)}
    factors = {'L0_ffn_wd': 8.0, 'L0_ffn_wu': 8.0, 'L0_ffn_swd': 8.0, 'L0_ffn_swu': 8.0}
    for name, (base, spread) in spreads.items():
        noise = np.random.default_rng([zlib.crc32(name.encode()), seed]).standard_normal(out[name].shape)
        drawn = base * np.exp(spread * noise) if base else spread * noise
        out[name] = jnp.asarray(drawn.astype(out[name].dtype))
    for name, factor in factors.items():
        out[name] = (out[name] * factor).astype(out[name].dtype)
    return out
```

```python
from contextlib import ExitStack

import numpy as np

import concourse.bass as bass
from concourse import mybir

F32 = mybir.dt.float32
BF16 = mybir.dt.bfloat16
U32 = mybir.dt.uint32
ALU = mybir.AluOpType
ACT = mybir.ActivationFunctionType
AX = mybir.AxisListType

P = 128
B, T, C = 16, 128, 256
NH, HD = 16, 128
NP = NH // 2
CC = C // P
GB = 4
NG = B // GB
GT = GB * T
NTOK = B * T
NT = NTOK // P
E, K, HID, RANK = 8, 2, 1024, 32
FC = HID // P
CAP = int(NTOK * 1.25 / E)
SLOTS = K * CAP
ST = SLOTS // P
ROW = C + 4
NOWHERE = 1 << 20
EPS_RMS, EPS_LN = 1e-6, 1e-5
NEG = -1e38

PIECES = {"qk0": (0, 512), "v": (512, 1024), "g0": (1024, 1280), "qk1": (1280, 1792), "g1": (1792, 2048)}
WCOLS = 2048


def wait_apart(eng, sem, value, waits):
    eng.wait_ge(sem, value)
    eng.sem_inc(waits, 1)


class Count:

    def __init__(self, eng, sem):
        self.eng, self.sem, self.base, self.n = eng, sem, 0, 0

    def at(self, base):
        self.base, self.n = base, 0

    def link(self, ins, waits=None):
        ins.then_inc(self.sem, 1)
        self.n += 1
        self.eng.wait_ge(self.sem, self.base + self.n)
        if waits is not None:
            self.eng.sem_inc(waits, 1)


def decoder_layer(nc, xT, x, ctxT, wp, wout, norm_w, slope, mix_w, mix_u, gate_w,
                  w1, b1, w2, wd, wu, sw1, sb1, sw2, swd, swu, out):
    ctx = ExitStack()
    with ctx:
        def sb(name, shape, dt=F32):
            return ctx.enter_context(nc.sbuf_tensor(name, shape, dt))

        def pb(name, shape, dt=F32):
            return ctx.enter_context(nc.psum_tensor(name, shape, dt))

        def sem(name):
            return ctx.enter_context(nc.semaphore(name))

        slot_rows = nc.dram_tensor("slot_rows", [E * SLOTS, ROW], F32).ap()
        expert_out = nc.dram_tensor("expert_out", [K * NTOK, C], F32).ap()

        proj_ps = [pb(f"proj_ps{i}", [P, GT]) for i in range(2)]
        val_ps = pb("val_ps", [P, GB, 2 * HD])
        score_ps = pb("score_ps", [P, GT])
        mixed_ps = pb("mixed_ps", [P, GT])
        y_ps = pb("y_ps", [P, GB, C])

        region = sb("region", [P, 18432])

        def views(*shapes):
            at, found = 0, []
            for shape in shapes:
                n = int(np.prod(shape))
                v = region[:, at:at + n]
                found.append(v if len(shape) == 1 else v.rearrange("p (a b) -> p a b", b=shape[1]))
                at += n
            assert at <= region.shape[1]
            return found

        (x_slot, w_slot, wout_sb, decay, tanh_v, v_sb, *rest) = views(
            (CC, GT), (WCOLS,), (NH, C), (NH, T), (GB, 2 * HD), (GB, 2 * HD), *[(GT,)] * 14)
        tanh_qk, tanh_g, q_sb, k_sb, masked, square, gated = (rest[i:i + 2] for i in range(0, 14, 2))
        hid_sb, rows_in, slotT, rows_out, w1_sb, w2_sb, low_all = views(
            (FC, SLOTS), (ST, ROW), (CC, SLOTS), (ST, C), (CC, HID), (FC, C), (SLOTS,))
        low_sb = low_all[0:RANK + 1, :]
        dist = sb("dist", [P, T])
        norm_sb = sb("norm_sb", [P, NH])
        slope_sb = sb("slope_sb", [P, NH])
        neg_slope = sb("neg_slope", [P, NH])
        sq_sum = sb("sq_sum", [P, GT])
        zeros_b = sb("zeros_b", [P, GT], BF16)
        ones_b = sb("ones_b", [P, P], BF16)
        prefix_b = sb("prefix_b", [P, P], BF16)
        ones_f = sb("ones_f", [P, 1])
        ident = sb("ident", [P, P])
        init_row = sb("init_row", [P, ROW])
        y_all = sb("y_all", [P, NT, C])
        ms_all = sb("ms_all", [P, NT])
        x_in = sb("x_in", [P, GB, C])
        x2T = sb("x2T", [P, CC, NTOK])
        half = sb("half", [P, NT])
        SEG = CC * GB
        GL = SEG * T
        mixw_sb, mixu_sb = sb("mixw_sb", [P, CC]), sb("mixu_sb", [P, CC])
        step_w, step_u = sb("step_w", [P, GL]), sb("step_u", [P, GL])
        ctx_sb = sb("ctx_sb", [P, GL])
        key = sb("key", [P, GL])
        top = sb("top", [P, 1 + GL])
        num = sb("num", [P, 1 + GL])
        den = sb("den", [P, 1 + GL])
        diff = sb("diff", [P, GL])
        keep_e, new_e = sb("keep_e", [P, GL]), sb("new_e", [P, GL])
        keep_d, new_d = sb("keep_d", [P, GL]), sb("new_d", [P, GL])
        mix = sb("mix", [P, GL])
        pre = sb("pre", [P, GB, C])
        x1 = sb("x1", [P, GB, C])
        row = sb("row", [P, GB, ROW])
        x2T_now = sb("x2T_now", [P, CC, GT])
        stats, moments = sb("stats", [P, GB, 6]), sb("moments", [P, GB, 2])
        var_eps, rstd = sb("var_eps", [P, NT]), sb("rstd", [P, NT])
        gate_sb = sb("gate_sb", [P, CC, E])
        token = sb("token", [P, NT])
        expert8 = sb("expert8", [P, E])
        choice = sb("choice", [P, K])
        logit, prob = sb("logit", [P, GB, E]), sb("prob", [P, GB, E])
        peak, total = sb("peak", [P, GB]), sb("total", [P, GB])
        best = sb("best", [P, GB, E])
        best_at = sb("best_at", [P, GB, E], U32)
        best_f = sb("best_f", [P, GB, E])
        onehot = sb("onehot", [P, GB, K, E])
        onehot_b = sb("onehot_b", [P, GB, K * E], BF16)
        seen, seen_b = sb("seen", [P, K * E]), sb("seen_b", [P, K * E], BF16)
        group_sum = sb("group_sum", [P, K * E])
        picked = sb("picked", [P, GB, K, E])
        pos = sb("pos", [P, GB, K])
        over = sb("over", [P, GB, K])
        slot_f = sb("slot_f", [P, GB, K])
        slot_at = sb("slot_at", [P, GB, K], U32)
        wd_sb, wu_sb, b1_sb = sb("wd_sb", [P, CC, RANK]), sb("wu_sb", [RANK + 1, C]), sb("b1_sb", [P, FC])
        weight, target_f = sb("weight", [P, ST]), sb("target_f", [P, ST])
        target = sb("target", [P, ST], U32)

        rms, rms_var = sb("rms", [P, NT]), sb("rms_var", [P, NT])

        s = {n: sem(n) for n in (
            "const_ld dve_const act_const pool_const x_ld w_qk0 w_v w_g0 w_qk1 w_g1 proj0_done proj1_done "
            "proj0_free proj1_free val_done val_free score_done masked_done tanh_done mixed_done square_done "
            "gated_done sq_added sq_zeroed y_done y_evac ms_done ms_evac "
            "x_in_moved ctx_ld var_done rstd_done x1_done key_turned key_copied args_done exps_done mix_done "
            "mix_turned x2_done x2_turned x2_copied base_copied logit_done shifted_done prob_done onehot_done "
            "pos_done rows_done scattered "
            "w_up_ld w_down_ld low_ready up_done gelu_done down_done down_evac rows_ld slots_turned slots_copied "
            "meta_done up_end combined out_ld sum_done "
            "dve_chain dve_waits pe_waits pool_waits sp_waits").split()}

        ONE = 1
        from_one = ("proj0_done proj1_done val_done x2_done slots_turned meta_done sum_done ms_done proj0_free "
                    "proj1_free masked_done gated_done val_free y_evac ms_evac gelu_done down_evac slots_copied "
                    "mix_done").split()

        y_flat = y_ps[:].rearrange("p b c -> p (b c)")

        block = ctx.enter_context(nc.Block())

        @block.sync
        def _(sp):
            consts = [(norm_sb[:], norm_w), (slope_sb[:], slope.rearrange("(a h) -> a h", a=1).to_broadcast([P, NH])),
                      (wout_sb, wout), (mixw_sb[:], mix_w), (mixu_sb[:], mix_u), (gate_sb[:], gate_w)]
            for to, of in consts:
                sp.dma_start(to, of).then_inc(s["const_ld"], 16)

            with sp.Fori(0, NG) as g:
                wait_apart(sp, s["proj1_done"], ONE + 3 * NP * g, s["sp_waits"])
                sp.dma_start(x_slot, xT[g]).then_inc(s["x_ld"], 16)
                with sp.Fori(0, NP) as hp:
                    it = g * NP + hp
                    for name, used, n in (("qk0", "val_done", it), ("v", "val_done", it), ("g0", "proj0_done", 3 * it),
                                          ("qk1", "proj0_done", 3 * it), ("g1", "proj1_done", 3 * it)):
                        a, b = PIECES[name]
                        wait_apart(sp, s[used], ONE + n, s["sp_waits"])
                        sp.dma_start(w_slot[:, a:b], wp[hp, :, a:b]).then_inc(s["w_" + name], 16)

            def load_up(w1_of, wd_of, b1_of):
                sp.dma_start(w1_sb, w1_of).then_inc(s["w_up_ld"], 16)
                sp.dma_start(wd_sb[:], wd_of).then_inc(s["w_up_ld"], 16)
                sp.dma_start(b1_sb[:], b1_of).then_inc(s["w_up_ld"], 16)

            def load_down(w2_of, wu_of):
                sp.dma_start(w2_sb, w2_of).then_inc(s["w_down_ld"], 16)
                sp.dma_start(wu_sb[:], wu_of).then_inc(s["w_down_ld"], 16)

            sp.wait_ge(s["y_evac"], ONE + NG)
            sp.wait_ge(s["ms_evac"], ONE + NG)
            load_up(sw1, swd, sb1)
            load_down(sw2, swu)

            with sp.Fori(0, NG) as g:
                wait_apart(sp, s["x2_done"], ONE + g, s["sp_waits"])
                sp.dma_start(x_in[:], x[g]).then_inc(s["x_in_moved"], 16)
                sp.dma_start(ctx_sb[:], ctxT[g]).then_inc(s["ctx_ld"], 16)

            sp.wait_ge(s["scattered"], 16 + 16 * NT * K)
            with sp.Fori(0, E) as e:
                wait_apart(sp, s["up_end"], e + NG, s["sp_waits"])
                load_up(w1[e], wd[e], b1[e])
                wait_apart(sp, s["slots_turned"], ONE + CC * e, s["sp_waits"])
                wait_apart(sp, s["meta_done"], ONE + e, s["sp_waits"])
                sp.dma_start(rows_in, slot_rows.rearrange("(e j p) c -> e p j c", p=P, j=ST)[e]).then_inc(s["rows_ld"], 16)
                wait_apart(sp, s["down_done"], GB * NG + ST * e, s["sp_waits"])
                load_down(w2[e], wu[e])

            sp.wait_ge(s["combined"], 16 + 16 * ST * E)
            with sp.Fori(0, NG) as g:
                wait_apart(sp, s["sum_done"], ONE + g, s["sp_waits"])
                for k in range(K):
                    sp.dma_start([x1, pre][k][:], expert_out.rearrange("(k g b p) c -> k g p b c", k=K, g=NG, p=P)[k, g])\
                      .then_inc(s["out_ld"], 16)
                wait_apart(sp, s["sum_done"], ONE + g + 1, s["sp_waits"])
                sp.dma_start(out[g], x_in[:]).then_inc(s["x_in_moved"], 16)
            sp.wait_ge(s["x_in_moved"], 2 * 16 * NG)

        @block.gpsimd
        def _(pool):
            g_ = nc.gpsimd

            waits = s["pool_waits"]

            def const(ins):
                ins.then_inc(s["pool_const"], 1)

            const(g_.memset(zeros_b[:], 0.0))
            const(g_.memset(ones_b[:], 1.0))
            const(g_.memset(ones_f[:], 1.0))
            const(g_.memset(ident[:], 0.0))
            const(g_.memset(half[:], -0.5))
            const(g_.iota(dist[:], [[1, T]], base=0, channel_multiplier=-1, allow_small_or_imprecise_dtypes=True))
            const(g_.iota(token[:], [[P, NT]], base=0, channel_multiplier=1, allow_small_or_imprecise_dtypes=True))
            const(g_.iota(expert8[:], [[1, E]], base=0, channel_multiplier=0, allow_small_or_imprecise_dtypes=True))
            const(g_.iota(choice[:], [[CAP, K]], base=-1, channel_multiplier=0, allow_small_or_imprecise_dtypes=True))
            const(g_.memset(init_row[:, 0:C], 0.0))
            const(g_.memset(init_row[:, C:C + K], float(NOWHERE)))
            const(g_.memset(init_row[:, C + K:ROW], 0.0))
            for r in range(2):
                g_.memset(square[r], 0.0).then_inc(s["sq_added"], 1)
            pool.wait_ge(s["pool_const"], 12)
            const(g_.affine_select(out=ident[:], in_=ident[:], compare_op=ALU.not_equal, fill=1.0, base=0,
                                   pattern=[[-1, P]], channel_multiplier=1))
            const(g_.affine_select(out=prefix_b[:], in_=ones_b[:], compare_op=ALU.is_ge, fill=0.0, base=0,
                                   pattern=[[1, P]], channel_multiplier=-1))
            pool.dma_start(slot_rows.rearrange("(n p) c -> p n c", p=P),
                           init_row[:].unsqueeze(1).to_broadcast([P, E * ST, ROW])).then_inc(s["scattered"], 16)
            pool.dma_start(expert_out.rearrange("(n p) c -> p n c", p=P),
                           init_row[:, 0:C].unsqueeze(1).to_broadcast([P, K * NT, C])).then_inc(s["combined"], 16)
            pool.wait_ge(s["act_const"], 1)
            const(g_.affine_select(out=decay, in_=decay, compare_op=ALU.is_ge, fill=0.0, base=0,
                                   pattern=[[0, NH], [1, T]], channel_multiplier=-1))

            with pool.Fori(0, NG) as g:
                wait_apart(pool, s["ms_done"], ONE + g, waits)
                g_.memset(sq_sum[:], 0.0).then_inc(s["sq_zeroed"], 1)
                wait_apart(pool, s["sq_zeroed"], g + 1, waits)
                with pool.Fori(0, NP) as hp:
                    for r in range(2):
                        n = 2 * (g * NP + hp) + r
                        wait_apart(pool, s["square_done"], n + 1, waits)
                        wait_apart(pool, s["sq_added"], n + 2, waits)
                        g_.tensor_tensor(out=sq_sum[:], in0=sq_sum[:], in1=square[r], op=ALU.add).then_inc(s["sq_added"], 1)

            def inverse_root(n, to, of, width):
                wait_apart(pool, s["var_done"], n, waits)
                g_.tensor_tensor(out=to, in0=of, in1=half[:, 0:width], op=ALU.pow).then_inc(s["rstd_done"], 1)

            inverse_root(1, rms[:], rms_var[:], NT)
            pool.wait_ge(s["scattered"], 16)
            pool.wait_ge(s["combined"], 16)
            with pool.Fori(0, NG) as g:
                inverse_root(2 * g + 2, rstd[:, 0:GB], var_eps[:, 0:GB], GB)
                inverse_root(2 * g + 3, rstd[:, 0:GB], var_eps[:, 0:GB], GB)
                wait_apart(pool, s["rows_done"], g + 1, waits)
                for b in range(GB):
                    for k in range(K):
                        pool.indirect_dma_start(
                            slot_rows, bass.IndirectOffsetOnAxis(slot_at[:, b, k:k + 1], 0), row[:, b, :], None,
                            bounds_check=E * SLOTS - 1, oob_is_err=False).then_inc(s["scattered"], 16)

            with pool.Fori(0, E) as e:
                for j in range(ST):
                    wait_apart(pool, s["down_evac"], ONE + GB * NG + ST * e + j + 1, waits)
                    pool.indirect_dma_start(
                        expert_out, bass.IndirectOffsetOnAxis(target[:, j:j + 1], 0), rows_out[:, j, :], None,
                        bounds_check=K * NTOK - 1, oob_is_err=False).then_inc(s["combined"], 16)

            with pool.Fori(0, NG) as g:
                inverse_root(2 * NG + 2 + g, rstd[:, 0:GB], var_eps[:, 0:GB], GB)

        @block.tensor
        def _(pe):
            waits = s["pe_waits"]

            def project(bank, used, name, j=0):
                pe.wait_ge(s[f"proj{bank}_free"], ONE + used)
                for c in range(CC):
                    a = PIECES[name][0] + (j * CC + c) * HD
                    m = nc.tensor.matmul(proj_ps[bank][:], w_slot[:, a:a + HD], x_slot[:, c, :], start=(c == 0), stop=(c == CC - 1))
                m.then_inc(s[f"proj{bank}_done"], 1)

            def first_qk(it, j):
                pe.wait_ge(s["w_qk0"], 16 * it + 16)
                project(j, 3 * it, "qk0", j)

            def scores(it, r):
                pe.wait_ge(s["proj0_free"], ONE + 3 * it + 1 + 2 * r)
                pe.wait_ge(s["proj1_free"], ONE + 3 * it + 1 + r)
                pe.wait_ge(s["masked_done"], ONE + 2 * it + r)
                for b in range(GB):
                    t = slice(b * T, (b + 1) * T)
                    m = nc.tensor.matmul(score_ps[:, t], k_sb[r][:, t], q_sb[r][:, t], start=True, stop=True)
                m.then_inc(s["score_done"], 1)

            def mixes(it, r):
                pe.wait_ge(s["masked_done"], ONE + 2 * it + r + 1)
                pe.wait_ge(s["val_free"], ONE + it + 1)
                pe.wait_ge(s["gated_done"], ONE + 2 * it + r)
                for b in range(GB):
                    t = slice(b * T, (b + 1) * T)
                    m = nc.tensor.matmul(mixed_ps[:, t], v_sb[:, b, r * HD:(r + 1) * HD], masked[r][:, t], start=True, stop=True)
                m.then_inc(s["mixed_done"], 1)

            def outs(it, hp, r, last):
                pe.wait_ge(s["gated_done"], ONE + 2 * it + r + 1)
                for b in range(GB):
                    w = wout_sb[:, bass.ds(2 * hp + r, 1), :].rearrange("p a c -> p (a c)")
                    m = nc.tensor.matmul(y_ps[:, b, :], gated[r][:, b * T:(b + 1) * T], w, start=False, stop=last,
                                         skip_group_check=True)
                if last:
                    m.then_inc(s["y_done"], 1)

            def pair(g, hp, last):
                it = g * NP + hp
                pe.wait_ge(s["w_v"], 16 * it + 16)
                pe.wait_ge(s["val_free"], ONE + it)
                for b in range(GB):
                    for c in range(CC):
                        a = PIECES["v"][0] + c * 2 * HD
                        m = nc.tensor.matmul(val_ps[:, b, :], x_slot[:, c, b * T:(b + 1) * T], w_slot[:, a:a + 2 * HD],
                                             start=(c == 0), stop=(c == CC - 1))
                m.then_inc(s["val_done"], 1)
                scores(it, 0)
                pe.wait_ge(s["w_g0"], 16 * it + 16)
                project(0, 3 * it + 1, "g0")
                mixes(it, 0)
                pe.wait_ge(s["w_qk1"], 16 * it + 16)
                project(1, 3 * it + 1, "qk1", 0)
                outs(it, hp, 0, False)
                project(0, 3 * it + 2, "qk1", 1)
                pe.wait_ge(s["w_g1"], 16 * it + 16)
                project(1, 3 * it + 2, "g1")
                scores(it, 1)
                if not last:
                    first_qk(it + 1, 0)
                mixes(it, 1)
                if not last:
                    first_qk(it + 1, 1)
                outs(it, hp, 1, last)

            pe.wait_ge(s["pool_const"], 15)
            pe.wait_ge(s["dve_const"], 3)
            with pe.Fori(0, NG) as g:
                pe.wait_ge(s["x_ld"], 16 * g + 16)
                first_qk(g * NP, 0)
                first_qk(g * NP, 1)
                pe.wait_ge(s["y_evac"], ONE + g)
                for b in range(0, GB, 2):
                    nc.tensor.matmul(y_ps[:, b:b + 2, :], zeros_b[:, 0:P], zeros_b[:], start=True, stop=False,
                                     skip_group_check=True)
                wait_apart(pe, s["ms_evac"], ONE + g, waits)
                with pe.Fori(0, NP - 1) as hp:
                    pair(g, hp, False)
                pair(g, NP - 1, True)
                pe.wait_ge(s["sq_added"], 2 * NP * (g + 1) + 2)
                pe.wait_ge(s["masked_done"], ONE + 2 * NP * (g + 1))
                for b in range(GB):
                    m = nc.tensor.matmul(score_ps[:, b:b + 1], sq_sum[:, b * T:(b + 1) * T], ones_f[:], start=True, stop=True)
                m.then_inc(s["ms_done"], 1)

            def turn(pairs, done):
                for to, of in pairs:
                    m = nc.tensor.transpose(to, of, ident[:])
                m.then_inc(s[done], 1)

            halves = [(b, c) for c in range(CC) for b in range(GB)]
            pe.wait_ge(s["y_evac"], ONE + NG)
            pe.wait_ge(s["ms_evac"], ONE + NG)
            with pe.Fori(0, NG) as g:
                pe.wait_ge(s["x1_done"], g + 1)
                turn([(y_flat[:, (c * GB + b) * T:(c * GB + b + 1) * T], x1[:, b, c * P:(c + 1) * P]) for b, c in halves], "key_turned")
                pe.wait_ge(s["mix_done"], ONE + g + 1)
                turn([(val_ps[:, b, c * P:(c + 1) * P], mix[:, (c * GB + b) * T:(c * GB + b + 1) * T]) for b, c in halves], "mix_turned")
                pe.wait_ge(s["x2_done"], ONE + g + 1)
                turn([(proj_ps[c][:, b * T:(b + 1) * T], row[:, b, c * P:(c + 1) * P]) for b, c in halves], "x2_turned")
                pe.wait_ge(s["x2_copied"], 2 * CC * (g + 1))
                for b in range(GB):
                    for c in range(CC):
                        m = nc.tensor.matmul(score_ps[:, b * E:(b + 1) * E], x2T_now[:, c, b * T:(b + 1) * T], gate_sb[:, c, :],
                                             start=(c == 0), stop=(c == CC - 1))
                m.then_inc(s["logit_done"], 1)
                pe.wait_ge(s["onehot_done"], g + 1)
                for b in range(GB):
                    parts = [(prefix_b, onehot_b[:, b, :])] + [(ones_b, onehot_b[:, i, :]) for i in range(b)] + [(ones_b, seen_b[:])]
                    for i, (m1, m2) in enumerate(parts):
                        m = nc.tensor.matmul(mixed_ps[:, b * K * E:(b + 1) * K * E], m1[:], m2, start=(i == 0), stop=(i == len(parts) - 1))
                m.then_inc(s["pos_done"], 1)

            banks = [proj_ps[0], proj_ps[1], score_ps, mixed_ps]

            def up(unit, base, cols_, lhs, rhs):
                if unit >= len(banks):
                    wait_apart(pe, s["gelu_done"], ONE + base + unit - len(banks) + 1, waits)
                n = lhs(0).shape[1]
                for c in range(CC):
                    m = nc.tensor.matmul(banks[unit % len(banks)][0:n, 0:cols_], lhs(c), rhs(c), start=(c == 0), stop=(c == CC - 1))
                m.then_inc(s["up_done"], 1)

            def down(j, base):
                pe.wait_ge(s["down_evac"], ONE + base + max(j - 1, 0))
                to = val_ps[:, 2 * (j % 2), :]
                t = slice(j * P, (j + 1) * P)
                for f in range(FC):
                    nc.tensor.matmul(to, hid_sb[:, f, t], w2_sb[:, f, :], start=(f == 0), stop=False)
                nc.tensor.matmul(to, low_sb[:, t], wu_sb[:], start=False, stop=True).then_inc(s["down_done"], 1)

            pe.wait_ge(s["w_up_ld"], 48)
            pe.wait_ge(s["low_ready"], 1)
            pe.wait_ge(s["rows_done"], NG)
            with pe.Fori(0, NG) as g:
                base = (FC + 1) * g
                pe.wait_ge(s["gelu_done"], ONE + base)
                now = x2T[:, :, bass.ds(g * GT, GT)]
                for f in range(FC):
                    up(f, base, GT, lambda c: w1_sb[:, c, f * P:(f + 1) * P], lambda c: now[:, c, :])
                up(FC, base, GT, lambda c: wd_sb[:, c, :], lambda c: now[:, c, :])
                pe.wait_ge(s["w_down_ld"], 32)
                pe.wait_ge(s["gelu_done"], ONE + base + FC + 1)
                for j in range(GB):
                    down(j, GB * g)
            with pe.Fori(0, E) as e:
                pe.wait_ge(s["rows_ld"], 16 * e + 16)
                for c in range(CC):
                    pe.wait_ge(s["slots_copied"], ONE + CC * e + c)
                    turn([(y_flat[:, j * P:(j + 1) * P], rows_in[:, j, c * P:(c + 1) * P]) for j in range(ST)], "slots_turned")
                pe.wait_ge(s["slots_copied"], ONE + CC * e + CC)
                pe.wait_ge(s["w_up_ld"], 48 * e + 96)
                base = (FC + 1) * NG + 2 * (FC + 1) * e
                for f in range(FC):
                    for h in range(2):
                        up(2 * f + h, base, CAP, lambda c: w1_sb[:, c, f * P:(f + 1) * P], lambda c: slotT[:, c, h * CAP:(h + 1) * CAP])
                for h in range(2):
                    up(2 * FC + h, base, CAP, lambda c: wd_sb[:, c, :], lambda c: slotT[:, c, h * CAP:(h + 1) * CAP])
                pe.wait_ge(s["w_down_ld"], 32 * e + 64)
                pe.wait_ge(s["gelu_done"], ONE + base + 2 * (FC + 1))
                for j in range(ST):
                    down(j, GB * NG + ST * e)

        @block.scalar
        def _(act):
            def tanh(n, bank, to, of, done="tanh_done"):
                act.wait_ge(s[bank + "_done"], ONE + n)
                nc.scalar.activation(to, of, ACT.Tanh, scale=0.5).then_inc(s[done], 1)

            def squares(it, r):
                act.wait_ge(s["mixed_done"], 2 * it + r + 1)
                act.wait_ge(s["sq_added"], 2 * it + r + 1)
                nc.scalar.activation(square[r], mixed_ps[:], ACT.Square).then_inc(s["square_done"], 1)

            def pair(g, hp, last):
                it = g * NP + hp
                tanh(it + 1, "val", tanh_v, val_ps[:])
                tanh(3 * it + 2, "proj0", tanh_g[0], proj_ps[0][:], "proj0_free")
                squares(it, 0)
                tanh(3 * it + 2, "proj1", tanh_qk[1], proj_ps[1][:])
                tanh(3 * it + 3, "proj0", tanh_qk[0], proj_ps[0][:])
                tanh(3 * it + 3, "proj1", tanh_g[1], proj_ps[1][:], "proj1_free")
                if not last:
                    tanh(3 * it + 4, "proj0", tanh_qk[0], proj_ps[0][:])
                squares(it, 1)
                if not last:
                    tanh(3 * it + 4, "proj1", tanh_qk[1], proj_ps[1][:])

            act.wait_ge(s["dve_const"], 2)
            for h in range(NH):
                m = nc.scalar.activation(decay[:, h, :], dist[:], ACT.Exp, scale=neg_slope[:, h:h + 1])
            m.then_inc(s["act_const"], 1)
            with act.Fori(0, NG) as g:
                for j in range(2):
                    tanh(3 * NP * g + 1, f"proj{j}", tanh_qk[j], proj_ps[j][:])
                with act.Fori(0, NP - 1) as hp:
                    pair(g, hp, False)
                pair(g, NP - 1, True)
                act.wait_ge(s["y_done"], g + 1)
                nc.scalar.copy(y_all[:, bass.ds(g * GB, GB), :], y_ps[:]).then_inc(s["y_evac"], 1)

            with act.Fori(0, NG) as g:
                act.wait_ge(s["key_turned"], g + 1)
                act.wait_ge(s["mix_done"], ONE + g)
                nc.scalar.copy(key[:], y_flat).then_inc(s["key_copied"], 1)
                for n, (keep, new) in enumerate(((keep_e, new_e), (keep_d, new_d))):
                    act.wait_ge(s["args_done"], 2 * g + n + 1)
                    nc.scalar.activation(keep[:], keep[:], ACT.Exp, scale=-1.0)
                    nc.scalar.activation(new[:], new[:], ACT.Exp).then_inc(s["exps_done"], 1)
                act.wait_ge(s["x2_turned"], g + 1)
                for c in range(CC):
                    nc.scalar.copy(x2T_now[:, c, :], proj_ps[c][:]).then_inc(s["x2_copied"], 1)
                    nc.scalar.copy(x2T[:, c, bass.ds(g * GT, GT)], proj_ps[c][:]).then_inc(s["x2_copied"], 1)
                nc.scalar.copy(y_all[:, bass.ds(g * GB, GB), :], row[:, :, 0:C]).then_inc(s["base_copied"], 1)
                act.wait_ge(s["shifted_done"], g + 1)
                nc.scalar.activation(prob[:], logit[:], ACT.Exp).then_inc(s["prob_done"], 1)

            def gelu(n, bank, to, bias):
                act.wait_ge(s["up_done"], n)
                nc.scalar.activation(to, bank, ACT.Gelu, bias=bias).then_inc(s["gelu_done"], 1)

            banks = [proj_ps[0], proj_ps[1], score_ps, mixed_ps]
            act.wait_ge(s["w_up_ld"], 48)
            with act.Fori(0, NG) as g:
                base = (FC + 1) * g
                for f in range(FC):
                    gelu(base + f + 1, banks[f % 4][:], hid_sb[:, f, 0:GT], b1_sb[:, f:f + 1])
                gelu(base + FC + 1, banks[FC % 4][0:RANK, :], low_sb[0:RANK, 0:GT], 0.0)
                act.sem_inc(s["up_end"], 1) if False else nc.scalar.activation(
                    ones_f[0:1, :], ones_f[0:1, :], ACT.Copy).then_inc(s["up_end"], 1)
            with act.Fori(0, E) as e:
                for c in range(CC):
                    act.wait_ge(s["slots_turned"], ONE + CC * e + c + 1)
                    nc.scalar.copy(slotT[:, c, :], y_flat[:, 0:SLOTS]).then_inc(s["slots_copied"], 1)
                act.wait_ge(s["w_up_ld"], 48 * e + 96)
                base = (FC + 1) * NG + 2 * (FC + 1) * e
                for u in range(2 * FC):
                    f, h = divmod(u, 2)
                    gelu(base + u + 1, banks[u % 4][:, 0:CAP], hid_sb[:, f, h * CAP:(h + 1) * CAP], b1_sb[:, f:f + 1])
                for u in (2 * FC, 2 * FC + 1):
                    h = u - 2 * FC
                    gelu(base + u + 1, banks[u % 4][0:RANK, 0:CAP], low_sb[0:RANK, h * CAP:(h + 1) * CAP], 0.0)
                nc.scalar.activation(ones_f[0:1, :], ones_f[0:1, :], ACT.Copy).then_inc(s["up_end"], 1)

        @block.vector
        def _(dve):
            v = nc.vector
            waits = s["dve_waits"]
            chain = Count(dve, s["dve_chain"])
            link = chain.link

            def scaled(n, r, to, ps, done):
                dve.wait_ge(s["tanh_done"], n)
                v.scalar_tensor_tensor(out=to, in0=r, scalar=1.0, in1=ps, op0=ALU.add, op1=ALU.mult).then_inc(s[done], 1)

            def mask(it, hp, r):
                dve.wait_ge(s["score_done"], 2 * it + r + 1)
                v.scalar_tensor_tensor(
                    out=masked[r].rearrange("p (b t) -> p b t", t=T), in0=score_ps[:].rearrange("p (b t) -> p b t", t=T),
                    scalar=0.125, in1=decay[:, bass.ds(2 * hp + r, 1), :].to_broadcast([P, GB, T]),
                    op0=ALU.mult, op1=ALU.mult).then_inc(s["masked_done"], 1)

            def gate(it, r):
                dve.wait_ge(s["square_done"], 2 * it + r + 1)
                dve.wait_ge(s[f"proj{r}_free"], ONE + 3 * it + 2 + r)
                v.scalar_tensor_tensor(out=gated[r], in0=tanh_g[r], scalar=1.0, in1=mixed_ps[:], op0=ALU.add,
                                       op1=ALU.mult).then_inc(s["gated_done"], 1)

            def pair(g, hp, last):
                it = g * NP + hp
                scaled(5 * it + 3, tanh_v, v_sb, val_ps[:], "val_free")
                mask(it, hp, 0)
                gate(it, 0)
                scaled(5 * it + 4, tanh_qk[1], q_sb[1], proj_ps[1][:], "proj1_free")
                scaled(5 * it + 5, tanh_qk[0], k_sb[1], proj_ps[0][:], "proj0_free")
                mask(it, hp, 1)
                if not last:
                    scaled(5 * it + 6, tanh_qk[0], q_sb[0], proj_ps[0][:], "proj0_free")
                gate(it, 1)
                if not last:
                    scaled(5 * it + 7, tanh_qk[1], k_sb[0], proj_ps[1][:], "proj1_free")

            for name in from_one:
                dve.sem_inc(s[name], ONE)
            dve.wait_ge(s["const_ld"], 16 * 6)
            v.tensor_scalar(neg_slope[:], slope_sb[:], -1.0, None, ALU.mult).then_inc(s["dve_const"], 1)
            dve.wait_ge(s["pool_const"], 12)
            v.tensor_scalar(dist[:], dist[:], 0.0, None, ALU.max).then_inc(s["dve_const"], 1)
            v.scalar_tensor_tensor(out=wout_sb, in0=wout_sb, scalar=0.5, in1=norm_sb[:].unsqueeze(2).to_broadcast([P, NH, C]),
                                   op0=ALU.mult, op1=ALU.mult).then_inc(s["dve_const"], 1)
            step_w4 = step_w[:].rearrange("p (c x) -> p c x", c=CC)
            step_u4 = step_u[:].rearrange("p (c x) -> p c x", c=CC)
            v.tensor_copy(step_w4, mixw_sb[:].unsqueeze(2).to_broadcast([P, CC, GT]))
            link(v.tensor_copy(step_u4, mixu_sb[:].unsqueeze(2).to_broadcast([P, CC, GT])))
            v.memset(step_w[:].rearrange("p (s t) -> p s t", t=T)[:, :, 0:1], NEG)
            v.memset(step_u[:].rearrange("p (s t) -> p s t", t=T)[:, :, 0:1], -NEG)
            for buf in (top, num, den):
                v.memset(buf[:, 0:1], 0.0)
            v.memset(seen[:], 0.0)
            link(v.memset(seen_b[:], 0.0))

            with dve.Fori(0, NG) as g:
                for j in range(2):
                    scaled(5 * NP * g + j + 1, tanh_qk[j], [q_sb, k_sb][j][0], proj_ps[j][:], f"proj{j}_free")
                with dve.Fori(0, NP - 1) as hp:
                    pair(g, hp, False)
                pair(g, NP - 1, True)
                dve.wait_ge(s["ms_done"], ONE + g + 1)
                v.tensor_copy(ms_all[:, bass.ds(g * GB, GB)], score_ps[:, 0:GB]).then_inc(s["ms_evac"], 1)
            dve.wait_ge(s["ms_evac"], ONE + NG)
            dve.wait_ge(s["y_evac"], ONE + NG)
            v.memset(low_sb[RANK:RANK + 1, :], 1.0).then_inc(s["low_ready"], 1)
            v.tensor_scalar(rms_var[:], ms_all[:], 1.0 / (NH * HD), EPS_RMS, ALU.mult, ALU.add).then_inc(s["var_done"], 1)
            dve.wait_ge(s["rstd_done"], 1)

            def layer_norm(n, of, to, done):
                for b in range(GB):
                    m = v.bn_stats(stats[:, b, :], of[:, b, :])
                link(m, waits)
                for b in range(GB):
                    m = v.bn_aggr(moments[:, b, :], stats[:, b, :])
                link(m)
                v.tensor_scalar(var_eps[:, 0:GB], moments[:, :, 1], EPS_LN, None, ALU.add).then_inc(s["var_done"], 1)
                dve.wait_ge(s["rstd_done"], n)
                for b in range(GB):
                    m = v.tensor_scalar(to[:, b, 0:C], of[:, b, :], moments[:, b, 0:1], rstd[:, b:b + 1], ALU.subtract, ALU.mult)
                m.then_inc(s[done], 1)

            GROUP_LINKS = 30
            start = chain.n
            with dve.Fori(0, NG) as g:
                chain.at(start + GROUP_LINKS * g)
                dve.wait_ge(s["x_in_moved"], 16 * g + 16)
                for b in range(GB):
                    y_b = y_all[:, bass.ds(g * GB + b, 1), :].rearrange("p a c -> p (a c)")
                    m = v.scalar_tensor_tensor(out=pre[:, b, :], in0=y_b, scalar=rms[:, bass.ds(g * GB + b, 1)],
                                               in1=x_in[:, b, :], op0=ALU.mult, op1=ALU.add)
                link(m)
                layer_norm(2 * g + 2, pre, x1, "x1_done")

                dve.wait_ge(s["key_copied"], g + 1)
                link(v.tensor_tensor_scan(top[:, 1:], step_w[:], key[:], 0.0, ALU.add, ALU.max))
                link(v.tensor_tensor(diff[:], key[:], top[:, 0:GL], ALU.subtract))
                link(v.tensor_tensor(keep_e[:], diff[:], step_w[:], ALU.subtract))
                link(v.tensor_scalar(new_e[:], keep_e[:], 0.0, None, ALU.min))
                v.tensor_scalar(keep_e[:], keep_e[:], 0.0, None, ALU.max).then_inc(s["args_done"], 1)
                link(v.tensor_tensor(keep_d[:], diff[:], step_u[:], ALU.add))
                link(v.tensor_scalar(new_d[:], keep_d[:], 0.0, None, ALU.min))
                v.tensor_scalar(keep_d[:], keep_d[:], 0.0, None, ALU.max).then_inc(s["args_done"], 1)
                dve.wait_ge(s["ctx_ld"], 16 * g + 16)
                dve.wait_ge(s["exps_done"], 2 * g + 1)
                link(v.tensor_tensor(diff[:], new_e[:], ctx_sb[:], ALU.mult))
                v.tensor_tensor_scan(num[:, 1:], keep_e[:], diff[:], 0.0, ALU.mult, ALU.add)
                link(v.tensor_tensor_scan(den[:, 1:], keep_e[:], new_e[:], 0.0, ALU.mult, ALU.add))
                dve.wait_ge(s["exps_done"], 2 * g + 2)
                v.tensor_tensor(diff[:], new_d[:], ctx_sb[:], ALU.mult)
                v.tensor_tensor(mix[:], keep_d[:], num[:, 0:GL], ALU.mult)
                link(v.tensor_tensor(keep_e[:], keep_d[:], den[:, 0:GL], ALU.mult))
                v.tensor_tensor(mix[:], mix[:], diff[:], ALU.add)
                link(v.tensor_tensor(keep_e[:], keep_e[:], new_d[:], ALU.add))
                link(v.reciprocal(keep_e[:], keep_e[:]))
                v.tensor_tensor(mix[:], mix[:], keep_e[:], ALU.mult).then_inc(s["mix_done"], 1)

                dve.wait_ge(s["mix_turned"], g + 1)
                link(v.tensor_tensor(pre[:], x1[:], val_ps[:], ALU.add))
                dve.wait_ge(s["scattered"], 16 + 16 * K * GB * g)
                layer_norm(2 * g + 3, pre, row, "x2_done")

                dve.wait_ge(s["logit_done"], g + 1)
                logit_ps = score_ps[:, 0:GB * E].rearrange("p (b e) -> p b e", e=E)
                link(v.tensor_reduce(peak[:], logit_ps, AX.X, ALU.max))
                v.tensor_tensor(logit[:], logit_ps, peak[:].unsqueeze(2).to_broadcast([P, GB, E]), ALU.subtract)\
                 .then_inc(s["shifted_done"], 1)
                dve.wait_ge(s["prob_done"], g + 1)
                link(v.tensor_reduce(total[:], prob[:], AX.X, ALU.add))
                link(v.reciprocal(total[:], total[:]))
                link(v.tensor_tensor(prob[:], prob[:], total[:].unsqueeze(2).to_broadcast([P, GB, E]), ALU.mult), waits)
                for b in range(GB):
                    m = v.max(best[:, b, :], prob[:, b, :])
                link(m, waits)
                for b in range(GB):
                    m = v.max_index(best_at[:, b, :], best[:, b, :], prob[:, b, :])
                link(m)
                link(v.tensor_copy(best_f[:], best_at[:]))
                for k in range(K):
                    m = v.tensor_tensor(onehot[:, :, k, :], expert8[:].unsqueeze(1).to_broadcast([P, GB, E]),
                                        best_f[:, :, k:k + 1].to_broadcast([P, GB, E]), ALU.is_equal)
                link(m)
                flat = onehot[:].rearrange("p b k e -> p b (k e)")
                v.tensor_copy(onehot_b[:], flat).then_inc(s["onehot_done"], 1)
                dve.wait_ge(s["pos_done"], g + 1)
                v.tensor_tensor(picked[:].rearrange("p b k e -> p (b k e)"), onehot[:].rearrange("p b k e -> p (b k e)"),
                                mixed_ps[:, 0:GB * K * E], ALU.mult)
                link(v.tensor_reduce(group_sum[:], flat.rearrange("p b x -> p x b"), AX.X, ALU.add))
                v.tensor_reduce(pos[:], picked[:], AX.X, ALU.add)
                link(v.tensor_tensor(seen[:], seen[:], group_sum[:], ALU.add))
                v.tensor_copy(seen_b[:], seen[:])
                v.tensor_scalar(over[:], pos[:], float(CAP), float(NOWHERE), ALU.is_gt, ALU.mult)
                link(v.scalar_tensor_tensor(out=slot_f[:], in0=best_f[:, :, 0:K], scalar=float(SLOTS),
                                            in1=choice[:].unsqueeze(1).to_broadcast([P, GB, K]), op0=ALU.mult, op1=ALU.add))
                link(v.tensor_tensor(slot_f[:], slot_f[:], pos[:], ALU.add))
                link(v.tensor_tensor(slot_f[:], slot_f[:], over[:], ALU.add))
                v.tensor_copy(slot_at[:], slot_f[:])
                v.tensor_copy(row[:, :, C], token[:, bass.ds(g * GB, GB)])
                v.tensor_scalar(row[:, :, C + 1], token[:, bass.ds(g * GB, GB)], float(NTOK), None, ALU.add)
                v.tensor_copy(row[:, :, C + K:ROW], best[:, :, 0:K]).then_inc(s["rows_done"], 1)
                assert chain.n == GROUP_LINKS, chain.n

            with dve.Fori(0, NG) as g:
                for j in range(GB):
                    dve.wait_ge(s["down_done"], GB * g + j + 1)
                    y_b = y_all[:, bass.ds(g * GB + j, 1), :].rearrange("p a c -> p (a c)")
                    v.scalar_tensor_tensor(out=y_b, in0=val_ps[:, 2 * (j % 2), :], scalar=0.2, in1=y_b, op0=ALU.mult,
                                           op1=ALU.add).then_inc(s["down_evac"], 1)

            chain2 = start + GROUP_LINKS * NG
            with dve.Fori(0, E) as e:
                chain.at(chain2 + e)
                dve.wait_ge(s["rows_ld"], 16 * e + 16)
                dve.wait_ge(s["combined"], 16 + 16 * ST * e)
                n0, mid = CAP // P, CAP % P
                parts = [(slice(0, P), slice(0, n0), 0), (slice(0, mid), slice(n0, n0 + 1), 0),
                         (slice(mid, P), slice(n0, n0 + 1), 1), (slice(0, P), slice(n0 + 1, ST), 1)]
                for ps, js, k in parts:
                    v.tensor_copy(target_f[ps, js], rows_in[ps, js, C + k])
                    m = v.tensor_copy(weight[ps, js], rows_in[ps, js, C + K + k])
                link(m)
                v.tensor_copy(target[:], target_f[:]).then_inc(s["meta_done"], 1)
                dve.wait_ge(s["meta_done"], ONE + e + 1)
                for j in range(ST):
                    dve.wait_ge(s["down_done"], GB * NG + ST * e + j + 1)
                    v.tensor_scalar(rows_out[:, j, :], val_ps[:, 2 * (j % 2), :], weight[:, j:j + 1], None, ALU.mult)\
                     .then_inc(s["down_evac"], 1)

            chain3 = chain2 + E
            with dve.Fori(0, NG) as g:
                chain.at(chain3 + 4 * g)
                dve.wait_ge(s["out_ld"], 32 * g + 32)
                link(v.tensor_tensor(x1[:], x1[:], pre[:], ALU.add))
                link(v.tensor_tensor(pre[:], x1[:], y_all[:, bass.ds(g * GB, GB), :], ALU.add))
                dve.wait_ge(s["x_in_moved"], 16 * NG + 16 * g)
                layer_norm(2 * NG + 2 + g, pre, x_in, "sum_done")


_OUTS = [((B, T, C), "float32")]


def kernel(**inputs):
    import concourse.bacc as bacc
    from concourse.bass_utils import run_bass_kernel_spmd

    f = {n: np.asarray(a) for n, a in inputs.items()}

    def turned(a):
        return a.reshape(NG, GT, CC, P).transpose(0, 3, 2, 1)

    qkv = f["L0_attn_w_qkv"].reshape(NP, 2, 3, HD, CC, P)
    gates = f["L0_attn_w_gate"].reshape(NP, 2, HD, CC, P)

    def piece(a):
        return a.transpose(0, 4, 1, 3, 2).reshape(NP, P, -1)

    values = qkv[:, :, 2].transpose(0, 4, 3, 1, 2).reshape(NP, P, -1)
    w_pairs = np.concatenate([piece(qkv[:, 0, 0:2]), values, piece(gates[:, 0:1]), piece(qkv[:, 1, 0:2]), piece(gates[:, 1:2])], axis=2)

    def up_of(w):
        return w.reshape(-1, CC, P, w.shape[-1]).transpose(0, 2, 1, 3)

    def down_of(w):
        return w.reshape(-1, FC, P, C).transpose(0, 2, 1, 3)

    arrays = dict(
        xT=turned(f["x"].reshape(NTOK, C)),
        x=f["x"].reshape(NG, GB, P, C).transpose(0, 2, 1, 3),
        ctxT=turned(f["ctx_2048"].reshape(NTOK, C)).reshape(NG, P, CC * GT),
        wp=w_pairs,
        wout=f["L0_attn_w_out"].reshape(C, NH, HD).transpose(2, 1, 0),
        norm_w=f["L0_attn_norm_w"].reshape(NH, HD).T,
        slope=f["L0_attn_slope_rate"].reshape(NH),
        mix_w=f["L0_xattn_w"].reshape(CC, P).T,
        mix_u=f["L0_xattn_u"].reshape(CC, P).T,
        gate_w=f["L0_ffn_gate_w"].reshape(CC, P, E).transpose(1, 0, 2),
        w1=up_of(f["L0_ffn_w1"]), b1=f["L0_ffn_b1"].reshape(E, FC, P).transpose(0, 2, 1), w2=down_of(f["L0_ffn_w2"]),
        wd=up_of(f["L0_ffn_wd"]), wu=np.concatenate([f["L0_ffn_wu"], f["L0_ffn_b2"][:, None, :]], axis=1),
        sw1=up_of(f["L0_ffn_sw1"])[0], sb1=f["L0_ffn_sb1"].reshape(FC, P).T, sw2=down_of(f["L0_ffn_sw2"])[0],
        swd=up_of(f["L0_ffn_swd"])[0], swu=np.concatenate([f["L0_ffn_swu"], f["L0_ffn_sb2"][None, :]], axis=0),
    )
    arrays = {n: np.ascontiguousarray(a) for n, a in arrays.items()}
    nc = bacc.Bacc("TRN2", target_bir_lowering=False, num_devices=1)
    args = {n: nc.dram_tensor("in_" + n, a.shape, mybir.dt.from_np(a.dtype), kind="ExternalInput").ap() for n, a in arrays.items()}
    out = nc.dram_tensor("out", (NG, P, GB, C), F32, kind="ExternalOutput").ap()
    decoder_layer(nc, **args, out=out)
    r = run_bass_kernel_spmd(nc, [{"in_" + n: a for n, a in arrays.items()}], core_ids=[0])
    return r.results[0]["out"].transpose(0, 2, 1, 3).reshape(B, T, C)
```

```python
from contextlib import ExitStack

import numpy as np

import concourse.bass as bass
from concourse import mybir

F32 = mybir.dt.float32
BF16 = mybir.dt.bfloat16
U32 = mybir.dt.uint32
ALU = mybir.AluOpType
ACT = mybir.ActivationFunctionType
AX = mybir.AxisListType

P = 128
B, T, C = 16, 128, 256
NH, HD = 16, 128
NP = NH // 2
CC = C // P
GB = 4
NG = B // GB
GT = GB * T
NTOK = B * T
NT = NTOK // P
E, K, HID, RANK = 8, 2, 1024, 32
FC = HID // P
CAP = int(NTOK * 1.25 / E)
SLOTS = K * CAP
ST = SLOTS // P
ROW = C + 4
NOWHERE = 1 << 20
EPS_RMS, EPS_LN = 1e-6, 1e-5
NEG = -1e38

PIECES = {"qk0": (0, 512), "g0": (512, 768), "v": (768, 1280), "qk1": (1280, 1792), "g1": (1792, 2048)}
WCOLS = 2048


def wait_apart(eng, sem, value, waits):
    eng.wait_ge(sem, value)
    eng.sem_inc(waits, 1)


class Count:

    def __init__(self, eng, sem):
        self.eng, self.sem, self.base, self.n = eng, sem, 0, 0

    def at(self, base):
        self.base, self.n = base, 0

    def link(self, ins, waits=None):
        ins.then_inc(self.sem, 1)
        self.n += 1
        self.eng.wait_ge(self.sem, self.base + self.n)
        if waits is not None:
            self.eng.sem_inc(waits, 1)


def decoder_layer(nc, xT, x, ctxT, wp, wout, norm_w, slope, mix_w, mix_u, gate_w,
                  w1, b1, w2, wd, wu, sw1, sb1, sw2, swd, swu, out):
    ctx = ExitStack()
    with ctx:
        def sb(name, shape, dt=F32):
            return ctx.enter_context(nc.sbuf_tensor(name, shape, dt))

        def pb(name, shape, dt=F32):
            return ctx.enter_context(nc.psum_tensor(name, shape, dt))

        def sem(name):
            return ctx.enter_context(nc.semaphore(name))

        slot_rows = nc.dram_tensor("slot_rows", [E * SLOTS, ROW], F32).ap()
        expert_out = nc.dram_tensor("expert_out", [K * NTOK, C], F32).ap()

        proj_ps = [pb(f"proj_ps{i}", [P, GT]) for i in range(2)]
        val_ps = pb("val_ps", [P, GB // 2, 2 * HD])
        turn_ps = pb("turn_ps", [P, GT])
        score_ps = pb("score_ps", [P, GT])
        mixed_ps = pb("mixed_ps", [P, GT])
        y_ps = pb("y_ps", [P, GB, C])

        region = sb("region", [P, 18432])

        def views(*shapes):
            at, found = 0, []
            for shape in shapes:
                n = int(np.prod(shape))
                v = region[:, at:at + n]
                found.append(v if len(shape) == 1 else v.rearrange("p (a b) -> p a b", b=shape[1]))
                at += n
            assert at <= region.shape[1]
            return found

        (x_st, w_slot, wout_sb, decay, tanh_v, v_sb, *rest) = views(
            (CC, GT), (WCOLS,), (NH, C), (NH, T), (GB // 2, 2 * HD), (GB, 2 * HD), *[(GT,)] * 14)
        tanh_qk, tanh_g, q_sb, k_sb, masked, square, gated = (rest[i:i + 2] for i in range(0, 14, 2))
        hid_sb, rows_in, slotT_all, rows_out, w1_sb, w2_sb, low_all = views(
            (FC, SLOTS), (ST, ROW), (2 * CC, SLOTS), (ST, C), (CC, HID), (FC, C), (SLOTS,))
        low_sb = low_all[0:RANK + 1, :]
        ends = views(*[(GB, C)] * 4, (1024 + 1300,), *[(GB, C)] * 2)
        parts, results = [ends[0:2], ends[2:4]], ends[5:7]
        x_all = sb("x_all", [P, CC, NTOK])
        dist = sb("dist", [P, T])
        norm_sb = sb("norm_sb", [P, NH])
        slope_sb = sb("slope_sb", [P, NH])
        neg_slope = sb("neg_slope", [P, NH])
        sq_sum = sb("sq_sum", [P, GT])
        zeros_b = sb("zeros_b", [P, GT], BF16)
        ones_b = sb("ones_b", [P, P], BF16)
        prefix_b = sb("prefix_b", [P, P], BF16)
        ones_f = sb("ones_f", [P, 1])
        ident = sb("ident", [P, P])
        init_row = sb("init_row", [P, ROW])
        y_all = sb("y_all", [P, NT, C])
        x_in = sb("x_in", [P, GB, C])
        x2T = sb("x2T", [P, CC, NTOK])
        half = sb("half", [P, NT])
        SEG = CC * GB
        GL = SEG * T
        mixw_sb, mixu_sb = sb("mixw_sb", [P, CC]), sb("mixu_sb", [P, CC])
        step_w, step_u = sb("step_w", [P, GL]), sb("step_u", [P, GL])
        ctx_sb = sb("ctx_sb", [P, GL])
        key = sb("key", [P, GL])
        top = sb("top", [P, 1 + GL])
        num = sb("num", [P, 1 + GL])
        den = sb("den", [P, 1 + GL])
        diff = sb("diff", [P, GL])
        keep_e, new_e = sb("keep_e", [P, GL]), sb("new_e", [P, GL])
        keep_d, new_d = sb("keep_d", [P, GL]), sb("new_d", [P, GL])
        mix = sb("mix", [P, GL])
        pre = sb("pre", [P, GB, C])
        x1 = sb("x1", [P, GB, C])
        row = sb("row", [P, GB, ROW])
        x2T_now = sb("x2T_now", [P, CC, GT])
        stats, moments = sb("stats", [P, GB, 6]), sb("moments", [P, GB, 2])
        var_eps, rstd = sb("var_eps", [P, NT]), sb("rstd", [P, NT])
        gate_sb = sb("gate_sb", [P, CC, E])
        token = sb("token", [P, NT])
        expert8 = sb("expert8", [P, E])
        choice = sb("choice", [P, K])
        logit, prob = sb("logit", [P, GB, E]), sb("prob", [P, GB, E])
        peak, total = sb("peak", [P, GB]), sb("total", [P, GB])
        best = sb("best", [P, GB, E])
        best_at = sb("best_at", [P, GB, E], U32)
        best_f = sb("best_f", [P, GB, E])
        onehot = sb("onehot", [P, GB, K, E])
        onehot_b = sb("onehot_b", [P, GB, K * E], BF16)
        seen, seen_b = sb("seen", [P, K * E]), sb("seen_b", [P, K * E], BF16)
        group_sum = sb("group_sum", [P, K * E])
        picked = sb("picked", [P, GB, K, E])
        pos = sb("pos", [P, GB, K])
        over = sb("over", [P, GB, K])
        slot_f = sb("slot_f", [P, GB, K])
        slot_at = sb("slot_at", [P, GB, K], U32)
        wd_sb, wu_sb, b1_sb = sb("wd_sb", [P, CC, RANK]), sb("wu_sb", [RANK + 1, C]), sb("b1_sb", [P, FC])
        weight, target_f = sb("weight", [P, ST]), sb("target_f", [P, ST])
        target = sb("target", [P, ST], U32)

        rms, rms_var = sb("rms", [P, GB]), sb("rms_var", [P, GB])
        end_stats, end_moments = sb("end_stats", [P, NT, 6]), sb("end_moments", [P, NT, 2])

        s = {n: sem(n) for n in (
            "const_ld dve_const act_const pool_const x0_ld x_ld x_st_ld w_qk0 w_v w_g0 w_qk1 w_g1 proj0_done proj1_done "
            "proj0_free proj1_free val_done val_free score_done masked_done tanh_done mixed_done square_done "
            "gated_done sq_added sq_zeroed y_done y_evac ms_done ms_evac "
            "x_in_ld ctx_ld var_done rstd_done x1_done key_turned key_copied args_done exps_done kept_done den_done quot_done mix_done "
            "mix_turned mix_added x2_done x2_turned x2_copied base_copied logit_done shifted_done prob_done "
            "onehot_done pos_done rows_done scattered "
            "w_up_ld w_down_ld low_ready up_done gelu_done down_done down_evac rows_ld slots_turned slots_copied "
            "meta_done combined out_ld0 out_ld1 sum_done out_st0 out_st1 "
            "dve_chain pool_chain dve_waits pe_waits pool_waits sp_waits").split()}

        ONE = 1
        from_one = ("proj0_done proj1_done val_done x2_done slots_turned meta_done ms_done proj0_free proj1_free "
                    "masked_done gated_done val_free y_evac gelu_done down_evac slots_copied mix_done rows_done "
                    "ms_evac").split()
        ROOTS = 3
        TURNS = 3
        SHARED_UPS = (FC + 1) * NG

        block = ctx.enter_context(nc.Block())

        @block.sync
        def _(sp):
            def piece(name, hp):
                a, b = PIECES[name]
                sp.dma_start(w_slot[:, a:b], wp[hp, :, a:b]).then_inc(s["w_" + name], 16)

            piece("qk0", 0)
            sp.dma_start(x_all[:, :, 0:GT], xT[0]).then_inc(s["x0_ld"], 16)
            consts = [(norm_sb[:], norm_w), (slope_sb[:], slope.rearrange("(a h) -> a h", a=1).to_broadcast([P, NH])),
                      (wout_sb, wout), (mixw_sb[:], mix_w), (mixu_sb[:], mix_u), (gate_sb[:], gate_w)]
            for to, of in consts[0:2]:
                sp.dma_start(to, of).then_inc(s["const_ld"], 16)

            def mixing_inputs(m):
                wait_apart(sp, s["x2_done"], ONE + m, s["sp_waits"])
                sp.dma_start(x_in[:], x[m]).then_inc(s["x_in_ld"], 16)
                sp.dma_start(ctx_sb[:], ctxT[m]).then_inc(s["ctx_ld"], 16)

            def group(g, first):
                wait_apart(sp, s["val_done"], ONE + 2 * NP * g, s["sp_waits"])
                sp.dma_start(x_st, xT[g]).then_inc(s["x_st_ld"], 16)
                if not first:
                    mixing_inputs(g - 1)
                with sp.Fori(0, NP) as hp:
                    it = g * NP + hp
                    for name, used, n, ahead in (("g0", "proj0_done", 3 * it, 0), ("v", "val_done", 2 * it, 0),
                                                 ("qk1", "proj0_done", 3 * it, 0), ("g1", "proj1_done", 3 * it, 0),
                                                 ("qk0", "proj1_done", 3 * it + 1, 1)):
                        wait_apart(sp, s[used], ONE + n, s["sp_waits"])
                        piece(name, hp + ahead)

            for g in range(1, NG):
                sp.dma_start(x_all[:, :, g * GT:(g + 1) * GT], xT[g]).then_inc(s["x_ld"], 16)
            for to, of in consts[2:]:
                sp.dma_start(to, of).then_inc(s["const_ld"], 16)
            group(0, True)
            with sp.Fori(1, NG) as g:
                group(g, False)
            mixing_inputs(NG - 1)

            def load_up(w1_of, wd_of, b1_of):
                sp.dma_start(w1_sb, w1_of).then_inc(s["w_up_ld"], 16)
                sp.dma_start(wd_sb[:], wd_of).then_inc(s["w_up_ld"], 16)
                sp.dma_start(b1_sb[:], b1_of).then_inc(s["w_up_ld"], 16)

            def load_down(w2_of, wu_of):
                sp.dma_start(w2_sb, w2_of).then_inc(s["w_down_ld"], 16)
                sp.dma_start(wu_sb[:], wu_of).then_inc(s["w_down_ld"], 16)

            sp.wait_ge(s["y_evac"], ONE + NG)
            sp.wait_ge(s["sq_added"], 2 * NP * NG + 2)
            sp.wait_ge(s["proj0_free"], ONE + 3 * NP * NG + 1)
            sp.wait_ge(s["proj1_free"], ONE + 3 * NP * NG + 1)
            load_up(sw1, swd, sb1)
            load_down(sw2, swu)

            def load_rows(e):
                sp.dma_start(rows_in, slot_rows.rearrange("(e j p) c -> e p j c", p=P, j=ST)[e]).then_inc(s["rows_ld"], 16)

            sp.wait_ge(s["scattered"], 16 + 16 * NT * K)
            load_rows(0)
            sp.wait_ge(s["gelu_done"], ONE + SHARED_UPS)
            load_up(w1[0], wd[0], b1[0])

            def expert(e, last):
                wait_apart(sp, s["down_done"], GB * NG + ST * e, s["sp_waits"])
                load_down(w2[e], wu[e])
                if not last:
                    wait_apart(sp, s["meta_done"], ONE + (e + 1), s["sp_waits"])
                    wait_apart(sp, s["slots_turned"], ONE + TURNS * (e + 1), s["sp_waits"])
                    load_rows(e + 1)
                    wait_apart(sp, s["gelu_done"], ONE + SHARED_UPS + 2 * (FC + 1) * (e + 1), s["sp_waits"])
                    load_up(w1[e + 1], wd[e + 1], b1[e + 1])

            with sp.Fori(0, E - 1) as e:
                expert(e, False)
            expert(E - 1, True)

            sp.wait_ge(s["combined"], 16 + 16 * ST * E)
            for g in range(NG):
                if g >= 2:
                    sp.wait_ge(s["sum_done"], g - 1)
                for k in range(K):
                    sp.dma_start(parts[g % 2][k], expert_out.rearrange("(k g b p) c -> k g p b c", k=K, g=NG, p=P)[k, g])\
                      .then_inc(s[f"out_ld{g % 2}"], 16)
            for g in range(NG):
                sp.wait_ge(s["sum_done"], g + 1)
                sp.dma_start(out[g], results[g % 2]).then_inc(s[f"out_st{g % 2}"], 16)
            for n in range(2):
                sp.wait_ge(s[f"out_st{n}"], 16 * (NG // 2))

        @block.gpsimd
        def _(pool):
            g_ = nc.gpsimd
            waits = s["pool_waits"]

            def const(ins):
                ins.then_inc(s["pool_const"], 1)

            const(g_.iota(dist[:], [[1, T]], base=0, channel_multiplier=-1, allow_small_or_imprecise_dtypes=True))
            const(g_.memset(zeros_b[:], 0.0))
            const(g_.memset(ones_b[:], 1.0))
            const(g_.memset(ones_f[:], 1.0))
            const(g_.memset(ident[:], 0.0))
            const(g_.memset(half[:], -0.5))
            const(g_.iota(token[:], [[P, NT]], base=0, channel_multiplier=1, allow_small_or_imprecise_dtypes=True))
            const(g_.iota(expert8[:], [[1, E]], base=0, channel_multiplier=0, allow_small_or_imprecise_dtypes=True))
            const(g_.iota(choice[:], [[CAP, K]], base=-1, channel_multiplier=0, allow_small_or_imprecise_dtypes=True))
            const(g_.memset(init_row[:, 0:C], 0.0))
            const(g_.memset(init_row[:, C:C + K], float(NOWHERE)))
            const(g_.memset(init_row[:, C + K:ROW], 0.0))
            for r in range(2):
                g_.memset(square[r], 0.0).then_inc(s["sq_added"], 1)
            pool.wait_ge(s["pool_const"], 12)
            pool.wait_ge(s["act_const"], 1)
            const(g_.affine_select(out=decay, in_=decay, compare_op=ALU.is_ge, fill=0.0, base=0,
                                   pattern=[[0, NH], [1, T]], channel_multiplier=-1))
            const(g_.affine_select(out=ident[:], in_=ident[:], compare_op=ALU.not_equal, fill=1.0, base=0,
                                   pattern=[[-1, P]], channel_multiplier=1))
            const(g_.affine_select(out=prefix_b[:], in_=ones_b[:], compare_op=ALU.is_ge, fill=0.0, base=0,
                                   pattern=[[1, P]], channel_multiplier=-1))
            pool.dma_start(slot_rows.rearrange("(n p) c -> p n c", p=P),
                           init_row[:].unsqueeze(1).to_broadcast([P, E * ST, ROW])).then_inc(s["scattered"], 16)
            pool.dma_start(expert_out.rearrange("(n p) c -> p n c", p=P),
                           init_row[:, 0:C].unsqueeze(1).to_broadcast([P, K * NT, C])).then_inc(s["combined"], 16)
            pool.wait_ge(s["scattered"], 16)
            pool.wait_ge(s["combined"], 16)

            def inverse_root(n, to, of):
                wait_apart(pool, s["var_done"], n, waits)
                g_.tensor_tensor(out=to, in0=of, in1=half[:, 0:GB], op=ALU.pow).then_inc(s["rstd_done"], 1)

            def zero_sums(g):
                g_.memset(sq_sum[:], 0.0).then_inc(s["sq_zeroed"], 1)
                wait_apart(pool, s["sq_zeroed"], g + 1, waits)

            def mixing(m, hp, place):
                if (hp, place) == (0, 0):
                    inverse_root(ROOTS * m + 1, rms[:], rms_var[:])
                if (hp, place) in ((0, 2), (6, 0)):
                    inverse_root(ROOTS * m + (2 if hp == 0 else 3), rstd[:, 0:GB], var_eps[:, 0:GB])
                if (hp, place) == (4, 1):
                    wait_apart(pool, s["kept_done"], 2 * m + 1, waits)
                    g_.tensor_tensor(out=keep_e[:], in0=keep_e[:], in1=new_d[:], op=ALU.add).then_inc(s["den_done"], 1)
                if (hp, place) == (4, 3):
                    wait_apart(pool, s["kept_done"], 2 * m + 2, waits)
                    g_.tensor_tensor(out=mix[:], in0=mix[:], in1=diff[:], op=ALU.add).then_inc(s["pool_chain"], 1)
                if (hp, place) == (5, 2):
                    wait_apart(pool, s["quot_done"], m + 1, waits)
                    wait_apart(pool, s["pool_chain"], m + 1, waits)
                    g_.tensor_tensor(out=mix[:], in0=mix[:], in1=keep_e[:], op=ALU.mult).then_inc(s["mix_done"], 1)
                if (hp, place) == (7, 3):
                    wait_apart(pool, s["rows_done"], ONE + m + 1, waits)
                    for b in range(GB):
                        for k in range(K):
                            g_.indirect_dma_start(
                                slot_rows, bass.IndirectOffsetOnAxis(slot_at[:, b, k:k + 1], 0), row[:, b, :], None,
                                bounds_check=E * SLOTS - 1, oob_is_err=False).then_inc(s["scattered"], 16)

            def pair(g, hp, mixing):
                for r in range(2):
                    mixing(2 * r)
                    n = 2 * (g * NP + hp) + r
                    wait_apart(pool, s["square_done"], n + 1, waits)
                    wait_apart(pool, s["sq_added"], n + 2, waits)
                    g_.tensor_tensor(out=sq_sum[:], in0=sq_sum[:], in1=square[r], op=ALU.add).then_inc(s["sq_added"], 1)
                    mixing(2 * r + 1)

            zero_sums(0)
            with pool.Fori(0, NP) as hp:
                pair(0, hp, lambda place: None)
            with pool.Fori(1, NG) as g:
                for hp in range(NP):
                    def step(place):
                        mixing(g - 1, hp, place)
                        if (hp, place) == (0, 0):
                            wait_apart(pool, s["ms_done"], ONE + g, waits)
                            zero_sums(g)
                    pair(g, hp, step)
            for hp in range(NP):
                for place in range(4):
                    mixing(NG - 1, hp, place)

            with pool.Fori(0, E) as e:
                for j in range(ST):
                    wait_apart(pool, s["down_evac"], ONE + GB * NG + ST * e + j + 1, waits)
                    pool.indirect_dma_start(
                        expert_out, bass.IndirectOffsetOnAxis(target[:, j:j + 1], 0), rows_out[:, j, :], None,
                        bounds_check=K * NTOK - 1, oob_is_err=False).then_inc(s["combined"], 16)

            for g in range(NG):
                pool.wait_ge(s["var_done"], ROOTS * NG + g + 1)
                g_.tensor_tensor(out=rstd[:, g * GB:(g + 1) * GB], in0=var_eps[:, g * GB:(g + 1) * GB], in1=half[:, 0:GB],
                                 op=ALU.pow).then_inc(s["rstd_done"], 1)

        @block.tensor
        def _(pe):
            waits = s["pe_waits"]

            def project(bank, used, name, g, j=0):
                pe.wait_ge(s[f"proj{bank}_free"], ONE + used)
                for c in range(CC):
                    a = PIECES[name][0] + (j * CC + c) * HD
                    m = nc.tensor.matmul(proj_ps[bank][:], w_slot[:, a:a + HD],
                                         x_all[:, c:c + 1, bass.ds(g * GT, GT)].rearrange("p a t -> p (a t)"),
                                         start=(c == 0), stop=(c == CC - 1))
                m.then_inc(s[f"proj{bank}_done"], 1)

            def values(it, h):
                pe.wait_ge(s["val_free"], ONE + 2 * it + h)
                for b in range(GB // 2):
                    for c in range(CC):
                        a = PIECES["v"][0] + c * 2 * HD
                        t = (h * GB // 2 + b) * T
                        m = nc.tensor.matmul(val_ps[:, b, :], x_st[:, c, t:t + T], w_slot[:, a:a + 2 * HD],
                                             start=(c == 0), stop=(c == CC - 1))
                m.then_inc(s["val_done"], 1)

            def scores(it, r):
                pe.wait_ge(s["proj0_free"], ONE + 3 * it + 1 + 2 * r)
                pe.wait_ge(s["proj1_free"], ONE + 3 * it + 1 + r)
                pe.wait_ge(s["masked_done"], ONE + 2 * it + r)
                for b in range(GB):
                    t = slice(b * T, (b + 1) * T)
                    m = nc.tensor.matmul(score_ps[:, t], k_sb[r][:, t], q_sb[r][:, t], start=True, stop=True)
                m.then_inc(s["score_done"], 1)

            def mixes(it, r):
                pe.wait_ge(s["masked_done"], ONE + 2 * it + r + 1)
                pe.wait_ge(s["val_free"], ONE + 2 * it + 2)
                pe.wait_ge(s["gated_done"], ONE + 2 * it + r)
                for b in range(GB):
                    t = slice(b * T, (b + 1) * T)
                    m = nc.tensor.matmul(mixed_ps[:, t], v_sb[:, b, r * HD:(r + 1) * HD], masked[r][:, t], start=True, stop=True)
                m.then_inc(s["mixed_done"], 1)

            def outs(it, hp, r, last):
                pe.wait_ge(s["gated_done"], ONE + 2 * it + r + 1)
                for b in range(GB):
                    w = wout_sb[:, bass.ds(2 * hp + r, 1), :].rearrange("p a c -> p (a c)")
                    m = nc.tensor.matmul(y_ps[:, b, :], gated[r][:, b * T:(b + 1) * T], w, start=False, stop=last,
                                         skip_group_check=True)
                if last:
                    m.then_inc(s["y_done"], 1)

            def zero_outs(g):
                pe.wait_ge(s["y_evac"], ONE + g)
                for b in range(0, GB, 2):
                    nc.tensor.matmul(y_ps[:, b:b + 2, :], zeros_b[:, 0:P], zeros_b[:], start=True, stop=False,
                                     skip_group_check=True)

            def turn(pairs, done):
                for to, of in pairs:
                    m = nc.tensor.transpose(to, of, ident[:])
                m.then_inc(s[done], 1)

            def mixing(m, hp, place):
                at = (hp, place)
                if at == (0, 0):
                    pe.wait_ge(s["rows_done"], ONE + m)
                    pe.wait_ge(s["sq_added"], 2 * NP * (m + 1) + 2)
                    for b in range(GB):
                        i = nc.tensor.matmul(turn_ps[:, b:b + 1], sq_sum[:, b * T:(b + 1) * T], ones_f[:], start=True, stop=True)
                    i.then_inc(s["ms_done"], 1)
                for c, when in enumerate(((1, 1), (1, 2))):
                    if at == when:
                        if c == 0:
                            pe.wait_ge(s["ms_evac"], ONE + m + 1)
                            pe.wait_ge(s["x1_done"], m + 1)
                        else:
                            pe.wait_ge(s["key_copied"], 2 * m + 1)
                        turn([(turn_ps[:, b * T:(b + 1) * T], x1[:, b, c * P:(c + 1) * P]) for b in range(GB)], "key_turned")
                for c, when in enumerate(((5, 3), (6, 0))):
                    if at == when:
                        if c == 0:
                            pe.wait_ge(s["key_copied"], 2 * m + 2)
                            pe.wait_ge(s["mix_done"], ONE + m + 1)
                        else:
                            pe.wait_ge(s["mix_added"], 2 * m + 1)
                        turn([(turn_ps[:, b * P:(b + 1) * P], mix[:, (c * GB + b) * T:(c * GB + b + 1) * T]) for b in range(GB)],
                             "mix_turned")
                for c, when in enumerate(((6, 2), (6, 3))):
                    if at == when:
                        if c == 0:
                            pe.wait_ge(s["mix_added"], 2 * m + 2)
                            pe.wait_ge(s["x2_done"], ONE + m + 1)
                        else:
                            pe.wait_ge(s["x2_copied"], 4 * m + 2)
                        turn([(turn_ps[:, b * T:(b + 1) * T], row[:, b, c * P:(c + 1) * P]) for b in range(GB)], "x2_turned")
                if at == (7, 0):
                    pe.wait_ge(s["x2_copied"], 4 * m + 4)
                    for b in range(GB):
                        for c in range(CC):
                            i = nc.tensor.matmul(turn_ps[:, b * E:(b + 1) * E], x2T_now[:, c, b * T:(b + 1) * T], gate_sb[:, c, :],
                                                 start=(c == 0), stop=(c == CC - 1))
                    i.then_inc(s["logit_done"], 1)
                if at == (7, 2):
                    pe.wait_ge(s["onehot_done"], m + 1)
                    for b in range(GB):
                        parts_ = [(prefix_b, onehot_b[:, b, :])] + [(ones_b, onehot_b[:, i, :]) for i in range(b)] + [(ones_b, seen_b[:])]
                        for n, (m1, m2) in enumerate(parts_):
                            i = nc.tensor.matmul(turn_ps[:, b * K * E:(b + 1) * K * E], m1[:], m2, start=(n == 0),
                                                 stop=(n == len(parts_) - 1))
                    i.then_inc(s["pos_done"], 1)

            def first_qk(it, g, j):
                pe.wait_ge(s["w_qk0"], 16 * it + 16)
                project(j, 3 * it, "qk0", g, j)

            def pair(g, hp, last, mixing, first=False):
                it = g * NP + hp
                g_next = (g + 1) % NG if last else g
                pe.wait_ge(s["w_v"], 16 * it + 16)
                values(it, 0)
                scores(it, 0)
                pe.wait_ge(s["w_g0"], 16 * it + 16)
                project(0, 3 * it + 1, "g0", g)
                mixing(0)
                values(it, 1)
                pe.wait_ge(s["w_qk1"], 16 * it + 16)
                project(1, 3 * it + 1, "qk1", g, 0)
                mixes(it, 0)
                mixing(1)
                project(0, 3 * it + 2, "qk1", g, 1)
                if first:
                    zero_outs(g)
                outs(it, hp, 0, False)
                pe.wait_ge(s["w_g1"], 16 * it + 16)
                project(1, 3 * it + 2, "g1", g)
                scores(it, 1)
                mixing(2)
                first_qk(it + 1, g_next, 0)
                mixes(it, 1)
                first_qk(it + 1, g_next, 1)
                outs(it, hp, 1, last)
                mixing(3)

            pe.wait_ge(s["x0_ld"], 16)
            first_qk(0, 0, 0)
            first_qk(0, 0, 1)
            pe.wait_ge(s["pool_const"], 15)
            pe.wait_ge(s["dve_const"], 3)
            nothing = lambda place: None
            pe.wait_ge(s["x_st_ld"], 16)
            pair(0, 0, False, nothing, first=True)
            with pe.Fori(1, NP - 1) as hp:
                pair(0, hp, False, nothing)
            pe.wait_ge(s["x_ld"], 16 * (NG - 1))
            pair(0, NP - 1, True, nothing)
            with pe.Fori(1, NG) as g:
                pe.wait_ge(s["x_st_ld"], 16 * g + 16)
                for hp in range(NP):
                    pair(g, hp, hp == NP - 1, lambda place: mixing(g - 1, hp, place), first=(hp == 0))

            banks = [proj_ps[0], proj_ps[1], score_ps, mixed_ps]

            def up(unit, base, cols_, lhs, rhs):
                if unit >= len(banks):
                    wait_apart(pe, s["gelu_done"], ONE + base + unit - len(banks) + 1, waits)
                n = lhs(0).shape[1]
                for c in range(CC):
                    m = nc.tensor.matmul(banks[unit % len(banks)][0:n, 0:cols_], lhs(c), rhs(c), start=(c == 0), stop=(c == CC - 1))
                m.then_inc(s["up_done"], 1)

            def down(j, base):
                pe.wait_ge(s["down_evac"], ONE + base + max(j - 1, 0))
                to = y_ps[:, 2 * (j % 2), :]
                t = slice(j * P, (j + 1) * P)
                for f in range(FC):
                    nc.tensor.matmul(to, hid_sb[:, f, t], w2_sb[:, f, :], start=(f == 0), stop=False)
                nc.tensor.matmul(to, low_sb[:, t], wu_sb[:], start=False, stop=True).then_inc(s["down_done"], 1)

            def shared_up(g):
                base = (FC + 1) * g
                pe.wait_ge(s["gelu_done"], ONE + base)
                for f in range(FC):
                    up(f, base, GT, lambda c: w1_sb[:, c, f * P:(f + 1) * P], lambda c: x2T[:, c, g * GT:(g + 1) * GT])
                up(FC, base, GT, lambda c: wd_sb[:, c, :], lambda c: x2T[:, c, g * GT:(g + 1) * GT])

            def shared_down(g):
                pe.wait_ge(s["gelu_done"], ONE + (FC + 1) * (g + 1))
                for j in range(GB):
                    down(j, GB * g)

            def mix_steps(*pairs):
                for hp in pairs:
                    for place in range(4):
                        mixing(NG - 1, hp, place)

            mix_steps(0, 1)
            pe.wait_ge(s["proj0_free"], ONE + 3 * NP * NG + 1)
            pe.wait_ge(s["proj1_free"], ONE + 3 * NP * NG + 1)
            pe.wait_ge(s["gated_done"], ONE + 2 * NP * NG)
            pe.wait_ge(s["y_evac"], ONE + NG)
            pe.wait_ge(s["w_up_ld"], 48)
            pe.wait_ge(s["low_ready"], 1)
            shared_up(0)
            pe.wait_ge(s["w_down_ld"], 32)
            shared_down(0)
            mix_steps(2, 3, 4, 5)
            shared_up(1)
            mix_steps(6)
            shared_down(1)
            mixing(NG - 1, 7, 0)
            shared_up(2)
            mixing(NG - 1, 7, 2)
            shared_down(2)
            shared_up(3)
            shared_down(3)

            def turn_slots(e):
                pe.wait_ge(s["rows_ld"], 16 * e + 16)
                for n in range(TURNS):
                    if n == 2:
                        pe.wait_ge(s["slots_copied"], ONE + TURNS * e + 1)
                    else:
                        pe.wait_ge(s["slots_copied"], ONE + TURNS * e)
                    to = [turn_ps[:], val_ps[:].rearrange("p b c -> p (b c)"), turn_ps[:]][n]
                    of = [(n, j) for j in range(4)] if n < CC else [(c, j) for c in range(CC) for j in range(4, ST)]
                    turn([(to[:, i * P:(i + 1) * P], rows_in[:, j, c * P:(c + 1) * P]) for i, (c, j) in enumerate(of)], "slots_turned")

            def expert(e, last):
                pe.wait_ge(s["slots_copied"], ONE + TURNS * (e + 1))
                pe.wait_ge(s["w_up_ld"], 48 * e + 96)
                base = SHARED_UPS + 2 * (FC + 1) * e
                pe.wait_ge(s["gelu_done"], ONE + base)
                def slots(c, h):
                    return slotT_all[:, bass.ds((e % 2) * CC + c, 1), h * CAP:(h + 1) * CAP].rearrange("p a t -> p (a t)")
                for f in range(FC):
                    for h in range(2):
                        up(2 * f + h, base, CAP, lambda c: w1_sb[:, c, f * P:(f + 1) * P], lambda c: slots(c, h))
                for h in range(2):
                    up(2 * FC + h, base, CAP, lambda c: wd_sb[:, c, :], lambda c: slots(c, h))
                if not last:
                    turn_slots(e + 1)
                pe.wait_ge(s["w_down_ld"], 32 * e + 64)
                pe.wait_ge(s["gelu_done"], ONE + base + 2 * (FC + 1))
                for j in range(ST):
                    down(j, GB * NG + ST * e)

            pe.wait_ge(s["rows_done"], ONE + NG)
            turn_slots(0)
            with pe.Fori(0, E - 1) as e:
                expert(e, False)
            expert(E - 1, True)

        @block.scalar
        def _(act):
            def tanh(n, bank, to, of, done="tanh_done"):
                act.wait_ge(s[bank + "_done"], ONE + n)
                nc.scalar.activation(to, of, ACT.Tanh, scale=0.5).then_inc(s[done], 1)

            def squares(it, r):
                act.wait_ge(s["mixed_done"], 2 * it + r + 1)
                act.wait_ge(s["sq_added"], 2 * it + r + 1)
                nc.scalar.activation(square[r], mixed_ps[:], ACT.Square).then_inc(s["square_done"], 1)

            def mixing(m, hp, place):
                at = (hp, place)
                for c, when in enumerate(((1, 1), (1, 2))):
                    if at == when:
                        act.wait_ge(s["key_turned"], 2 * m + c + 1)
                        if c == 0:
                            act.wait_ge(s["mix_done"], ONE + m)
                        nc.scalar.copy(key[:, c * GT:(c + 1) * GT], turn_ps[:]).then_inc(s["key_copied"], 1)
                for n, (when, keep, new) in enumerate((((2, 3), keep_e, new_e), ((3, 1), keep_d, new_d))):
                    if at == when:
                        act.wait_ge(s["args_done"], 2 * m + n + 1)
                        nc.scalar.activation(keep[:], keep[:], ACT.Exp, scale=-1.0)
                        nc.scalar.activation(new[:], new[:], ACT.Exp).then_inc(s["exps_done"], 1)
                for c, when in enumerate(((6, 2), (6, 3))):
                    if at == when:
                        act.wait_ge(s["x2_turned"], 2 * m + c + 1)
                        nc.scalar.copy(x2T_now[:, c, :], turn_ps[:]).then_inc(s["x2_copied"], 1)
                        nc.scalar.copy(x2T[:, c, bass.ds(m * GT, GT)], turn_ps[:]).then_inc(s["x2_copied"], 1)
                if at == (7, 0):
                    act.wait_ge(s["shifted_done"], m + 1)
                    nc.scalar.activation(prob[:], logit[:], ACT.Exp).then_inc(s["prob_done"], 1)
                    nc.scalar.copy(y_all[:, bass.ds(m * GB, GB), :], row[:, :, 0:C]).then_inc(s["base_copied"], 1)

            def pair(g, hp, mixing):
                it = g * NP + hp
                def half_values(h):
                    act.wait_ge(s["val_free"], ONE + 2 * it + h)
                    tanh(2 * it + 1 + h, "val", tanh_v, val_ps[:])
                half_values(0)
                tanh(3 * it + 2, "proj0", tanh_g[0], proj_ps[0][:], "proj0_free")
                mixing(0)
                half_values(1)
                tanh(3 * it + 2, "proj1", tanh_qk[1], proj_ps[1][:])
                squares(it, 0)
                mixing(1)
                tanh(3 * it + 3, "proj0", tanh_qk[0], proj_ps[0][:])
                tanh(3 * it + 3, "proj1", tanh_g[1], proj_ps[1][:], "proj1_free")
                mixing(2)
                tanh(3 * it + 4, "proj0", tanh_qk[0], proj_ps[0][:])
                squares(it, 1)
                tanh(3 * it + 4, "proj1", tanh_qk[1], proj_ps[1][:])
                mixing(3)

            def y_out(g):
                act.wait_ge(s["y_done"], g + 1)
                nc.scalar.copy(y_all[:, bass.ds(g * GB, GB), :], y_ps[:]).then_inc(s["y_evac"], 1)

            for j in range(2):
                tanh(1, f"proj{j}", tanh_qk[j], proj_ps[j][:])
            act.wait_ge(s["dve_const"], 2)
            for h in range(NH):
                m = nc.scalar.activation(decay[:, h, :], dist[:], ACT.Exp, scale=neg_slope[:, h:h + 1])
            m.then_inc(s["act_const"], 1)
            with act.Fori(0, NP) as hp:
                pair(0, hp, lambda place: None)
            y_out(0)
            with act.Fori(1, NG) as g:
                for hp in range(NP):
                    pair(g, hp, lambda place: mixing(g - 1, hp, place))
                y_out(g)

            def gelu(n, bank, to, bias):
                act.wait_ge(s["up_done"], n)
                nc.scalar.activation(to, bank, ACT.Gelu, bias=bias).then_inc(s["gelu_done"], 1)

            banks = [proj_ps[0], proj_ps[1], score_ps, mixed_ps]

            def shared_up(g):
                base = (FC + 1) * g
                if g:
                    act.wait_ge(s["down_done"], GB * g)
                for f in range(FC):
                    gelu(base + f + 1, banks[f % 4][:], hid_sb[:, f, 0:GT], b1_sb[:, f:f + 1])
                gelu(base + FC + 1, banks[FC % 4][0:RANK, :], low_sb[0:RANK, 0:GT], 0.0)

            def mix_steps(*pairs):
                for hp in pairs:
                    for place in range(4):
                        mixing(NG - 1, hp, place)

            mix_steps(0, 1)
            act.wait_ge(s["w_up_ld"], 48)
            shared_up(0)
            mix_steps(2, 3, 4, 5)
            shared_up(1)
            mix_steps(6, 7)
            shared_up(2)
            shared_up(3)

            def copy_slots(e):
                for n in range(TURNS):
                    act.wait_ge(s["slots_turned"], ONE + TURNS * e + n + 1)
                    if n < CC:
                        of = [turn_ps[:], val_ps[:].rearrange("p b c -> p (b c)")][n]
                        to = slotT_all[:, bass.ds((e % 2) * CC + n, 1), 0:4 * P].rearrange("p a t -> p (a t)")
                    else:
                        of = turn_ps[:, 0:CC * (ST - 4) * P].rearrange("p (c t) -> p c t", c=CC)
                        to = slotT_all[:, bass.ds((e % 2) * CC, CC), 4 * P:SLOTS]
                    nc.scalar.copy(to, of).then_inc(s["slots_copied"], 1)

            def expert(e, last):
                act.wait_ge(s["w_up_ld"], 48 * e + 96)
                base = SHARED_UPS + 2 * (FC + 1) * e
                act.wait_ge(s["down_done"], GB * NG + ST * e)
                for u in range(2 * FC):
                    f, h = divmod(u, 2)
                    gelu(base + u + 1, banks[u % 4][:, 0:CAP], hid_sb[:, f, h * CAP:(h + 1) * CAP], b1_sb[:, f:f + 1])
                for u in (2 * FC, 2 * FC + 1):
                    h = u - 2 * FC
                    gelu(base + u + 1, banks[u % 4][0:RANK, 0:CAP], low_sb[0:RANK, h * CAP:(h + 1) * CAP], 0.0)
                if not last:
                    copy_slots(e + 1)

            copy_slots(0)
            with act.Fori(0, E - 1) as e:
                expert(e, False)
            expert(E - 1, True)

        @block.vector
        def _(dve):
            v = nc.vector
            waits = s["dve_waits"]
            chain = Count(dve, s["dve_chain"])
            link = chain.link

            def scaled(n, r, to, ps, done):
                dve.wait_ge(s["tanh_done"], n)
                v.scalar_tensor_tensor(out=to, in0=r, scalar=1.0, in1=ps, op0=ALU.add, op1=ALU.mult).then_inc(s[done], 1)

            def mask(it, hp, r):
                dve.wait_ge(s["score_done"], 2 * it + r + 1)
                v.scalar_tensor_tensor(
                    out=masked[r].rearrange("p (b t) -> p b t", t=T), in0=score_ps[:].rearrange("p (b t) -> p b t", t=T),
                    scalar=0.125, in1=decay[:, bass.ds(2 * hp + r, 1), :].to_broadcast([P, GB, T]),
                    op0=ALU.mult, op1=ALU.mult).then_inc(s["masked_done"], 1)

            def gate(it, r):
                dve.wait_ge(s["square_done"], 2 * it + r + 1)
                dve.wait_ge(s[f"proj{r}_free"], ONE + 3 * it + 2 + r)
                v.scalar_tensor_tensor(out=gated[r], in0=tanh_g[r], scalar=1.0, in1=mixed_ps[:], op0=ALU.add,
                                       op1=ALU.mult).then_inc(s["gated_done"], 1)

            def statistics(of):
                for b in range(GB):
                    m = v.bn_stats(stats[:, b, :], of[:, b, :])
                link(m, waits)
                for b in range(GB):
                    m = v.bn_aggr(moments[:, b, :], stats[:, b, :])
                link(m)
                v.tensor_scalar(var_eps[:, 0:GB], moments[:, :, 1], EPS_LN, None, ALU.add).then_inc(s["var_done"], 1)

            def normalise(n, of, to, done):
                dve.wait_ge(s["rstd_done"], n)
                for b in range(GB):
                    m = v.tensor_scalar(to[:, b, 0:C], of[:, b, :], moments[:, b, 0:1], rstd[:, b:b + 1], ALU.subtract, ALU.mult)
                m.then_inc(s[done], 1)

            flat = onehot[:].rearrange("p b k e -> p b (k e)")

            def mixing(m, hp, place):
                at = (hp, place)
                if at == (0, 0):
                    dve.wait_ge(s["ms_done"], ONE + m + 1)
                    v.tensor_scalar(rms_var[:], turn_ps[:, 0:GB], 1.0 / (NH * HD), EPS_RMS, ALU.mult, ALU.add)\
                     .then_inc(s["var_done"], 1)
                    dve.wait_ge(s["var_done"], ROOTS * m + 1)
                    dve.sem_inc(s["ms_evac"], 1)
                if at == (0, 1):
                    dve.wait_ge(s["x_in_ld"], 16 * m + 16)
                    dve.wait_ge(s["y_evac"], ONE + m + 1)
                    dve.wait_ge(s["rstd_done"], ROOTS * m + 1)
                    for b in range(GB):
                        y_b = y_all[:, bass.ds(m * GB + b, 1), :].rearrange("p a c -> p (a c)")
                        i = v.scalar_tensor_tensor(out=pre[:, b, :], in0=y_b, scalar=rms[:, b:b + 1],
                                                   in1=x_in[:, b, :], op0=ALU.mult, op1=ALU.add)
                    link(i, waits)
                if at == (0, 2):
                    statistics(pre)
                if at == (1, 0):
                    normalise(ROOTS * m + 2, pre, x1, "x1_done")

                if at == (1, 3):
                    dve.wait_ge(s["key_copied"], 2 * m + 2)
                    link(v.tensor_tensor_scan(top[:, 1:], step_w[:], key[:], 0.0, ALU.add, ALU.max))
                if at == (2, 0):
                    link(v.tensor_tensor(diff[:], key[:], top[:, 0:GL], ALU.subtract))
                if at == (2, 1):
                    link(v.tensor_tensor(keep_e[:], diff[:], step_w[:], ALU.subtract))
                if at == (2, 2):
                    link(v.tensor_scalar(new_e[:], keep_e[:], 0.0, None, ALU.min))
                    v.tensor_scalar(keep_e[:], keep_e[:], 0.0, None, ALU.max).then_inc(s["args_done"], 1)
                if at == (2, 3):
                    link(v.tensor_tensor(keep_d[:], diff[:], step_u[:], ALU.add))
                if at == (3, 0):
                    link(v.tensor_scalar(new_d[:], keep_d[:], 0.0, None, ALU.min))
                    v.tensor_scalar(keep_d[:], keep_d[:], 0.0, None, ALU.max).then_inc(s["args_done"], 1)
                if at == (3, 2):
                    dve.wait_ge(s["ctx_ld"], 16 * m + 16)
                    dve.wait_ge(s["exps_done"], 2 * m + 1)
                    link(v.tensor_tensor(diff[:], new_e[:], ctx_sb[:], ALU.mult))
                if at == (3, 3):
                    v.tensor_tensor_scan(num[:, 1:], keep_e[:], diff[:], 0.0, ALU.mult, ALU.add)
                if at == (4, 0):
                    link(v.tensor_tensor_scan(den[:, 1:], keep_e[:], new_e[:], 0.0, ALU.mult, ALU.add))
                if at == (4, 1):
                    dve.wait_ge(s["exps_done"], 2 * m + 2)
                    v.tensor_tensor(keep_e[:], keep_d[:], den[:, 0:GL], ALU.mult).then_inc(s["kept_done"], 1)
                if at == (4, 2):
                    v.tensor_tensor(mix[:], keep_d[:], num[:, 0:GL], ALU.mult)
                if at == (4, 3):
                    v.tensor_tensor(diff[:], new_d[:], ctx_sb[:], ALU.mult).then_inc(s["kept_done"], 1)
                for n, when in enumerate(((4, 3), (5, 0), (5, 1), (5, 2))):
                    if at == when:
                        if n == 0:
                            wait_apart(dve, s["den_done"], m + 1, waits)
                        part = slice(n * GL // 4, (n + 1) * GL // 4)
                        i = v.reciprocal(keep_e[:, part], keep_e[:, part])
                        if n == 3:
                            i.then_inc(s["quot_done"], 1)

                for c, when in enumerate(((5, 3), (6, 0))):
                    if at == when:
                        dve.wait_ge(s["mix_turned"], 2 * m + c + 1)
                        half_ = slice(c * P, (c + 1) * P)
                        v.tensor_tensor(pre[:, :, half_], x1[:, :, half_], turn_ps[:].rearrange("p (b c) -> p b c", c=P), ALU.add)\
                         .then_inc(s["mix_added"], 1)
                if at == (6, 0):
                    wait_apart(dve, s["mix_added"], 2 * m + 2, waits)
                    statistics(pre)
                if at == (6, 1):
                    dve.wait_ge(s["scattered"], 16 + 16 * K * GB * m)
                    normalise(ROOTS * m + 3, pre, row, "x2_done")

                if at == (7, 0):
                    dve.wait_ge(s["logit_done"], m + 1)
                    logit_ps = turn_ps[:, 0:GB * E].rearrange("p (b e) -> p b e", e=E)
                    link(v.tensor_reduce(peak[:], logit_ps, AX.X, ALU.max))
                    v.tensor_tensor(logit[:], logit_ps, peak[:].unsqueeze(2).to_broadcast([P, GB, E]), ALU.subtract)\
                     .then_inc(s["shifted_done"], 1)
                if at == (7, 1):
                    dve.wait_ge(s["prob_done"], m + 1)
                    link(v.tensor_reduce(total[:], prob[:], AX.X, ALU.add))
                    link(v.reciprocal(total[:], total[:]))
                    link(v.tensor_tensor(prob[:], prob[:], total[:].unsqueeze(2).to_broadcast([P, GB, E]), ALU.mult), waits)
                    for b in range(GB):
                        i = v.max(best[:, b, :], prob[:, b, :])
                    link(i, waits)
                    for b in range(GB):
                        i = v.max_index(best_at[:, b, :], best[:, b, :], prob[:, b, :])
                    link(i)
                    link(v.tensor_copy(best_f[:], best_at[:]))
                    for k in range(K):
                        i = v.tensor_tensor(onehot[:, :, k, :], expert8[:].unsqueeze(1).to_broadcast([P, GB, E]),
                                            best_f[:, :, k:k + 1].to_broadcast([P, GB, E]), ALU.is_equal)
                    link(i)
                    v.tensor_copy(onehot_b[:], flat).then_inc(s["onehot_done"], 1)
                if at == (7, 2):
                    dve.wait_ge(s["pos_done"], m + 1)
                    v.tensor_tensor(picked[:].rearrange("p b k e -> p (b k e)"), onehot[:].rearrange("p b k e -> p (b k e)"),
                                    turn_ps[:, 0:GB * K * E], ALU.mult)
                    link(v.tensor_reduce(group_sum[:], flat.rearrange("p b x -> p x b"), AX.X, ALU.add))
                    v.tensor_reduce(pos[:], picked[:], AX.X, ALU.add)
                    link(v.tensor_tensor(seen[:], seen[:], group_sum[:], ALU.add))
                    v.tensor_copy(seen_b[:], seen[:])
                    v.tensor_scalar(over[:], pos[:], float(CAP), float(NOWHERE), ALU.is_gt, ALU.mult)
                    link(v.scalar_tensor_tensor(out=slot_f[:], in0=best_f[:, :, 0:K], scalar=float(SLOTS),
                                                in1=choice[:].unsqueeze(1).to_broadcast([P, GB, K]), op0=ALU.mult, op1=ALU.add))
                    link(v.tensor_tensor(slot_f[:], slot_f[:], pos[:], ALU.add))
                    link(v.tensor_tensor(slot_f[:], slot_f[:], over[:], ALU.add))
                    v.tensor_copy(slot_at[:], slot_f[:])
                    v.tensor_copy(row[:, :, C], token[:, bass.ds(m * GB, GB)])
                    v.tensor_scalar(row[:, :, C + 1], token[:, bass.ds(m * GB, GB)], float(NTOK), None, ALU.add)
                    v.tensor_copy(row[:, :, C + K:ROW], best[:, :, 0:K]).then_inc(s["rows_done"], 1)

            def pair(g, hp, mixing):
                it = g * NP + hp
                def half_values(h):
                    scaled(6 * it + 3 + h, tanh_v, v_sb[:, h * GB // 2:(h + 1) * GB // 2, :], val_ps[:], "val_free")
                half_values(0)
                mask(it, hp, 0)
                mixing(0)
                half_values(1)
                scaled(6 * it + 5, tanh_qk[1], q_sb[1], proj_ps[1][:], "proj1_free")
                gate(it, 0)
                mixing(1)
                scaled(6 * it + 6, tanh_qk[0], k_sb[1], proj_ps[0][:], "proj0_free")
                mask(it, hp, 1)
                mixing(2)
                scaled(6 * it + 7, tanh_qk[0], q_sb[0], proj_ps[0][:], "proj0_free")
                gate(it, 1)
                scaled(6 * it + 8, tanh_qk[1], k_sb[0], proj_ps[1][:], "proj1_free")
                mixing(3)

            for name in from_one:
                dve.sem_inc(s[name], ONE)
            for j in range(2):
                scaled(j + 1, tanh_qk[j], [q_sb, k_sb][j][0], proj_ps[j][:], f"proj{j}_free")
            dve.wait_ge(s["const_ld"], 16 * 6)
            v.tensor_scalar(neg_slope[:], slope_sb[:], -1.0, None, ALU.mult).then_inc(s["dve_const"], 1)
            dve.wait_ge(s["pool_const"], 12)
            v.tensor_scalar(dist[:], dist[:], 0.0, None, ALU.max).then_inc(s["dve_const"], 1)
            v.scalar_tensor_tensor(out=wout_sb, in0=wout_sb, scalar=0.5, in1=norm_sb[:].unsqueeze(2).to_broadcast([P, NH, C]),
                                   op0=ALU.mult, op1=ALU.mult).then_inc(s["dve_const"], 1)
            step_w4 = step_w[:].rearrange("p (c x) -> p c x", c=CC)
            step_u4 = step_u[:].rearrange("p (c x) -> p c x", c=CC)
            v.tensor_copy(step_w4, mixw_sb[:].unsqueeze(2).to_broadcast([P, CC, GT]))
            link(v.tensor_copy(step_u4, mixu_sb[:].unsqueeze(2).to_broadcast([P, CC, GT])))
            v.memset(step_w[:].rearrange("p (s t) -> p s t", t=T)[:, :, 0:1], NEG)
            v.memset(step_u[:].rearrange("p (s t) -> p s t", t=T)[:, :, 0:1], -NEG)
            for buf in (top, num, den):
                v.memset(buf[:, 0:1], 0.0)
            v.memset(seen[:], 0.0)
            link(v.memset(seen_b[:], 0.0))
            dve.wait_ge(s["pool_const"], 15)

            GROUP_LINKS = 26
            start = chain.n
            with dve.Fori(0, NP) as hp:
                pair(0, hp, lambda place: None)
            with dve.Fori(1, NG) as g:
                chain.at(start + GROUP_LINKS * (g - 1))
                for hp in range(NP):
                    pair(g, hp, lambda place: mixing(g - 1, hp, place))
                assert chain.n == GROUP_LINKS, chain.n

            def shared_evac(g, j):
                dve.wait_ge(s["down_done"], GB * g + j + 1)
                dve.wait_ge(s["base_copied"], g + 1)
                y_b = y_all[:, g * GB + j, :]
                v.scalar_tensor_tensor(out=y_b, in0=y_ps[:, 2 * (j % 2), :], scalar=0.2, in1=y_b, op0=ALU.mult,
                                       op1=ALU.add).then_inc(s["down_evac"], 1)

            def mix_steps(*pairs):
                for hp in pairs:
                    for place in range(4):
                        mixing(NG - 1, hp, place)

            chain.at(start + GROUP_LINKS * (NG - 1))
            dve.wait_ge(s["y_evac"], ONE + NG)
            dve.wait_ge(s["sq_added"], 2 * NP * NG + 2)
            v.memset(low_sb[RANK:RANK + 1, :], 1.0).then_inc(s["low_ready"], 1)
            mix_steps(0, 1, 2)
            mixing(NG - 1, 3, 0)
            for j in range(GB):
                shared_evac(0, j)
            for place in range(1, 4):
                mixing(NG - 1, 3, place)
            mix_steps(4, 5, 6)
            for j in range(GB):
                shared_evac(1, j)
            mixing(NG - 1, 7, 0)
            mixing(NG - 1, 7, 1)
            mixing(NG - 1, 7, 2)
            for g in (2, 3):
                for j in range(GB):
                    shared_evac(g, j)
            assert chain.n == GROUP_LINKS, chain.n

            def expert(e):
                chain.at(start + GROUP_LINKS * NG + e)
                dve.wait_ge(s["rows_ld"], 16 * e + 16)
                dve.wait_ge(s["combined"], 16 + 16 * ST * e)
                n0, mid = CAP // P, CAP % P
                parts_ = [(slice(0, P), slice(0, n0), 0), (slice(0, mid), slice(n0, n0 + 1), 0),
                          (slice(mid, P), slice(n0, n0 + 1), 1), (slice(0, P), slice(n0 + 1, ST), 1)]
                for ps, js, k in parts_:
                    v.tensor_copy(target_f[ps, js], rows_in[ps, js, C + k])
                    m = v.tensor_copy(weight[ps, js], rows_in[ps, js, C + K + k])
                link(m)
                v.tensor_copy(target[:], target_f[:]).then_inc(s["meta_done"], 1)
                dve.wait_ge(s["meta_done"], ONE + e + 1)
                for j in range(ST):
                    dve.wait_ge(s["down_done"], GB * NG + ST * e + j + 1)
                    v.tensor_scalar(rows_out[:, j, :], y_ps[:, 2 * (j % 2), :], weight[:, j:j + 1], None, ALU.mult)\
                     .then_inc(s["down_evac"], 1)

            with dve.Fori(0, E) as e:
                expert(e)

            chain.at(start + GROUP_LINKS * NG + E)

            def finish(g):
                dve.wait_ge(s["rstd_done"], ROOTS * NG + g + 1)
                if g >= 2:
                    dve.wait_ge(s[f"out_st{g % 2}"], 16 * (g // 2))
                for b in range(GB):
                    m = v.tensor_scalar(results[g % 2][:, b, :], parts[g % 2][1][:, b, :], end_moments[:, g * GB + b, 0:1],
                                        rstd[:, g * GB + b:g * GB + b + 1], ALU.subtract, ALU.mult)
                m.then_inc(s["sum_done"], 1)

            for g in range(NG):
                dve.wait_ge(s[f"out_ld{g % 2}"], 32 * (g // 2) + 32)
                first, second = parts[g % 2]
                link(v.tensor_tensor(second, first, second, ALU.add))
                link(v.tensor_tensor(second, second, y_all[:, g * GB:(g + 1) * GB, :], ALU.add))
                for b in range(GB):
                    m = v.bn_stats(end_stats[:, g * GB + b, :], second[:, b, :])
                link(m)
                for b in range(GB):
                    m = v.bn_aggr(end_moments[:, g * GB + b, :], end_stats[:, g * GB + b, :])
                link(m)
                v.tensor_scalar(var_eps[:, g * GB:(g + 1) * GB], end_moments[:, g * GB:(g + 1) * GB, 1], EPS_LN, None, ALU.add)\
                 .then_inc(s["var_done"], 1)
                finish(g)


_OUTS = [((B, T, C), "float32")]


def kernel(**inputs):
    import concourse.bacc as bacc
    from concourse.bass_utils import run_bass_kernel_spmd

    f = {n: np.asarray(a) for n, a in inputs.items()}

    def turned(a):
        return a.reshape(NG, GT, CC, P).transpose(0, 3, 2, 1)

    qkv = f["L0_attn_w_qkv"].reshape(NP, 2, 3, HD, CC, P)
    gates = f["L0_attn_w_gate"].reshape(NP, 2, HD, CC, P)

    def piece(a):
        return a.transpose(0, 4, 1, 3, 2).reshape(NP, P, -1)

    values = qkv[:, :, 2].transpose(0, 4, 3, 1, 2).reshape(NP, P, -1)
    w_pairs = np.concatenate([piece(qkv[:, 0, 0:2]), piece(gates[:, 0:1]), values, piece(qkv[:, 1, 0:2]), piece(gates[:, 1:2])], axis=2)

    w_pairs = np.concatenate([w_pairs, w_pairs[0:1]], axis=0)

    def up_of(w):
        return w.reshape(-1, CC, P, w.shape[-1]).transpose(0, 2, 1, 3)

    def down_of(w):
        return w.reshape(-1, FC, P, C).transpose(0, 2, 1, 3)

    arrays = dict(
        xT=turned(f["x"].reshape(NTOK, C)),
        x=f["x"].reshape(NG, GB, P, C).transpose(0, 2, 1, 3),
        ctxT=turned(f["ctx_2048"].reshape(NTOK, C)).reshape(NG, P, CC * GT),
        wp=w_pairs,
        wout=f["L0_attn_w_out"].reshape(C, NH, HD).transpose(2, 1, 0),
        norm_w=f["L0_attn_norm_w"].reshape(NH, HD).T,
        slope=f["L0_attn_slope_rate"].reshape(NH),
        mix_w=f["L0_xattn_w"].reshape(CC, P).T,
        mix_u=f["L0_xattn_u"].reshape(CC, P).T,
        gate_w=f["L0_ffn_gate_w"].reshape(CC, P, E).transpose(1, 0, 2),
        w1=up_of(f["L0_ffn_w1"]), b1=f["L0_ffn_b1"].reshape(E, FC, P).transpose(0, 2, 1), w2=down_of(f["L0_ffn_w2"]),
        wd=up_of(f["L0_ffn_wd"]), wu=np.concatenate([f["L0_ffn_wu"], f["L0_ffn_b2"][:, None, :]], axis=1),
        sw1=up_of(f["L0_ffn_sw1"])[0], sb1=f["L0_ffn_sb1"].reshape(FC, P).T, sw2=down_of(f["L0_ffn_sw2"])[0],
        swd=up_of(f["L0_ffn_swd"])[0], swu=np.concatenate([f["L0_ffn_swu"], f["L0_ffn_sb2"][None, :]], axis=0),
    )
    arrays = {n: np.ascontiguousarray(a) for n, a in arrays.items()}
    nc = bacc.Bacc("TRN2", target_bir_lowering=False, num_devices=1)
    args = {n: nc.dram_tensor("in_" + n, a.shape, mybir.dt.from_np(a.dtype), kind="ExternalInput").ap() for n, a in arrays.items()}
    out = nc.dram_tensor("out", (NG, P, GB, C), F32, kind="ExternalOutput").ap()
    decoder_layer(nc, **args, out=out)
    r = run_bass_kernel_spmd(nc, [{"in_" + n: a for n, a in arrays.items()}], core_ids=[0])
    return r.results[0]["out"].transpose(0, 2, 1, 3).reshape(B, T, C)
```

```python
from contextlib import ExitStack

import numpy as np

import concourse.bass as bass
from concourse import mybir

F32 = mybir.dt.float32
F32R = mybir.dt.float32r
BF16 = mybir.dt.bfloat16
U32 = mybir.dt.uint32
ALU = mybir.AluOpType
ACT = mybir.ActivationFunctionType
AX = mybir.AxisListType

P = 128
B, T, C = 16, 128, 256
NH, HD = 16, 128
NP = NH // 2
CC = C // P
GB = 4
NG = B // GB
GT = GB * T
NTOK = B * T
NT = NTOK // P
E, K, HID, RANK = 8, 2, 1024, 32
FC = HID // P
CAP = int(NTOK * 1.25 / E)
SLOTS = K * CAP
ST = SLOTS // P
ROW = C + 4
NOWHERE = 1 << 20
EPS_RMS, EPS_LN = 1e-6, 1e-5
NEG = -1e38

PIECES = {"qk0": (0, 512), "g0": (512, 768), "v": (768, 1280), "qk1": (1280, 1792), "g1": (1792, 2048)}
WCOLS = 2048
NPIECE = len(PIECES)


PLACES = 4
STEPS = ("ms sum1 stats1 x1 key0 key1 top diff keep_arg exp_args keep_arg_d exp_args_d new_terms num den den_kept "
         "num_kept num_new quot1 quot2 quot3 mix0 mix1 x2 x2T0 x2T1 logits choice places").split()
AT = {name: n for n, name in enumerate(STEPS)}
assert len(STEPS) <= PLACES * NP


def steps(first, last):
    return range(AT[first], AT[last] + 1)


def wait_apart(eng, sem, value, waits):
    eng.wait_ge(sem, value)
    eng.sem_inc(waits, 1)


class Count:

    def __init__(self, eng, sem):
        self.eng, self.sem, self.base, self.n = eng, sem, 0, 0

    def at(self, base):
        self.base, self.n = base, 0

    def link(self, ins, waits=None):
        ins.then_inc(self.sem, 1)
        self.n += 1
        self.eng.wait_ge(self.sem, self.base + self.n)
        if waits is not None:
            self.eng.sem_inc(waits, 1)


def decoder_layer(nc, xT, x, ctxT, wp, wout, norm_w, slope, mix_w, mix_u, gate_w,
                  w1, b1, w2, wd, wu, sw1, sb1, sw2, swd, swu, out):
    ctx = ExitStack()
    with ctx:
        def sbuf_in(scope):
            def sb(name, shape, dt=F32):
                return scope.enter_context(nc.sbuf_tensor(name, shape, dt))
            return sb

        sb = sbuf_in(ctx)

        def pb(name, shape, dt=F32):
            return ctx.enter_context(nc.psum_tensor(name, shape, dt))

        def sem(name):
            return ctx.enter_context(nc.semaphore(name))

        slot_rows = nc.dram_tensor("slot_rows", [E * SLOTS, ROW], F32).ap()
        expert_out = nc.dram_tensor("expert_out", [K * NTOK, C], F32).ap()

        x2T_dram = nc.dram_tensor("x2T_dram", [NG, P, CC, GT], F32).ap()

        proj_ps = [pb(f"proj_ps{i}", [P, GT]) for i in range(2)]
        val_ps = pb("val_ps", [P, GB // 2, 2 * HD])
        turn_ps = pb("turn_ps", [P, GT])
        score_ps = pb("score_ps", [P, GT])
        mixed_ps = pb("mixed_ps", [P, GT])
        y_ps = pb("y_ps", [P, GB, C])

        norm_sb = sb("norm_sb", [P, NH + 2])
        slope_sb = sb("slope_sb", [P, NH])
        neg_slope = sb("neg_slope", [P, NH])
        zeros_b = sb("zeros_b", [P, GT], BF16)
        ones_b = sb("ones_b", [P, P], BF16)
        prefix_b = sb("prefix_b", [P, P], BF16)
        ones_f = sb("ones_f", [P, 1])
        ident = sb("ident", [P, P])
        init_row = sb("init_row", [P, ROW])
        y_all = sb("y_all", [P, NT, C])
        half = sb("half", [P, NT])
        SEG = CC * GB
        GL = SEG * T
        mixw_sb, mixu_sb = sb("mixw_sb", [P, CC]), sb("mixu_sb", [P, CC])
        step_w = sb("step_w", [P, GL])
        ctx_sb = sb("ctx_sb", [P, GL])
        key = sb("key", [P, GL])
        top = sb("top", [P, 1 + GL])
        num = sb("num", [P, 1 + GL])
        den = sb("den", [P, 1 + GL])
        diff = sb("diff", [P, GL])
        keep_e, new_e = sb("keep_e", [P, GL]), sb("new_e", [P, GL])
        keep_d, new_d = top[:, 1:], sb("new_d", [P, GL])
        mix = sb("mix", [P, GL])
        pre = sb("pre", [P, GB, C])
        x1 = sb("x1", [P, GB, C])
        x_in = mix[:].rearrange("p (b c) -> p b c", c=C)
        x2T_now = key[:].rearrange("p (c t) -> p c t", c=CC)
        row = sb("row", [P, GB, ROW])
        stats, moments = sb("stats", [P, GB, 6]), sb("moments", [P, GB, 2])
        var_eps, rstd = sb("var_eps", [P, NT]), sb("rstd", [P, NT])
        gate_sb = sb("gate_sb", [P, CC, E])
        token = sb("token", [P, NT])
        expert8 = sb("expert8", [P, E])
        choice = sb("choice", [P, K])
        logit, prob = sb("logit", [P, GB, E]), sb("prob", [P, GB, E])
        peak, total = sb("peak", [P, GB]), sb("total", [P, GB])
        best = sb("best", [P, GB, E])
        best_at = sb("best_at", [P, GB, E], U32)
        best_f = sb("best_f", [P, GB, E])
        onehot = sb("onehot", [P, GB, K, E])
        onehot_b = sb("onehot_b", [P, GB, K * E], BF16)
        seen, seen_b = sb("seen", [P, K * E]), sb("seen_b", [P, K * E], BF16)
        group_sum = sb("group_sum", [P, K * E])
        picked = sb("picked", [P, GB, K, E])
        pos = sb("pos", [P, GB, K])
        over = sb("over", [P, GB, K])
        slot_f = sb("slot_f", [P, GB, K])
        slot_at = sb("slot_at", [P, GB, K], U32)
        weight, target_f = sb("weight", [P, ST]), sb("target_f", [P, ST])
        target = sb("target", [P, ST], U32)

        rms, rms_var = sb("rms", [P, GB]), sb("rms_var", [P, GB])
        shift, zero = sb("shift", [P, NT]), sb("zero", [P, GB])
        end_stats, end_moments = sb("end_stats", [P, NT, 6]), sb("end_moments", [P, NT, 2])

        with ExitStack() as scope:
            sb = sbuf_in(scope)
            x_all = [sb(f"x_all{i}", [P, CC, NTOK], F32R) for i in range(2)]
            x_st = [sb(f"x_st{i}", [P, CC, GT], F32R) for i in range(2)]
            w_slot = [sb(f"w_slot{i}", [P, WCOLS], F32R) for i in range(2)]
            w_stage = sb("w_stage", [P, WCOLS])
            decay = sb("decay", [P, NH, T])
            wo_stage = sb("wo_stage", [P, 2, C])
            wo = [sb(f"wo{i}", [P, 2 * 2, C], F32R) for i in range(2)]
            dist, sq_sum = sb("dist", [P, T]), sb("sq_sum", [P, GT])
            tanh_v, v_sb = sb("tanh_v", [P, GB // 2, 2 * HD]), sb("v_sb", [P, GB, 2 * HD])
            tanh_qk, tanh_g, q_sb, k_sb, masked, square = (
                [sb(f"{n}{r}", [P, GT]) for r in range(2)] for n in "tanh_qk tanh_g q_sb k_sb masked square".split())
            gated_full = sb("gated_full", [P, GT])
            gated = [[sb(f"gated{r}{i}", [P, GT], F32R) for i in range(2)] for r in range(2)]
        with ExitStack() as scope:
            sb = sbuf_in(scope)
            stage = sb("stage", [P, CC * HID])
            x2_stage = [sb(f"x2_stage{i}", [P, CC, GT]) for i in range(2)]
            w1_p = [sb(f"w1_p{i}", [P, CC * HID], F32R) for i in range(2)]
            feed = [[sb(f"feed{n}{i}", [P, CC, (SLOTS, GT)[n]], F32R) for i in range(2)] for n in range(2)]
            w2_p, wd_p, hid = ([sb(f"{n}_p{i}", shape, F32R) for i in range(2)] for n, shape in (
                ("w2", [P, FC * C]), ("wd", [P, CC, P]), ("hid", [P, FC, SLOTS])))
            wd_stage = sb("wd_stage", [P, CC, RANK])
            full = [sb(f"full{i}", [P, GT]) for i in range(4)]
            low_sb, wu_sb, b1_sb = sb("low_sb", [RANK + 1, SLOTS]), sb("wu_sb", [RANK + 1, C]), sb("b1_sb", [P, FC])
            rows_in = sb("rows_in", [P, ST, ROW])
        rows_out = [pre[:, j, :] for j in range(GB)] + [x1[:, 0, :]]
        with ExitStack() as scope:
            sb = sbuf_in(scope)
            parts = [[sb(f"part{i}{k}", [P, GB, C]) for k in range(K)] for i in range(NG)]
            results = [sb(f"result{i}", [P, GB, C]) for i in range(NG)]
        x_stage = [key, keep_e, new_e, new_d]

        s = {n: sem(n) for n in (
            "slope_ld const_ld dve_const act_const pool_const x0_ld x_ld x_st_done w_qk0 w_v w_g0 w_qk1 w_g1 w_wo "
            "wo_scaled wo_lead wo_split gated_split w_lead w_split x_split x_lead proj0_done proj1_done "
            "proj0_free proj1_free val_done val_free score_done masked_done tanh_done mixed_done square_done "
            "gated_done sq_added sq_zeroed y_done y_evac ms_done ms_evac "
            "x_in_ld ctx_ld var_done rstd_done x1_done key_turned key_copied args_done exps_done quot_done "
            "mix_done mix_turned mix_added x2_done x2_turned x2_copied x2T_st x2T_ld0 x2T_ld1 base_copied "
            "logit_done shifted_done prob_done onehot_done pos_done rows_done scattered "
            "w1_ld wd_ld b1_ld w2_ld wu_ld w1_lead w1_split w2_lead w2_split x2_lead x2_split hid_rest hid_rest_e "
            "slots_split low_ready up_done gelu_done down_done down_evac rows_ld slots_turned slots_copied "
            "meta_done combined out_ld0 out_ld1 out_ld2 out_ld3 parts_added sum_done out_st "
            "dve_chain pool_chain dve_waits pe_waits pool_waits sp_waits ").split()}

        ONE = 1
        from_one = ("proj0_done proj1_done val_done x2_done slots_turned meta_done ms_done proj0_free proj1_free "
                    "masked_done gated_done gated_split val_free y_evac gelu_done down_evac slots_copied mix_done rows_done "
                    "ms_evac logit_done x2T_st hid_rest_e slots_split").split()
        ROOTS = 3
        FILLED = 16 * NP
        SENT = 16 * K * GB
        TURNS = 3
        SHARED_UPS = (FC + 1) * NG

        def turned_slots(n, part):
            if n < CC:
                return feed[0][part][:, n, 0:4 * P], [turn_ps[:], val_ps[:].rearrange("p b c -> p (b c)")][n]
            return feed[0][part][:, :, 4 * P:SLOTS], y_ps[:, 2, :].rearrange("p (c t) -> p c t", c=CC)

        block = ctx.enter_context(nc.Block())

        @block.sync
        def _(sp):
            def piece(name, hp):
                a, b = PIECES[name]
                sp.dma_start(w_stage[:, a:b], wp[hp, :, a:b]).then_inc(s["w_" + name], 16)

            def load_wo(hp):
                sp.dma_start(wo_stage[:], wout[hp]).then_inc(s["w_wo"], 16)

            piece("qk0", 0)
            sp.dma_start(x_stage[0][:], xT[0].rearrange("p c t -> p (c t)")).then_inc(s["x0_ld"], 16)
            sp.dma_start(slope_sb[:], slope.rearrange("(a h) -> a h", a=1).to_broadcast([P, NH])).then_inc(s["slope_ld"], 16)
            for name in ("g0", "v", "qk1", "g1"):
                piece(name, 0)
            sp.wait_ge(s["w_split"], 1)
            piece("qk0", 1)
            load_wo(0)
            consts = [(norm_sb[:], norm_w), (mixw_sb[:], mix_w), (mixu_sb[:], mix_u), (gate_sb[:], gate_w)]
            for to, of in consts:
                sp.dma_start(to, of).then_inc(s["const_ld"], 16)
            for g in range(1, NG):
                sp.dma_start(x_stage[g][:], xT[g].rearrange("p c t -> p (c t)")).then_inc(s["x_ld"], 16)
            def mixing_inputs(m):
                wait_apart(sp, s["x2_done"], ONE + m, s["sp_waits"])
                sp.dma_start(x_in, x[m]).then_inc(s["x_in_ld"], 16)
                sp.dma_start(ctx_sb[:], ctxT[m]).then_inc(s["ctx_ld"], 16)

            def store_x2T(m):
                wait_apart(sp, s["x2_copied"], 2 * m + 2, s["sp_waits"])
                sp.dma_start(x2T_dram[m], x2T_now).then_inc(s["x2T_st"], 16)

            def group(g, first):
                if not first:
                    mixing_inputs(g - 1)

                def pieces(hp):
                    wait_apart(sp, s["wo_split"], g * NP + hp + 1, s["sp_waits"])
                    load_wo(hp + 1)
                    for n, (name, ahead) in enumerate((("g0", 1), ("v", 1), ("qk1", 1), ("g1", 1), ("qk0", 2))):
                        wait_apart(sp, s["w_split"], NPIECE * (g * NP + hp) + n + 2, s["sp_waits"])
                        piece(name, hp + ahead)

                with sp.Fori(0, NP - 1) as hp:
                    pieces(hp)
                if not first:
                    store_x2T(g - 1)
                pieces(NP - 1)

            group(0, True)
            with sp.Fori(1, NG) as g:
                group(g, False)
            mixing_inputs(NG - 1)

            sp.wait_ge(s["proj0_done"], ONE + 3 * NP * NG + 1)
            sp.wait_ge(s["proj1_done"], ONE + 3 * NP * NG + 1)
            sp.wait_ge(s["x_st_done"], 2 * (NG + 1))
            sp.dma_start(stage[:], sw1).then_inc(s["w1_ld"], 16)
            sp.wait_ge(s["x2T_st"], ONE + 16 * (NG - 1))
            for g in range(2):
                sp.dma_start(x2_stage[g][:], x2T_dram[g]).then_inc(s[f"x2T_ld{g}"], 16)
            sp.wait_ge(s["y_evac"], ONE + NG)
            sp.wait_ge(s["sq_added"], 2 * NP * NG + 2)
            sp.wait_ge(s["proj0_free"], ONE + 3 * NP * NG + 1)
            sp.wait_ge(s["proj1_free"], ONE + 3 * NP * NG + 1)
            for name in PIECES:
                sp.wait_ge(s["w_" + name], 16 * (NG * NP + (2 if name == "qk0" else 1)))
            sp.wait_ge(s["w_split"], NPIECE * (NG * NP + 1) + 1)
            sp.wait_ge(s["w_wo"], 16 * (NG * NP + 1))
            sp.wait_ge(s["wo_split"], NG * NP + 1)
            sp.dma_start(wd_stage[:], swd).then_inc(s["wd_ld"], 16)
            sp.dma_start(b1_sb[:], sb1).then_inc(s["b1_ld"], 16)
            sp.dma_start(wu_sb[:], swu).then_inc(s["wu_ld"], 16)
            sp.wait_ge(s["w1_split"], 2)
            sp.dma_start(stage[:], sw2).then_inc(s["w2_ld"], 16)
            sp.wait_ge(s["x2_split"], 1)
            sp.dma_start(x2_stage[0][:], x2T_dram[2]).then_inc(s["x2T_ld0"], 16)

            def load_rows(e):
                sp.dma_start(rows_in[:], slot_rows.rearrange("(e j p) c -> e p j c", p=P, j=ST)[e]).then_inc(s["rows_ld"], 16)

            def load_w1(e):
                wait_apart(sp, s["w2_split"], e + 1, s["sp_waits"])
                sp.dma_start(stage[:], w1[e]).then_inc(s["w1_ld"], 16)

            def load_low(e):
                wait_apart(sp, s["gelu_done"], ONE + SHARED_UPS + 2 * (FC + 1) * e, s["sp_waits"])
                sp.dma_start(wd_stage[:], wd[e]).then_inc(s["wd_ld"], 16)
                sp.dma_start(b1_sb[:], b1[e]).then_inc(s["b1_ld"], 16)

            load_w1(0)
            load_low(0)
            sp.wait_ge(s["scattered"], FILLED + SENT * (NG + 1))
            load_rows(0)

            def expert(e, last):
                wait_apart(sp, s["w1_split"], 2 * (e + 2), s["sp_waits"])
                sp.dma_start(stage[:], w2[e]).then_inc(s["w2_ld"], 16)
                wait_apart(sp, s["down_done"], GB * NG + ST * e, s["sp_waits"])
                sp.dma_start(wu_sb[:], wu[e]).then_inc(s["wu_ld"], 16)
                if not last:
                    load_w1(e + 1)
                    wait_apart(sp, s["meta_done"], ONE + (e + 1), s["sp_waits"])
                    wait_apart(sp, s["slots_turned"], ONE + TURNS * (e + 1), s["sp_waits"])
                    load_rows(e + 1)
                    load_low(e + 1)

            with sp.Fori(0, E - 1) as e:
                expert(e, False)
            expert(E - 1, True)

            sp.wait_ge(s["combined"], FILLED + 16 * ST * E)
            for g in range(NG):
                for k in range(K):
                    sp.dma_start(parts[g][k][:], expert_out.rearrange("(k g b p) c -> k g p b c", k=K, g=NG, p=P)[k, g])\
                      .then_inc(s[f"out_ld{g}"], 16)
            for g in range(NG):
                sp.wait_ge(s["sum_done"], g + 1)
                sp.dma_start(out[g], results[g][:]).then_inc(s["out_st"], 16)
            sp.wait_ge(s["out_st"], 16 * NG)

        @block.gpsimd
        def _(pool):
            g_ = nc.gpsimd
            waits = s["pool_waits"]

            def const(ins):
                ins.then_inc(s["pool_const"], 1)

            const(g_.iota(dist[:], [[1, T]], base=0, channel_multiplier=-1, allow_small_or_imprecise_dtypes=True))
            const(g_.memset(zeros_b[:], 0.0))
            const(g_.memset(ones_b[:], 1.0))
            const(g_.memset(ones_f[:], 1.0))
            const(g_.memset(ident[:], 0.0))
            const(g_.memset(half[:], -0.5))
            const(g_.iota(token[:], [[P, NT]], base=0, channel_multiplier=1, allow_small_or_imprecise_dtypes=True))
            const(g_.iota(expert8[:], [[1, E]], base=0, channel_multiplier=0, allow_small_or_imprecise_dtypes=True))
            const(g_.iota(choice[:], [[CAP, K]], base=-1, channel_multiplier=0, allow_small_or_imprecise_dtypes=True))
            const(g_.memset(row[:], 0.0))
            const(g_.memset(zero[:], 0.0))
            const(g_.iota(slot_at[:], [[0, GB * K]], base=NOWHERE, channel_multiplier=0))
            const(g_.memset(init_row[:, 0:C], 0.0))
            const(g_.memset(init_row[:, C:C + K], float(NOWHERE)))
            const(g_.memset(init_row[:, C + K:ROW], 0.0))
            for r in range(2):
                g_.memset(square[r][:], 0.0).then_inc(s["sq_added"], 1)
            def split_rest(n, name):
                a, b = PIECES[name]
                wait_apart(pool, s["w_lead"], n, waits)
                g_.tensor_tensor(out=w_slot[1][:, a:b], in0=w_stage[:, a:b], in1=w_slot[0][:, a:b].bitcast(F32),
                                 op=ALU.subtract).then_inc(s["w_split"], 1)

            def split_wo(n):
                wait_apart(pool, s["wo_lead"], n + 1, waits)
                of = bass.ds((n % 2) * 2, 2)
                g_.tensor_tensor(out=wo[1][:, of, :], in0=wo_stage[:], in1=wo[0][:, of, :].bitcast(F32), op=ALU.subtract)\
                  .then_inc(s["wo_split"], 1)

            for n, name in enumerate(PIECES):
                split_rest(n + 1, name)
            pool.wait_ge(s["pool_const"], 15)
            def cut_decays(n, heads):
                pool.wait_ge(s["act_const"], n)
                const(g_.affine_select(out=decay[:, heads, :], in_=decay[:, heads, :], compare_op=ALU.is_ge, fill=0.0, base=0,
                                       pattern=[[0, heads.stop - heads.start], [1, T]], channel_multiplier=-1))
            cut_decays(1, slice(0, 2))
            const(g_.affine_select(out=ident[:], in_=ident[:], compare_op=ALU.not_equal, fill=1.0, base=0,
                                   pattern=[[-1, P]], channel_multiplier=1))
            const(g_.affine_select(out=prefix_b[:], in_=ones_b[:], compare_op=ALU.is_ge, fill=0.0, base=0,
                                   pattern=[[1, P]], channel_multiplier=-1))
            split_rest(NPIECE + 1, "qk0")
            split_wo(0)

            def inverse_root(n, to, of):
                wait_apart(pool, s["var_done"], n, waits)
                g_.tensor_tensor(out=to, in0=of, in1=half[:, 0:GB], op=ALU.pow).then_inc(s["rstd_done"], 1)

            def fill(n):
                g_.dma_start(slot_rows.rearrange("(q n p) c -> q p n c", p=P, q=NP)[n],
                             init_row[:].unsqueeze(1).to_broadcast([P, E * ST // NP, ROW])).then_inc(s["scattered"], 16)
                g_.dma_start(expert_out.rearrange("(q n p) c -> q p n c", p=P, q=NP)[n],
                             init_row[:, 0:C].unsqueeze(1).to_broadcast([P, K * NT // NP, C])).then_inc(s["combined"], 16)

            def zero_sums(g):
                g_.memset(sq_sum[:], 0.0).then_inc(s["sq_zeroed"], 1)
                wait_apart(pool, s["sq_zeroed"], g + 1, waits)

            def scatter(b, k):
                g_.indirect_dma_start(
                    slot_rows, bass.IndirectOffsetOnAxis(slot_at[:, b, k:k + 1], 0), row[:, b, :], None,
                    bounds_check=E * SLOTS - 1, oob_is_err=False).then_inc(s["scattered"], 16)

            def mixing(m, at):
                if at == AT["ms"]:
                    inverse_root(ROOTS * m + 1, rms[:], rms_var[:])
                if at in (AT["stats1"], AT["mix1"]):
                    inverse_root(ROOTS * m + (2 if at == AT["stats1"] else 3), rstd[:, 0:GB], var_eps[:, 0:GB])
                if at == AT["quot3"]:
                    wait_apart(pool, s["quot_done"], m + 1, waits)
                    g_.tensor_tensor(out=mix[:], in0=mix[:], in1=keep_e[:], op=ALU.mult).then_inc(s["mix_done"], 1)
                n = at - AT["top"]
                if 0 <= n < K * GB:
                    if n == 0:
                        wait_apart(pool, s["rows_done"], ONE + m, waits)
                    scatter(*divmod(n, K))

            def pair(g, hp, mixing):
                piece_n = NPIECE * (g * NP + hp + 1) + 2
                for r in range(2):
                    mixing(2 * r)
                    n = 2 * (g * NP + hp) + r
                    wait_apart(pool, s["square_done"], n + 1, waits)
                    wait_apart(pool, s["sq_added"], n + 2, waits)
                    g_.tensor_tensor(out=sq_sum[:], in0=sq_sum[:], in1=square[r][:], op=ALU.add).then_inc(s["sq_added"], 1)
                    wait_apart(pool, s["gated_done"], ONE + n + 1, waits)
                    g_.tensor_tensor(out=gated[r][1][:], in0=gated_full[:], in1=gated[r][0][:].bitcast(F32), op=ALU.subtract)\
                      .then_inc(s["gated_split"], 1)
                    for i, name in enumerate((("g0", "v"), ("qk1", "g1", "qk0"))[r]):
                        split_rest(piece_n + 2 * r + i, name)
                    if r == 0:
                        split_wo(g * NP + hp + 1)
                    mixing(2 * r + 1)

            zero_sums(0)
            pair(0, 0, lambda place: cut_decays(3, slice(2, NH)) if place == 2 else None)
            fill(0)
            with pool.Fori(1, NP) as hp:
                pair(0, hp, lambda place: None)
                fill(hp)
            pool.wait_ge(s["scattered"], FILLED)
            pool.wait_ge(s["combined"], FILLED)
            with pool.Fori(1, NG) as g:
                for hp in range(NP):
                    def step(place):
                        mixing(g - 1, PLACES * hp + place)
                        if hp == place == 0:
                            wait_apart(pool, s["ms_done"], ONE + g, waits)
                            zero_sums(g)
                    pair(g, hp, step)

            def rest(n, lead, parts_, whole, done):
                wait_apart(pool, s[lead], n, waits)
                g_.tensor_tensor(out=parts_[1], in0=whole, in1=parts_[0].bitcast(F32), op=ALU.subtract).then_inc(s[done], 1)

            def rest_w1(n):
                rest(2 * n + 1, "w1_lead", [w[:] for w in w1_p], stage[:], "w1_split")
                rest(2 * n + 2, "w1_lead", [w[:, :, 0:RANK] for w in wd_p], wd_stage[:], "w1_split")

            def rest_w2(n):
                rest(n + 1, "w2_lead", [w[:] for w in w2_p], stage[:], "w2_split")

            def shared_rests(g):
                for f in range(FC):
                    i = (FC + 1) * g + f
                    rest(ONE + i + 1, "gelu_done", [h[:, f, 0:GT] for h in hid], full[f % 4][:], "hid_rest")

            def mix_steps(first, last):
                for at in steps(first, last):
                    mixing(NG - 1, at)

            mix_steps("ms", "stats1")
            shared_rests(0)
            mix_steps("x1", "num_new")
            shared_rests(1)
            mix_steps("quot1", "mix1")
            shared_rests(2)
            mix_steps("x2", "places")
            shared_rests(3)
            wait_apart(pool, s["rows_done"], ONE + NG, waits)
            for b in range(GB):
                for k in range(K):
                    scatter(b, k)
            rest_w1(1)
            rest_w2(1)

            def expert(e, last):
                if not last:
                    rest_w1(e + 2)
                for j in range(ST):
                    wait_apart(pool, s["down_evac"], ONE + GB * NG + ST * e + j + 1, waits)
                    pool.indirect_dma_start(
                        expert_out, bass.IndirectOffsetOnAxis(target[:, j:j + 1], 0), rows_out[j], None,
                        bounds_check=K * NTOK - 1, oob_is_err=False).then_inc(s["combined"], 16)
                if not last:
                    rest_w2(e + 2)

            with pool.Fori(0, E - 1) as e:
                expert(e, False)
            expert(E - 1, True)

            def add_parts(g):
                pool.wait_ge(s[f"out_ld{g}"], 32)
                first, second = parts[g]
                g_.tensor_tensor(out=second[:], in0=first[:], in1=second[:], op=ALU.add).then_inc(s["parts_added"], 1)

            add_parts(1)
            for g in range(NG):
                now = slice(g * GB, (g + 1) * GB)
                pool.wait_ge(s["var_done"], ROOTS * NG + g + 1)
                g_.tensor_tensor(out=rstd[:, now], in0=var_eps[:, now], in1=half[:, 0:GB], op=ALU.pow).then_inc(s["pool_chain"], 1)
                pool.wait_ge(s["pool_chain"], 2 * g + 1)
                g_.tensor_tensor(out=shift[:, now], in0=end_moments[:, now, 0], in1=rstd[:, now], op=ALU.mult).then_inc(s["pool_chain"], 1)
                pool.wait_ge(s["pool_chain"], 2 * g + 2)
                g_.tensor_tensor(out=shift[:, now], in0=zero[:, 0:GB], in1=shift[:, now], op=ALU.subtract).then_inc(s["rstd_done"], 1)
                if 2 <= g + 2 < NG:
                    add_parts(g + 2)

        @block.tensor
        def _(pe):
            waits = s["pe_waits"]

            products = [(c, i, k) for c in range(CC) for i, k in ((0, 0), (0, 1), (1, 0))]

            def project(bank, used, name, g, j=0):
                pe.wait_ge(s[f"proj{bank}_free"], ONE + used)
                for n, (c, i, k) in enumerate(products):
                    a = PIECES[name][0] + (j * CC + c) * HD
                    m = nc.tensor.matmul(proj_ps[bank][:], w_slot[i][:, a:a + HD],
                                         x_all[k][:, c:c + 1, bass.ds(g * GT, GT)].rearrange("p a t -> p (a t)"),
                                         start=(n == 0), stop=(n == len(products) - 1))
                m.then_inc(s[f"proj{bank}_done"], 1)

            def values(it, h):
                pe.wait_ge(s["val_free"], ONE + 2 * it + h)
                for b in range(GB // 2):
                    for n, (c, i, k) in enumerate(products):
                        a = PIECES["v"][0] + c * 2 * HD
                        t = (h * GB // 2 + b) * T
                        m = nc.tensor.matmul(val_ps[:, b, :], x_st[k][:, c, t:t + T], w_slot[i][:, a:a + 2 * HD],
                                             start=(n == 0), stop=(n == len(products) - 1))
                m.then_inc(s["val_done"], 1)

            def scores(it, r):
                pe.wait_ge(s["proj0_free"], ONE + 3 * it + 1 + 2 * r)
                pe.wait_ge(s["proj1_free"], ONE + 3 * it + 1 + r)
                pe.wait_ge(s["masked_done"], ONE + 2 * it + r)
                for b in range(GB):
                    t = slice(b * T, (b + 1) * T)
                    m = nc.tensor.matmul(score_ps[:, t], k_sb[r][:, t], q_sb[r][:, t], start=True, stop=True)
                m.then_inc(s["score_done"], 1)

            def mixes(it, r):
                pe.wait_ge(s["masked_done"], ONE + 2 * it + r + 1)
                pe.wait_ge(s["val_free"], ONE + 2 * it + 2)
                pe.wait_ge(s["gated_done"], ONE + 2 * it + r)
                for b in range(GB):
                    t = slice(b * T, (b + 1) * T)
                    m = nc.tensor.matmul(mixed_ps[:, t], v_sb[:, b, r * HD:(r + 1) * HD], masked[r][:, t], start=True, stop=True)
                m.then_inc(s["mixed_done"], 1)

            def outs(it, r, last):
                pe.wait_ge(s["gated_split"], ONE + 2 * it + r + 1)
                pe.wait_ge(s["wo_split"], it + 1)
                for b in range(GB):
                    for i, k in ((0, 0), (0, 1), (1, 0)):
                        w = wo[k][:, bass.ds((it % 2) * 2 + r, 1), :].rearrange("p a c -> p (a c)")
                        m = nc.tensor.matmul(y_ps[:, b, :], gated[r][i][:, b * T:(b + 1) * T], w, start=False,
                                             stop=(last and i == 1), skip_group_check=True)
                if last:
                    m.then_inc(s["y_done"], 1)

            def zero_outs(g):
                pe.wait_ge(s["y_evac"], ONE + g)
                for b in range(0, GB, 2):
                    nc.tensor.matmul(y_ps[:, b:b + 2, :], zeros_b[:, 0:P], zeros_b[:], start=True, stop=False,
                                     skip_group_check=True)

            def turn(pairs, done):
                for to, of in pairs:
                    m = nc.tensor.transpose(to, of, ident[:])
                m.then_inc(s[done], 1)

            def mixing(m, at):
                if at == AT["ms"]:
                    pe.wait_ge(s["rows_done"], ONE + m)
                    pe.wait_ge(s["sq_added"], 2 * NP * (m + 1) + 2)
                    for b in range(GB):
                        i = nc.tensor.matmul(turn_ps[:, b:b + 1], sq_sum[:, b * T:(b + 1) * T], ones_f[:], start=True, stop=True)
                    i.then_inc(s["ms_done"], 1)
                for c, when in enumerate((AT["key0"], AT["key1"])):
                    if at == when:
                        if c == 0:
                            pe.wait_ge(s["ms_evac"], ONE + m + 1)
                            pe.wait_ge(s["x1_done"], m + 1)
                        else:
                            pe.wait_ge(s["key_copied"], 2 * m + 1)
                        turn([(turn_ps[:, b * T:(b + 1) * T], x1[:, b, c * P:(c + 1) * P]) for b in range(GB)], "key_turned")
                for c, when in enumerate((AT["mix0"], AT["mix1"])):
                    if at == when:
                        if c == 0:
                            pe.wait_ge(s["key_copied"], 2 * m + 2)
                            pe.wait_ge(s["mix_done"], ONE + m + 1)
                        else:
                            pe.wait_ge(s["mix_added"], 2 * m + 1)
                        turn([(turn_ps[:, b * P:(b + 1) * P], mix[:, (c * GB + b) * T:(c * GB + b + 1) * T]) for b in range(GB)],
                             "mix_turned")
                for c, when in enumerate((AT["x2T0"], AT["x2T1"])):
                    if at == when:
                        if c == 0:
                            pe.wait_ge(s["mix_added"], 2 * m + 2)
                            pe.wait_ge(s["x2_done"], ONE + m + 1)
                        else:
                            pe.wait_ge(s["x2_copied"], 2 * m + 1)
                        turn([(turn_ps[:, b * T:(b + 1) * T], row[:, b, c * P:(c + 1) * P]) for b in range(GB)], "x2_turned")
                if at == AT["logits"]:
                    pe.wait_ge(s["x2_copied"], 2 * m + 2)
                    for b in range(GB):
                        for c in range(CC):
                            i = nc.tensor.matmul(turn_ps[:, b * E:(b + 1) * E], x2T_now[:, c, b * T:(b + 1) * T], gate_sb[:, c, :],
                                                 start=(c == 0), stop=(c == CC - 1))
                    i.then_inc(s["logit_done"], 1)
                if at == AT["places"]:
                    pe.wait_ge(s["onehot_done"], m + 1)
                    for b in range(GB):
                        parts_ = [(prefix_b, onehot_b[:, b, :])] + [(ones_b, onehot_b[:, i, :]) for i in range(b)] + [(ones_b, seen_b[:])]
                        for n, (m1, m2) in enumerate(parts_):
                            i = nc.tensor.matmul(turn_ps[:, b * K * E:(b + 1) * K * E], m1[:], m2, start=(n == 0),
                                                 stop=(n == len(parts_) - 1))
                    i.then_inc(s["pos_done"], 1)

            def first_qk(it, g, j):
                pe.wait_ge(s["w_split"], NPIECE * it + 1)
                project(j, 3 * it, "qk0", g, j)

            def pair(g, hp, last, mixing, first=False, start=False):
                it = g * NP + hp
                g_next = (g + 1) % NG if last else g
                pe.wait_ge(s["w_split"], NPIECE * it + 3)
                values(it, 0)
                scores(it, 0)
                project(0, 3 * it + 1, "g0", g)
                if not start:
                    outs(it - 1, 1, first)
                mixing(0)
                values(it, 1)
                pe.wait_ge(s["w_split"], NPIECE * it + 4)
                project(1, 3 * it + 1, "qk1", g, 0)
                project(0, 3 * it + 2, "qk1", g, 1)
                mixes(it, 0)
                mixing(1)
                pe.wait_ge(s["w_split"], NPIECE * it + 5)
                project(1, 3 * it + 2, "g1", g)
                scores(it, 1)
                mixing(2)
                first_qk(it + 1, g_next, 0)
                first_qk(it + 1, g_next, 1)
                mixes(it, 1)
                if first:
                    pe.wait_ge(s["pool_const"], 18)
                    zero_outs(g)
                outs(it, 0, False)
                mixing(3)

            pe.wait_ge(s["x_split"], 1)
            first_qk(0, 0, 0)
            first_qk(0, 0, 1)
            nothing = lambda place: None
            pe.wait_ge(s["x_st_done"], 2)
            pair(0, 0, False, nothing, first=True, start=True)
            with pe.Fori(1, NP - 1) as hp:
                pair(0, hp, False, nothing)
            pe.wait_ge(s["x_split"], NG)
            pair(0, NP - 1, True, nothing)
            with pe.Fori(1, NG) as g:
                pe.wait_ge(s["x_st_done"], 2 * g + 2)
                for hp in range(NP):
                    pair(g, hp, hp == NP - 1, lambda place: mixing(g - 1, PLACES * hp + place), first=(hp == 0))

            banks = [proj_ps[0], proj_ps[1], score_ps, mixed_ps]

            def up(unit, base, cols_, lhs, rhs):
                if unit >= len(banks):
                    wait_apart(pe, s["gelu_done"], ONE + base + unit - len(banks) + 1, waits)
                for n, (c, i, k) in enumerate(products):
                    m = nc.tensor.matmul(banks[unit % len(banks)][:, 0:cols_], lhs(c, i), rhs(c, k), start=(n == 0),
                                         stop=(n == len(products) - 1))
                m.then_inc(s["up_done"], 1)

            def w1_of(c, i, f):
                return w1_p[i][:, c * HID + f * P:c * HID + (f + 1) * P]

            def down(j, base):
                pe.wait_ge(s["down_evac"], ONE + base + max(j - 1, 0))
                to = y_ps[:, 2 * (j % 2), :]
                t = slice(j * P, (j + 1) * P)
                for f in range(FC):
                    for i, k in ((0, 0), (0, 1), (1, 0)):
                        nc.tensor.matmul(to, hid[i][:, f, t], w2_p[k][:, f * C:(f + 1) * C], start=(f == i == k == 0), stop=False)
                nc.tensor.matmul(to, low_sb[:, t], wu_sb[:], start=False, stop=True).then_inc(s["down_done"], 1)

            def shared_up(g):
                base = (FC + 1) * g
                pe.wait_ge(s["x2_split"], g + 1)
                pe.wait_ge(s["gelu_done"], ONE + base)
                for f in range(FC):
                    up(f, base, GT, lambda c, i: w1_of(c, i, f), lambda c, k: feed[g % 2][k][:, c, 0:GT])
                up(FC, base, GT, lambda c, i: wd_p[i][:, c, :], lambda c, k: feed[g % 2][k][:, c, 0:GT])

            def shared_down(g):
                pe.wait_ge(s["gelu_done"], ONE + (FC + 1) * (g + 1))
                pe.wait_ge(s["hid_rest"], FC * (g + 1))
                for j in range(GB):
                    down(j, GB * g)

            def mix_steps(first, last):
                for at in steps(first, last):
                    mixing(NG - 1, at)

            outs(NG * NP - 1, 1, True)
            mix_steps("ms", "ms")
            pe.wait_ge(s["proj0_free"], ONE + 3 * NP * NG + 1)
            pe.wait_ge(s["proj1_free"], ONE + 3 * NP * NG + 1)
            pe.wait_ge(s["gated_done"], ONE + 2 * NP * NG)
            pe.wait_ge(s["y_evac"], ONE + NG)
            pe.wait_ge(s["w1_split"], 2)
            pe.wait_ge(s["low_ready"], 2)
            shared_up(0)
            mix_steps("sum1", "key1")
            pe.wait_ge(s["w2_split"], 1)
            pe.wait_ge(s["wu_ld"], 16)
            shared_down(0)
            shared_up(1)
            shared_down(1)
            mix_steps("top", "mix1")
            shared_up(2)
            mix_steps("x2", "logits")
            shared_down(2)
            mix_steps("choice", "places")
            shared_up(3)
            shared_down(3)

            def turn_slots(e, downs):
                pe.wait_ge(s["rows_ld"], 16 * e + 16)
                pe.wait_ge(s["slots_split"], ONE + TURNS * e)
                for n, to in enumerate((turn_ps[:], val_ps[:].rearrange("p b c -> p (b c)"), y_ps[:, 2, :])):
                    if n == CC:
                        pe.wait_ge(s["down_evac"], ONE + downs)
                    of = [(n, j) for j in range(4)] if n < CC else [(c, 4) for c in range(CC)]
                    turn([(to[:, i * P:(i + 1) * P], rows_in[:, j, c * P:(c + 1) * P]) for i, (c, j) in enumerate(of)], "slots_turned")

            def expert(e, last):
                pe.wait_ge(s["slots_split"], ONE + TURNS * (e + 1))
                pe.wait_ge(s["w1_split"], 2 * (e + 2))
                base = SHARED_UPS + 2 * (FC + 1) * e
                pe.wait_ge(s["gelu_done"], ONE + base)
                halves_ = [slice(h * CAP, (h + 1) * CAP) for h in range(2)]
                for f in range(FC):
                    for h in range(2):
                        up(2 * f + h, base, CAP, lambda c, i: w1_of(c, i, f), lambda c, k: feed[0][k][:, c, halves_[h]])
                for h in range(2):
                    up(2 * FC + h, base, CAP, lambda c, i: wd_p[i][:, c, :], lambda c, k: feed[0][k][:, c, halves_[h]])
                if not last:
                    turn_slots(e + 1, GB * NG + ST * e)
                pe.wait_ge(s["w2_split"], e + 2)
                pe.wait_ge(s["wu_ld"], 16 * e + 32)
                pe.wait_ge(s["gelu_done"], ONE + base + 2 * (FC + 1))
                pe.wait_ge(s["hid_rest_e"], ONE + 2 * FC * (e + 1))
                for j in range(ST):
                    if j == 1 and not last:
                        pe.wait_ge(s["slots_split"], ONE + TURNS * (e + 2))
                    down(j, GB * NG + ST * e)

            pe.wait_ge(s["rows_done"], ONE + NG)
            turn_slots(0, GB * NG)
            with pe.Fori(0, E - 1) as e:
                expert(e, False)
            expert(E - 1, True)

        @block.scalar
        def _(act):
            def tanh(n, bank, to, of, done="tanh_done"):
                act.wait_ge(s[bank + "_done"], ONE + n)
                nc.scalar.activation(to, of, ACT.Tanh, scale=0.5).then_inc(s[done], 1)

            def squares(it, r):
                act.wait_ge(s["mixed_done"], 2 * it + r + 1)
                act.wait_ge(s["sq_added"], 2 * it + r + 1)
                nc.scalar.activation(square[r][:], mixed_ps[:], ACT.Square).then_inc(s["square_done"], 1)

            def mixing(m, at):
                for c, when in enumerate((AT["key0"], AT["key1"])):
                    if at == when:
                        act.wait_ge(s["key_turned"], 2 * m + c + 1)
                        if c == 0:
                            act.wait_ge(s["x2T_st"], ONE + 16 * m)
                            act.wait_ge(s["logit_done"], ONE + m)
                        nc.scalar.copy(key[:, c * GT:(c + 1) * GT], turn_ps[:]).then_inc(s["key_copied"], 1)
                for n, (when, keep, new) in enumerate(((AT["keep_arg_d"], keep_e, new_e), (AT["new_terms"], keep_d, new_d))):
                    if at == when:
                        act.wait_ge(s["args_done"], 2 * m + n + 1)
                        nc.scalar.activation(keep[:], keep[:], ACT.Exp, scale=-1.0)
                        nc.scalar.activation(new[:], new[:], ACT.Exp).then_inc(s["exps_done"], 1)
                for c, when in enumerate((AT["x2T0"], AT["x2T1"])):
                    if at == when:
                        act.wait_ge(s["x2_turned"], 2 * m + c + 1)
                        nc.scalar.copy(x2T_now[:, c, :], turn_ps[:]).then_inc(s["x2_copied"], 1)
                if at == AT["logits"]:
                    act.wait_ge(s["shifted_done"], m + 1)
                    nc.scalar.activation(prob[:], logit[:], ACT.Exp).then_inc(s["prob_done"], 1)
                    nc.scalar.copy(y_all[:, bass.ds(m * GB, GB), :], row[:, :, 0:C]).then_inc(s["base_copied"], 1)

            def pair(g, hp, mixing):
                it = g * NP + hp
                def half_values(h):
                    act.wait_ge(s["val_free"], ONE + 2 * it + h)
                    tanh(2 * it + 1 + h, "val", tanh_v[:], val_ps[:])
                half_values(0)
                tanh(3 * it + 2, "proj0", tanh_g[0][:], proj_ps[0][:], "proj0_free")
                mixing(0)
                half_values(1)
                tanh(3 * it + 2, "proj1", tanh_qk[1][:], proj_ps[1][:])
                tanh(3 * it + 3, "proj0", tanh_qk[0][:], proj_ps[0][:])
                squares(it, 0)
                split_lead("g0", it + 2)
                split_lead("v", it + 2)
                lead_wo(it + 1)
                mixing(1)
                tanh(3 * it + 3, "proj1", tanh_g[1][:], proj_ps[1][:], "proj1_free")
                split_lead("qk1", it + 2)
                split_lead("g1", it + 2)
                mixing(2)
                tanh(3 * it + 4, "proj0", tanh_qk[0][:], proj_ps[0][:])
                tanh(3 * it + 4, "proj1", tanh_qk[1][:], proj_ps[1][:])
                squares(it, 1)
                split_lead("qk0", it + 3)
                mixing(3)

            def split_lead(name, n):
                a, b = PIECES[name]
                act.wait_ge(s["w_" + name], 16 * n)
                nc.scalar.copy(w_slot[0][:, a:b], w_stage[:, a:b]).then_inc(s["w_lead"], 1)

            def lead_wo(n):
                act.wait_ge(s["wo_scaled"], n + 1)
                nc.scalar.copy(wo[0][:, bass.ds((n % 2) * 2, 2), :], wo_stage[:]).then_inc(s["wo_lead"], 1)

            def y_out(g):
                act.wait_ge(s["y_done"], g + 1)
                nc.scalar.copy(y_all[:, bass.ds(g * GB, GB), :], y_ps[:]).then_inc(s["y_evac"], 1)

            for name in PIECES:
                split_lead(name, 1)
            def decays(heads):
                for h in heads:
                    m = nc.scalar.activation(decay[:, h, :], dist[:], ACT.Exp, scale=neg_slope[:, h:h + 1])
                m.then_inc(s["act_const"], 1)

            act.wait_ge(s["dve_const"], 2)
            decays(range(0, 2))
            for j in range(2):
                tanh(1, f"proj{j}", tanh_qk[j][:], proj_ps[j][:])
            split_lead("qk0", 2)
            lead_wo(0)
            def other_decays(place):
                if place in (1, 2):
                    middle = NH // 2 + 1
                    decays(range(2, middle) if place == 1 else range(middle, NH))

            pair(0, 0, other_decays)
            with act.Fori(1, NP) as hp:
                pair(0, hp, lambda place: None)
            with act.Fori(1, NG) as g:
                for hp in range(NP):
                    def step(place):
                        if hp == place == 0:
                            y_out(g - 1)
                        mixing(g - 1, PLACES * hp + place)
                    pair(g, hp, step)
            y_out(NG - 1)

            def gelu(n, bank, to, bias):
                act.wait_ge(s["up_done"], n)
                for i, o in enumerate(to):
                    m = nc.scalar.activation(o, bank, ACT.Gelu, bias=bias)
                m.then_inc(s["gelu_done"], 1)

            banks = [proj_ps[0], proj_ps[1], score_ps, mixed_ps]

            def lead(loaded, n, to, of, done):
                if loaded is not None:
                    act.wait_ge(s[loaded], n)
                nc.scalar.copy(to, of).then_inc(s[done], 1)

            def lead_w1(n):
                lead("w1_ld", 16 * n + 16, w1_p[0][:], stage[:], "w1_lead")
                lead("wd_ld", 16 * n + 16, wd_p[0][:, :, 0:RANK], wd_stage[:], "w1_lead")

            def shared_up(g, midway=None):
                base = (FC + 1) * g
                if g:
                    act.wait_ge(s["down_done"], GB * g)
                for f in range(FC):
                    if midway is not None and f == FC // 2:
                        midway()
                    if f >= 4 or g:
                        act.wait_ge(s["hid_rest"], FC * g + f - 3)
                    gelu(base + f + 1, banks[f % 4][:], [full[f % 4][:], hid[0][:, f, 0:GT]], b1_sb[:, f:f + 1])
                gelu(base + FC + 1, banks[FC % 4][0:RANK, :], [low_sb[0:RANK, 0:GT]], 0.0)

            def mix_steps(first, last):
                for at in steps(first, last):
                    mixing(NG - 1, at)

            lead("w1_ld", 16, w1_p[0][:], stage[:], "w1_lead")
            act.wait_ge(s["low_ready"], 2)
            lead("wd_ld", 16, wd_p[0][:, :, 0:RANK], wd_stage[:], "w1_lead")
            act.wait_ge(s["b1_ld"], 16)
            shared_up(0, midway=lambda: lead("w2_ld", 16, w2_p[0][:], stage[:], "w2_lead"))
            mix_steps("ms", "new_terms")
            shared_up(1)
            shared_up(2)
            mix_steps("num", "places")
            shared_up(3)
            lead_w1(1)

            def copy_slots(e):
                for n in range(TURNS):
                    act.wait_ge(s["slots_turned"], ONE + TURNS * e + n + 1)
                    to, of = turned_slots(n, 0)
                    nc.scalar.copy(to, of).then_inc(s["slots_copied"], 1)

            def expert(e, last):
                act.wait_ge(s["b1_ld"], 16 * e + 32)
                base = SHARED_UPS + 2 * (FC + 1) * e
                act.wait_ge(s["down_done"], GB * NG + ST * e)
                for u in range(2 * FC):
                    f, h = divmod(u, 2)
                    act.wait_ge(s["hid_rest_e"], ONE + 2 * FC * e + max(u - 3, 0))
                    gelu(base + u + 1, banks[u % 4][:, 0:CAP], [full[u % 4][:, 0:CAP], hid[0][:, f, h * CAP:(h + 1) * CAP]],
                         b1_sb[:, f:f + 1])
                for u in (2 * FC, 2 * FC + 1):
                    h = u - 2 * FC
                    gelu(base + u + 1, banks[u % 4][0:RANK, 0:CAP], [low_sb[0:RANK, h * CAP:(h + 1) * CAP]], 0.0)
                if not last:
                    copy_slots(e + 1)
                    lead_w1(e + 2)

            copy_slots(0)
            with act.Fori(0, E - 1) as e:
                expert(e, False)
            expert(E - 1, True)

            for g in range(NG):
                act.wait_ge(s["rstd_done"], ROOTS * NG + g + 1)
                for b in range(GB):
                    t = slice(g * GB + b, g * GB + b + 1)
                    m = nc.scalar.activation(results[g][:, b, :], parts[g][1][:, b, :], ACT.Identity, scale=rstd[:, t], bias=shift[:, t])
                m.then_inc(s["sum_done"], 1)

        @block.vector
        def _(dve):
            v = nc.vector
            waits = s["dve_waits"]
            chain = Count(dve, s["dve_chain"])
            link = chain.link

            def scaled(n, r, to, ps, done):
                dve.wait_ge(s["tanh_done"], n)
                v.scalar_tensor_tensor(out=to, in0=r, scalar=1.0, in1=ps, op0=ALU.add, op1=ALU.mult).then_inc(s[done], 1)

            def mask(it, hp, r):
                dve.wait_ge(s["score_done"], 2 * it + r + 1)
                v.scalar_tensor_tensor(
                    out=masked[r][:].rearrange("p (b t) -> p b t", t=T), in0=score_ps[:].rearrange("p (b t) -> p b t", t=T),
                    scalar=0.125, in1=decay[:, bass.ds(2 * hp + r, 1), :].to_broadcast([P, GB, T]),
                    op0=ALU.mult, op1=ALU.mult).then_inc(s["masked_done"], 1)

            def gate(it, r):
                dve.wait_ge(s["square_done"], 2 * it + r + 1)
                dve.wait_ge(s[f"proj{r}_free"], ONE + 3 * it + 2 + r)
                dve.wait_ge(s["gated_split"], ONE + 2 * it + r)
                for to in (gated_full, gated[r][0]):
                    m = v.scalar_tensor_tensor(out=to[:], in0=tanh_g[r][:], scalar=1.0, in1=mixed_ps[:], op0=ALU.add, op1=ALU.mult)
                m.then_inc(s["gated_done"], 1)

            def statistics(of):
                for b in range(GB):
                    m = v.bn_stats(stats[:, b, :], of[:, b, :])
                link(m, waits)
                for b in range(GB):
                    m = v.bn_aggr(moments[:, b, :], stats[:, b, :])
                link(m)
                v.tensor_scalar(var_eps[:, 0:GB], moments[:, :, 1], EPS_LN, None, ALU.add).then_inc(s["var_done"], 1)

            def normalise(n, of, to, done):
                dve.wait_ge(s["rstd_done"], n)
                for b in range(GB):
                    m = v.tensor_scalar(to[:, b, 0:C], of[:, b, :], moments[:, b, 0:1], rstd[:, b:b + 1], ALU.subtract, ALU.mult)
                m.then_inc(s[done], 1)

            flat = onehot[:].rearrange("p b k e -> p b (k e)")

            def mixing(m, at):
                if at == AT["ms"]:
                    dve.wait_ge(s["ms_done"], ONE + m + 1)
                    v.tensor_scalar(rms_var[:], turn_ps[:, 0:GB], 1.0 / (NH * HD), EPS_RMS, ALU.mult, ALU.add)\
                     .then_inc(s["var_done"], 1)
                    dve.wait_ge(s["var_done"], ROOTS * m + 1)
                    dve.sem_inc(s["ms_evac"], 1)
                if at == AT["sum1"]:
                    dve.wait_ge(s["x_in_ld"], 16 * m + 16)
                    dve.wait_ge(s["y_evac"], ONE + m + 1)
                    dve.wait_ge(s["rstd_done"], ROOTS * m + 1)
                    for b in range(GB):
                        y_b = y_all[:, bass.ds(m * GB + b, 1), :].rearrange("p a c -> p (a c)")
                        i = v.scalar_tensor_tensor(out=pre[:, b, :], in0=y_b, scalar=rms[:, b:b + 1],
                                                   in1=x_in[:, b, :], op0=ALU.mult, op1=ALU.add)
                    link(i, waits)
                if at == AT["stats1"]:
                    statistics(pre)
                if at == AT["x1"]:
                    normalise(ROOTS * m + 2, pre, x1, "x1_done")

                if at == AT["top"]:
                    dve.wait_ge(s["key_copied"], 2 * m + 2)
                    link(v.tensor_tensor_scan(top[:, 1:], step_w[:], key[:], 0.0, ALU.add, ALU.max))
                if at == AT["diff"]:
                    link(v.tensor_tensor(diff[:], key[:], top[:, 0:GL], ALU.subtract))
                if at == AT["keep_arg"]:
                    link(v.tensor_tensor(keep_e[:], diff[:], step_w[:], ALU.subtract))
                if at == AT["exp_args"]:
                    link(v.tensor_scalar(new_e[:], keep_e[:], 0.0, None, ALU.min))
                    v.tensor_scalar(keep_e[:], keep_e[:], 0.0, None, ALU.max).then_inc(s["args_done"], 1)
                if at == AT["keep_arg_d"]:
                    for c in range(CC):
                        half_ = slice(c * GT, (c + 1) * GT)
                        i = v.tensor_scalar(keep_d[:, half_], diff[:, half_], mixu_sb[:, c:c + 1], None, ALU.add)
                    link(i)
                    link(v.memset(keep_d.rearrange("p (s t) -> p s t", t=T)[:, :, 0:1], -NEG))
                if at == AT["exp_args_d"]:
                    link(v.tensor_scalar(new_d[:], keep_d, 0.0, None, ALU.min))
                    v.tensor_scalar(keep_d, keep_d, 0.0, None, ALU.max).then_inc(s["args_done"], 1)
                if at == AT["new_terms"]:
                    dve.wait_ge(s["ctx_ld"], 16 * m + 16)
                    dve.wait_ge(s["exps_done"], 2 * m + 1)
                    link(v.tensor_tensor(diff[:], new_e[:], ctx_sb[:], ALU.mult))
                if at == AT["num"]:
                    v.tensor_tensor_scan(num[:, 1:], keep_e[:], diff[:], 0.0, ALU.mult, ALU.add)
                if at == AT["den"]:
                    link(v.tensor_tensor_scan(den[:, 1:], keep_e[:], new_e[:], 0.0, ALU.mult, ALU.add))
                if at == AT["den_kept"]:
                    dve.wait_ge(s["exps_done"], 2 * m + 2)
                    link(v.tensor_tensor(keep_e[:], keep_d, den[:, 0:GL], ALU.mult))
                    link(v.tensor_tensor(keep_e[:], keep_e[:], new_d[:], ALU.add))
                if at == AT["num_kept"]:
                    v.tensor_tensor(mix[:], keep_d, num[:, 0:GL], ALU.mult)
                if at == AT["num_new"]:
                    link(v.tensor_tensor(diff[:], new_d[:], ctx_sb[:], ALU.mult))
                    v.tensor_tensor(mix[:], mix[:], diff[:], ALU.add)
                for n, when in enumerate((AT["num_kept"], AT["quot1"], AT["quot2"], AT["quot3"])):
                    if at == when:
                        part = slice(n * GL // 4, (n + 1) * GL // 4)
                        i = v.reciprocal(keep_e[:, part], keep_e[:, part])
                        if n == 3:
                            i.then_inc(s["quot_done"], 1)

                for c, when in enumerate((AT["mix0"], AT["mix1"])):
                    if at == when:
                        dve.wait_ge(s["mix_turned"], 2 * m + c + 1)
                        half_ = slice(c * P, (c + 1) * P)
                        v.tensor_tensor(pre[:, :, half_], x1[:, :, half_], turn_ps[:].rearrange("p (b c) -> p b c", c=P), ALU.add)\
                         .then_inc(s["mix_added"], 1)
                if at == AT["mix1"]:
                    wait_apart(dve, s["mix_added"], 2 * m + 2, waits)
                    statistics(pre)
                if at == AT["x2"]:
                    dve.wait_ge(s["scattered"], FILLED + SENT * (m + 1))
                    normalise(ROOTS * m + 3, pre, row, "x2_done")

                if at == AT["logits"]:
                    dve.wait_ge(s["logit_done"], ONE + m + 1)
                    logit_ps = turn_ps[:, 0:GB * E].rearrange("p (b e) -> p b e", e=E)
                    link(v.tensor_reduce(peak[:], logit_ps, AX.X, ALU.max))
                    v.tensor_tensor(logit[:], logit_ps, peak[:].unsqueeze(2).to_broadcast([P, GB, E]), ALU.subtract)\
                     .then_inc(s["shifted_done"], 1)
                if at == AT["choice"]:
                    dve.wait_ge(s["prob_done"], m + 1)
                    link(v.tensor_reduce(total[:], prob[:], AX.X, ALU.add))
                    link(v.reciprocal(total[:], total[:]))
                    link(v.tensor_tensor(prob[:], prob[:], total[:].unsqueeze(2).to_broadcast([P, GB, E]), ALU.mult), waits)
                    for b in range(GB):
                        i = v.max(best[:, b, :], prob[:, b, :])
                    link(i, waits)
                    for b in range(GB):
                        i = v.max_index(best_at[:, b, :], best[:, b, :], prob[:, b, :])
                    link(i)
                    link(v.tensor_copy(best_f[:], best_at[:]))
                    for k in range(K):
                        i = v.tensor_tensor(onehot[:, :, k, :], expert8[:].unsqueeze(1).to_broadcast([P, GB, E]),
                                            best_f[:, :, k:k + 1].to_broadcast([P, GB, E]), ALU.is_equal)
                    link(i)
                    v.tensor_copy(onehot_b[:], flat).then_inc(s["onehot_done"], 1)
                if at == AT["places"]:
                    dve.wait_ge(s["pos_done"], m + 1)
                    v.tensor_tensor(picked[:].rearrange("p b k e -> p (b k e)"), onehot[:].rearrange("p b k e -> p (b k e)"),
                                    turn_ps[:, 0:GB * K * E], ALU.mult)
                    link(v.tensor_reduce(group_sum[:], flat.rearrange("p b x -> p x b"), AX.X, ALU.add))
                    v.tensor_reduce(pos[:], picked[:], AX.X, ALU.add)
                    link(v.tensor_tensor(seen[:], seen[:], group_sum[:], ALU.add))
                    v.tensor_copy(seen_b[:], seen[:])
                    v.tensor_scalar(over[:], pos[:], float(CAP), float(NOWHERE), ALU.is_gt, ALU.mult)
                    link(v.scalar_tensor_tensor(out=slot_f[:], in0=best_f[:, :, 0:K], scalar=float(SLOTS),
                                                in1=choice[:].unsqueeze(1).to_broadcast([P, GB, K]), op0=ALU.mult, op1=ALU.add))
                    link(v.tensor_tensor(slot_f[:], slot_f[:], pos[:], ALU.add))
                    link(v.tensor_tensor(slot_f[:], slot_f[:], over[:], ALU.add))
                    v.tensor_copy(slot_at[:], slot_f[:])
                    v.tensor_copy(row[:, :, C], token[:, bass.ds(m * GB, GB)])
                    v.tensor_scalar(row[:, :, C + 1], token[:, bass.ds(m * GB, GB)], float(NTOK), None, ALU.add)
                    v.tensor_copy(row[:, :, C + K:ROW], best[:, :, 0:K]).then_inc(s["rows_done"], 1)

            def scale_wo(n, hp):
                dve.wait_ge(s["w_wo"], 16 * n + 16)
                v.scalar_tensor_tensor(out=wo_stage[:], in0=wo_stage[:], scalar=0.5,
                                       in1=norm_sb[:, bass.ds(2 * hp, 2)].unsqueeze(2).to_broadcast([P, 2, C]),
                                       op0=ALU.mult, op1=ALU.mult).then_inc(s["wo_scaled"], 1)

            def stationary(g):
                for i in range(2):
                    v.tensor_copy(x_st[i][:], x_all[i][:, :, bass.ds(g * GT, GT)].bitcast(F32)).then_inc(s["x_st_done"], 1)

            def pair(g, hp, mixing, last=False):
                it = g * NP + hp
                def half_values(h):
                    scaled(6 * it + 3 + h, tanh_v[:], v_sb[:, h * GB // 2:(h + 1) * GB // 2, :], val_ps[:], "val_free")
                half_values(0)
                mask(it, hp, 0)
                scale_wo(it + 1, hp + 1)
                mixing(0)
                half_values(1)
                if last:
                    stationary((g + 1) % NG)
                scaled(6 * it + 5, tanh_qk[1][:], q_sb[1][:], proj_ps[1][:], "proj1_free")
                scaled(6 * it + 6, tanh_qk[0][:], k_sb[1][:], proj_ps[0][:], "proj0_free")
                gate(it, 0)
                mixing(1)
                mask(it, hp, 1)
                mixing(2)
                scaled(6 * it + 7, tanh_qk[0][:], q_sb[0][:], proj_ps[0][:], "proj0_free")
                scaled(6 * it + 8, tanh_qk[1][:], k_sb[0][:], proj_ps[1][:], "proj1_free")
                gate(it, 1)
                mixing(3)

            for name in from_one:
                dve.sem_inc(s[name], ONE)
            def split_tokens(g):
                now = [x_all[i][:, :, g * GT:(g + 1) * GT] for i in range(2)]
                stage = x_stage[g][:].rearrange("p (c t) -> p c t", c=CC)
                v.tensor_copy(now[0], stage).then_inc(s["x_lead"], 1)
                dve.wait_ge(s["x_lead"], g + 1)
                v.tensor_tensor(now[1], stage, now[0].bitcast(F32), ALU.subtract).then_inc(s["x_split"], 1)

            dve.wait_ge(s["x0_ld"], 16)
            split_tokens(0)
            dve.wait_ge(s["slope_ld"], 16)
            v.tensor_scalar(neg_slope[:], slope_sb[:], -1.0, None, ALU.mult).then_inc(s["dve_const"], 1)
            dve.wait_ge(s["pool_const"], 15)
            v.tensor_scalar(dist[:], dist[:], 0.0, None, ALU.max).then_inc(s["dve_const"], 1)
            dve.wait_ge(s["x_split"], 1)
            stationary(0)
            for j in range(2):
                scaled(j + 1, tanh_qk[j][:], [q_sb, k_sb][j][0][:], proj_ps[j][:], f"proj{j}_free")

            dve.wait_ge(s["const_ld"], 16 * 4)
            scale_wo(0, 0)
            def other_tokens(place):
                if place == 1:
                    dve.wait_ge(s["x_ld"], 16 * (NG - 1))
                if place:
                    split_tokens(place)

            dve.wait_ge(s["pool_const"], 16)
            assert NG - 1 < PLACES
            pair(0, 0, other_tokens)
            step_w4 = step_w[:].rearrange("p (c x) -> p c x", c=CC)
            link(v.tensor_copy(step_w4, mixw_sb[:].unsqueeze(2).to_broadcast([P, CC, GT])))
            v.memset(step_w[:].rearrange("p (s t) -> p s t", t=T)[:, :, 0:1], NEG)
            for buf in (top, num, den):
                v.memset(buf[:, 0:1], 0.0)
            v.memset(seen[:], 0.0)
            link(v.memset(seen_b[:], 0.0))

            GROUP_LINKS = 30
            start = chain.n
            dve.wait_ge(s["pool_const"], 19)
            with dve.Fori(1, NP - 1) as hp:
                pair(0, hp, lambda place: None)
            dve.wait_ge(s["x_split"], NG)
            pair(0, NP - 1, lambda place: None, last=True)
            with dve.Fori(1, NG) as g:
                chain.at(start + GROUP_LINKS * (g - 1))
                for hp in range(NP):
                    pair(g, hp, lambda place: mixing(g - 1, PLACES * hp + place), last=(hp == NP - 1))
                assert chain.n == GROUP_LINKS, chain.n

            def shared_evac(g, j):
                dve.wait_ge(s["down_done"], GB * g + j + 1)
                dve.wait_ge(s["base_copied"], g + 1)
                y_b = y_all[:, g * GB + j, :]
                v.scalar_tensor_tensor(out=y_b, in0=y_ps[:, 2 * (j % 2), :], scalar=0.2, in1=y_b, op0=ALU.mult,
                                       op1=ALU.add).then_inc(s["down_evac"], 1)

            def mix_steps(first, last):
                for at in steps(first, last):
                    mixing(NG - 1, at)

            chain.at(start + GROUP_LINKS * (NG - 1))
            dve.wait_ge(s["y_evac"], ONE + NG)
            dve.wait_ge(s["sq_added"], 2 * NP * NG + 2)
            dve.wait_ge(s["w_split"], NPIECE * (NG * NP + 1) + 1)
            dve.wait_ge(s["wo_split"], NG * NP + 1)
            v.memset(low_sb[RANK:RANK + 1, :], 1.0).then_inc(s["low_ready"], 1)
            for i in range(2):
                m = v.tensor_copy(wd_p[i][:].rearrange("p c x -> p (c x)"), zeros_b[:, 0:CC * P])
            m.then_inc(s["low_ready"], 1)

            def split_x2(g):
                to = [f[:, :, 0:GT] for f in feed[g % 2]]
                if g < NG - 1:
                    dve.wait_ge(s[f"x2T_ld{g % 2}"], 16 * (g // 2) + 16)
                    of = x2_stage[g % 2][:]
                else:
                    dve.wait_ge(s["x2_copied"], 2 * NG)
                    of = x2T_now
                v.tensor_copy(to[0], of).then_inc(s["x2_lead"], 1)
                dve.wait_ge(s["x2_lead"], g + 1)
                v.tensor_tensor(to[1], of, to[0].bitcast(F32), ALU.subtract).then_inc(s["x2_split"], 1)

            def split_rest(n, lead, parts_, whole, done):
                dve.wait_ge(s[lead], n)
                v.tensor_tensor(parts_[1], whole, parts_[0].bitcast(F32), ALU.subtract).then_inc(s[done], 1)

            mix_steps("ms", "ms")
            split_x2(0)
            split_rest(1, "w1_lead", [w[:] for w in w1_p], stage[:], "w1_split")
            split_rest(2, "w1_lead", [w[:, :, 0:RANK] for w in wd_p], wd_stage[:], "w1_split")
            mix_steps("sum1", "stats1")
            split_rest(1, "w2_lead", [w[:] for w in w2_p], stage[:], "w2_split")
            mix_steps("x1", "diff")
            shared_evac(0, 0)
            mix_steps("keep_arg", "exp_args")
            shared_evac(0, 1)
            mix_steps("keep_arg_d", "exp_args_d")
            split_x2(1)
            shared_evac(0, 2)
            shared_evac(0, 3)
            mix_steps("new_terms", "quot3")
            split_x2(2)
            for j in range(GB):
                shared_evac(1, j)
            mix_steps("mix0", "logits")
            split_x2(3)
            shared_evac(2, 0)
            mix_steps("choice", "choice")
            for j in range(1, GB):
                shared_evac(2, j)
            mix_steps("places", "places")
            for j in range(GB):
                shared_evac(3, j)
            dve.wait_ge(s["hid_rest"], FC * NG)
            assert chain.n == GROUP_LINKS, chain.n

            def lead_w2(n):
                dve.wait_ge(s["w2_ld"], 16 * n + 16)
                v.tensor_copy(w2_p[0][:], stage[:]).then_inc(s["w2_lead"], 1)

            def split_slots(e):
                for n in range(TURNS):
                    dve.wait_ge(s["slots_copied"], ONE + TURNS * e + n + 1)
                    rest, of = turned_slots(n, 1)
                    v.tensor_tensor(rest, of, turned_slots(n, 0)[0].bitcast(F32), ALU.subtract).then_inc(s["slots_split"], 1)

            def hidden_rest(e, u):
                f, h = divmod(u, 2)
                cols = slice(h * CAP, (h + 1) * CAP)
                dve.wait_ge(s["gelu_done"], ONE + SHARED_UPS + 2 * (FC + 1) * e + u + 1)
                v.tensor_tensor(hid[1][:, f, cols], full[u % 4][:, 0:CAP], hid[0][:, f, cols].bitcast(F32), ALU.subtract)\
                 .then_inc(s["hid_rest_e"], 1)

            def expert(e, last):
                chain.at(start + GROUP_LINKS * NG + e)
                for u in range(FC):
                    hidden_rest(e, u)
                dve.wait_ge(s["rows_ld"], 16 * e + 16)
                dve.wait_ge(s["combined"], FILLED + 16 * ST * e)
                n0, mid = CAP // P, CAP % P
                parts_ = [(slice(0, P), slice(0, n0), 0), (slice(0, mid), slice(n0, n0 + 1), 0),
                          (slice(mid, P), slice(n0, n0 + 1), 1), (slice(0, P), slice(n0 + 1, ST), 1)]
                for ps, js, k in parts_:
                    v.tensor_copy(target_f[ps, js], rows_in[ps, js, C + k])
                    m = v.tensor_copy(weight[ps, js], rows_in[ps, js, C + K + k])
                link(m)
                v.tensor_copy(target[:], target_f[:]).then_inc(s["meta_done"], 1)
                for u in range(FC, 2 * FC):
                    hidden_rest(e, u)
                if not last:
                    split_slots(e + 1)
                dve.wait_ge(s["meta_done"], ONE + e + 1)
                for j in range(ST):
                    dve.wait_ge(s["down_done"], GB * NG + ST * e + j + 1)
                    v.tensor_scalar(rows_out[j], y_ps[:, 2 * (j % 2), :], weight[:, j:j + 1], None, ALU.mult)\
                     .then_inc(s["down_evac"], 1)
                if not last:
                    lead_w2(e + 2)

            split_slots(0)
            lead_w2(1)
            with dve.Fori(0, E - 1) as e:
                expert(e, False)
            expert(E - 1, True)

            chain.at(start + GROUP_LINKS * NG + E)

            for g in range(NG):
                first, second = parts[g]
                first, second = parts[g]
                if g == 0:
                    dve.wait_ge(s["out_ld0"], 32)
                    link(v.tensor_tensor(second[:], first[:], second[:], ALU.add))
                else:
                    dve.wait_ge(s["parts_added"], g)
                link(v.tensor_tensor(second[:], second[:], y_all[:, g * GB:(g + 1) * GB, :], ALU.add))
                for b in range(GB):
                    m = v.bn_stats(end_stats[:, g * GB + b, :], second[:, b, :])
                link(m)
                for b in range(GB):
                    m = v.bn_aggr(end_moments[:, g * GB + b, :], end_stats[:, g * GB + b, :])
                link(m)
                v.tensor_scalar(var_eps[:, g * GB:(g + 1) * GB], end_moments[:, g * GB:(g + 1) * GB, 1], EPS_LN, None, ALU.add)\
                 .then_inc(s["var_done"], 1)


_OUTS = [((B, T, C), "float32")]


def kernel(**inputs):
    import concourse.bacc as bacc
    from concourse.bass_utils import run_bass_kernel_spmd

    f = {n: np.asarray(a) for n, a in inputs.items()}

    def turned(a):
        return a.reshape(NG, GT, CC, P).transpose(0, 3, 2, 1)

    qkv = f["L0_attn_w_qkv"].reshape(NP, 2, 3, HD, CC, P)
    gates = f["L0_attn_w_gate"].reshape(NP, 2, HD, CC, P)

    def piece(a):
        return a.transpose(0, 4, 1, 3, 2).reshape(NP, P, -1)

    values = qkv[:, :, 2].transpose(0, 4, 3, 1, 2).reshape(NP, P, -1)
    w_pairs = np.concatenate([piece(qkv[:, 0, 0:2]), piece(gates[:, 0:1]), values, piece(qkv[:, 1, 0:2]), piece(gates[:, 1:2])], axis=2)

    def wrapped(a, n):
        return np.concatenate([a, a[0:n]], axis=0)

    w_pairs = wrapped(w_pairs, 2)

    def up_of(w):
        return w.reshape(-1, CC, P, w.shape[-1]).transpose(0, 2, 1, 3)

    def down_of(w):
        return w.reshape(-1, FC, P, C).transpose(0, 2, 1, 3)

    arrays = dict(
        xT=turned(f["x"].reshape(NTOK, C)),
        x=f["x"].reshape(NG, GB, P, C).transpose(0, 2, 1, 3),
        ctxT=turned(f["ctx_2048"].reshape(NTOK, C)).reshape(NG, P, CC * GT),
        wp=w_pairs,
        wout=wrapped(f["L0_attn_w_out"].reshape(C, NP, 2, HD).transpose(1, 3, 2, 0), 1),
        norm_w=wrapped(f["L0_attn_norm_w"].reshape(NH, HD), 2).T,
        slope=f["L0_attn_slope_rate"].reshape(NH),
        mix_w=f["L0_xattn_w"].reshape(CC, P).T,
        mix_u=f["L0_xattn_u"].reshape(CC, P).T,
        gate_w=f["L0_ffn_gate_w"].reshape(CC, P, E).transpose(1, 0, 2),
        w1=up_of(f["L0_ffn_w1"]).reshape(E, P, CC * HID), b1=f["L0_ffn_b1"].reshape(E, FC, P).transpose(0, 2, 1), w2=down_of(f["L0_ffn_w2"]).reshape(E, P, FC * C),
        wd=up_of(f["L0_ffn_wd"]), wu=np.concatenate([f["L0_ffn_wu"], f["L0_ffn_b2"][:, None, :]], axis=1),
        sw1=up_of(f["L0_ffn_sw1"]).reshape(P, CC * HID), sb1=f["L0_ffn_sb1"].reshape(FC, P).T, sw2=down_of(f["L0_ffn_sw2"]).reshape(P, FC * C),
        swd=up_of(f["L0_ffn_swd"])[0], swu=np.concatenate([f["L0_ffn_swu"], f["L0_ffn_sb2"][None, :]], axis=0),
    )
    arrays = {n: np.ascontiguousarray(a) for n, a in arrays.items()}
    nc = bacc.Bacc("TRN2", target_bir_lowering=False, num_devices=1)
    args = {n: nc.dram_tensor("in_" + n, a.shape, mybir.dt.from_np(a.dtype), kind="ExternalInput").ap() for n, a in arrays.items()}
    out = nc.dram_tensor("out", (NG, P, GB, C), F32, kind="ExternalOutput").ap()
    decoder_layer(nc, **args, out=out)
    r = run_bass_kernel_spmd(nc, [{"in_" + n: a for n, a in arrays.items()}], core_ids=[0])
    return r.results[0]["out"].transpose(0, 2, 1, 3).reshape(B, T, C)
```
